# Optimizing a Trainium2 kernel written in Bass

```python
import numpy as np
import jax
import jax.numpy as jnp

def _softmax(x, axis=-1):
    return jax.nn.softmax(x, axis=axis)

def _gelu(x):
    return jax.nn.gelu(x, approximate=True)

def _silu(x):
    return jax.nn.silu(x)

def _sigmoid(x):
    return jax.nn.sigmoid(x)

def _layernorm(x, axis=-1, eps=1e-05):
    m = jnp.mean(x, axis=axis, keepdims=True)
    v = jnp.var(x, axis=axis, keepdims=True)
    return (x - m) / jnp.sqrt(v + eps)

def _scatter_add(tgt, idx, src, axis=0):
    return tgt.at[idx].add(src)

def _segment_sum(src, seg, n):
    return jax.ops.segment_sum(src, seg, n)
kernel_name = 'mk_vit_tower_cls_d2_tok_img768_r4_91ecee'

def setup_inputs(seed: int=0):
    np.random.seed(seed)
    _w = jnp.asarray

    def _rec_inputs():
        import jax
        import jax.numpy as jnp
        _rk = jax.random.key(seed)
        x = -0.000222058 + 0.999998 * jax.random.normal(jax.random.fold_in(_rk, 1), (32, 3, 64, 64), jnp.float32)
        cls_tok = 0.02 * jax.random.normal(jax.random.fold_in(_rk, 5), (1, 1, 192), jnp.float32)
        return (x, cls_tok)
    x, cls_tok = _rec_inputs()

    def _L0_tok_setup():
        import jax, jax.numpy as jnp
        import numpy as np
        B, C, IMG, P = (128, 3, 64, 16)
        HP = IMG // P
        EMBED = 192

        def dct_basis(N, dtype=jnp.float32):
            n = jnp.arange(N, dtype=dtype)
            k = jnp.arange(N, dtype=dtype)[:, None]
            return 2.0 * jnp.cos(jnp.pi * (2.0 * n + 1.0) * k / (2.0 * N))
        key = jax.random.key(seed)
        k1, k2 = jax.random.split(key)
        x = jax.random.normal(k1, (B, C, IMG, IMG), dtype=jnp.float32)
        W = jax.random.normal(k2, (EMBED, C * P * P), dtype=jnp.float32) / np.sqrt(C * P * P)
        return {'x': x, 'W': W}
    _L0_tok_all = _L0_tok_setup()
    _L0_tok_in = {k: v for k, v in _L0_tok_all.items() if k in ('W',)}
    del _L0_tok_all

    def _L0_attn_setup():
        import jax, jax.numpy as jnp
        import numpy as np
        import math
        B, S, E = (2, 512, 192)
        H = 12
        V = 50257
        EPS = 1e-05

        def _layernorm(x, w):
            mu = jnp.mean(x, axis=-1, keepdims=True)
            var = jnp.mean(jnp.square(x - mu), axis=-1, keepdims=True)
            return (x - mu) * jax.lax.rsqrt(var + EPS) * w
        key = jax.random.key(seed)
        ks = jax.random.split(key, 7)
        x = jax.random.normal(ks[0], (B, S, E), dtype=jnp.float32)
        e = jax.random.normal(ks[1], (B, S, E), dtype=jnp.float32)
        p = jax.random.normal(ks[2], (B, S, E), dtype=jnp.float32)
        ln_w = jnp.ones((E,), dtype=jnp.float32)
        W_qk = 0.02 * jax.random.normal(ks[3], (H, E), dtype=jnp.float32)
        W_o = 0.02 / math.sqrt(2 * 12) * jax.random.normal(ks[4], (E, H * E), dtype=jnp.float32)
        wte = 0.02 * jax.random.normal(ks[5], (V, E), dtype=jnp.float32)
        return {'x': x, 'e': e, 'p': p, 'ln_w': ln_w, 'W_qk': W_qk, 'W_o': W_o, 'wte': wte}
    _L0_attn_all = _L0_attn_setup()
    _L0_attn_in = {k: v for k, v in _L0_attn_all.items() if k in ('e', 'p', 'ln_w', 'W_qk', 'W_o', 'wte')}
    del _L0_attn_all

    def _L0_ffn_setup():
        import jax, jax.numpy as jnp
        import numpy as np
        B, S, D, F = (2, 128, 192, 768)
        L, H, DK = (4, 12, 64)
        E, K = (8, 2)
        NB, MAXD = (32, 128)
        MOE_LAYERS = (1, 3)
        EPS = 1e-06

        def t5_layer_norm(x, w):
            var = jnp.mean(x * x, axis=-1, keepdims=True)
            return w * x * jax.lax.rsqrt(var + EPS)

        def relative_position_bias(rel_emb, seq_len):
            ctx = jnp.arange(seq_len)[:, None]
            mem = jnp.arange(seq_len)[None, :]
            rel = mem - ctx
            nb = NB // 2
            buckets = (rel > 0).astype(jnp.int32) * nb
            n = jnp.abs(rel)
            max_exact = nb // 2
            is_small = n < max_exact
            nf = jnp.maximum(n, 1).astype(jnp.float32)
            large = max_exact + (jnp.log(nf / max_exact) / np.log(MAXD / max_exact) * (nb - max_exact)).astype(jnp.int32)
            large = jnp.minimum(large, nb - 1)
            buckets = buckets + jnp.where(is_small, n, large)
            return rel_emb[buckets].transpose(2, 0, 1)[None]

        def moe_ffn(x2d, gw, w1, w2):
            logits = x2d @ gw
            vals, idx = jax.lax.top_k(logits, K)
            gsc = jax.nn.softmax(vals, axis=-1)
            T = x2d.shape[0]
            cw = jnp.zeros((T, E), x2d.dtype).at[jnp.arange(T)[:, None], idx].add(gsc)

            def body(acc, xs):
                w1e, w2e, cwe = xs
                y = jax.nn.gelu(x2d @ w1e, approximate=False) @ w2e
                return (acc + cwe[:, None] * y, None)
            out, _ = jax.lax.scan(body, jnp.zeros_like(x2d), (w1, w2, cw.T))
            return out
        key = jax.random.key(seed)
        ks = list(jax.random.split(key, 16))

        def nrm(k, shape, scale=0.02):
            return jax.random.normal(k, shape, jnp.float32) * scale
        M = len(MOE_LAYERS)
        return {'x': nrm(ks[0], (B, S, D), 1.0), 'attn_q': nrm(ks[1], (L, D, H * DK)), 'attn_k': nrm(ks[2], (L, D, H * DK)), 'attn_v': nrm(ks[3], (L, D, H * DK)), 'attn_o': nrm(ks[4], (L, H * DK, D)), 'ffn_wi': nrm(ks[5], (L, D, F)), 'ffn_wo': nrm(ks[6], (L, F, D)), 'ln1': jnp.ones((L, D), jnp.float32), 'ln2': jnp.ones((L, D), jnp.float32), 'ln_f': jnp.ones((D,), jnp.float32), 'rel_emb': nrm(ks[7], (NB, H), 0.1), 'gate_w': nrm(ks[8], (M, D, E)), 'moe_w1': nrm(ks[9], (M, E, D, F)), 'moe_w2': nrm(ks[10], (M, E, F, D))}
    _L0_ffn_all = _L0_ffn_setup()
    _L0_ffn_in = {k: v for k, v in _L0_ffn_all.items() if k in ('attn_q', 'attn_k', 'attn_v', 'attn_o', 'ffn_wi', 'ffn_wo', 'ln1', 'ln2', 'ln_f', 'rel_emb', 'gate_w', 'moe_w1', 'moe_w2')}
    del _L0_ffn_all

    def _L1_attn_setup():
        import jax, jax.numpy as jnp
        import numpy as np
        DT = 0.01
        DAMP_MIN = 0.0005
        key = jax.random.key(seed)
        k_u, k_ar, k_ai, k_b, k_c = jax.random.split(key, 5)
        batch, seq_len, input_dim, state_dim = (8, 1024, 192, 64)
        u = jax.random.normal(k_u, (batch, seq_len, input_dim), dtype=jnp.float32)
        A_real = -jnp.abs(jax.random.normal(k_ar, (state_dim,), dtype=jnp.float32) * 0.1) - DAMP_MIN
        A_imag = jax.random.normal(k_ai, (state_dim,), dtype=jnp.float32)
        B = jax.random.normal(k_b, (state_dim, input_dim), dtype=jnp.float32) * 0.02
        C = jax.random.normal(k_c, (input_dim, state_dim), dtype=jnp.float32) * 0.02
        return {'u': u, 'A_real': A_real, 'A_imag': A_imag, 'B': B, 'C': C}
    _L1_attn_all = _L1_attn_setup()
    _L1_attn_in = {k: v for k, v in _L1_attn_all.items() if k in ('A_real', 'A_imag', 'B', 'C')}
    del _L1_attn_all

    def _L1_ffn_setup():
        import jax, jax.numpy as jnp
        import numpy as np
        B, L, D, E, F, K = (2, 256, 192, 16, 768, 2)
        key = jax.random.key(seed)
        ks = jax.random.split(key, 6)
        s = 0.02
        x = jax.random.normal(ks[0], (B, L, D), dtype=jnp.float32)
        wr = jax.random.normal(ks[1], (E, D), dtype=jnp.float32) * s
        w1 = jax.random.normal(ks[2], (E, F, D), dtype=jnp.float32) * s
        b1 = jnp.zeros((E, F), dtype=jnp.float32)
        w2 = jax.random.normal(ks[3], (E, D, F), dtype=jnp.float32) * s
        b2 = jnp.zeros((E, D), dtype=jnp.float32)
        return {'x': x, 'wr': wr, 'w1': w1, 'b1': b1, 'w2': w2, 'b2': b2}
    _L1_ffn_all = _L1_ffn_setup()
    _L1_ffn_in = {k: v for k, v in _L1_ffn_all.items() if k in ('wr', 'w1', 'b1', 'w2', 'b2')}
    del _L1_ffn_all
    return {'x': x, 'cls_tok': cls_tok, 'L0_tok_W': _L0_tok_in['W'], 'L0_attn_e': _L0_attn_in['e'], 'L0_attn_p': _L0_attn_in['p'], 'L0_attn_ln_w': _L0_attn_in['ln_w'], 'L0_attn_W_qk': _L0_attn_in['W_qk'], 'L0_attn_W_o': _L0_attn_in['W_o'], 'L0_attn_wte': _L0_attn_in['wte'], 'L0_ffn_attn_q': _L0_ffn_in['attn_q'], 'L0_ffn_attn_k': _L0_ffn_in['attn_k'], 'L0_ffn_attn_v': _L0_ffn_in['attn_v'], 'L0_ffn_attn_o': _L0_ffn_in['attn_o'], 'L0_ffn_ffn_wi': _L0_ffn_in['ffn_wi'], 'L0_ffn_ffn_wo': _L0_ffn_in['ffn_wo'], 'L0_ffn_ln1': _L0_ffn_in['ln1'], 'L0_ffn_ln2': _L0_ffn_in['ln2'], 'L0_ffn_ln_f': _L0_ffn_in['ln_f'], 'L0_ffn_rel_emb': _L0_ffn_in['rel_emb'], 'L0_ffn_gate_w': _L0_ffn_in['gate_w'], 'L0_ffn_moe_w1': _L0_ffn_in['moe_w1'], 'L0_ffn_moe_w2': _L0_ffn_in['moe_w2'], 'L1_attn_A_real': _L1_attn_in['A_real'], 'L1_attn_A_imag': _L1_attn_in['A_imag'], 'L1_attn_B': _L1_attn_in['B'], 'L1_attn_C': _L1_attn_in['C'], 'L1_ffn_wr': _L1_ffn_in['wr'], 'L1_ffn_w1': _L1_ffn_in['w1'], 'L1_ffn_b1': _L1_ffn_in['b1'], 'L1_ffn_w2': _L1_ffn_in['w2'], 'L1_ffn_b2': _L1_ffn_in['b2']}

def reference(x, cls_tok, L0_tok_W, L0_attn_e, L0_attn_p, L0_attn_ln_w, L0_attn_W_qk, L0_attn_W_o, L0_attn_wte, L0_ffn_attn_q, L0_ffn_attn_k, L0_ffn_attn_v, L0_ffn_attn_o, L0_ffn_ffn_wi, L0_ffn_ffn_wo, L0_ffn_ln1, L0_ffn_ln2, L0_ffn_ln_f, L0_ffn_rel_emb, L0_ffn_gate_w, L0_ffn_moe_w1, L0_ffn_moe_w2, L1_attn_A_real, L1_attn_A_imag, L1_attn_B, L1_attn_C, L1_ffn_wr, L1_ffn_w1, L1_ffn_b1, L1_ffn_w2, L1_ffn_b2):
    import jax
    import jax.numpy as jnp

    def _L0_tok_ref(x, W):
        import jax, jax.numpy as jnp
        import numpy as np
        B, C, IMG, P = (128, 3, 64, 16)
        HP = IMG // P
        EMBED = 192

        def dct_basis(N, dtype=jnp.float32):
            n = jnp.arange(N, dtype=dtype)
            k = jnp.arange(N, dtype=dtype)[:, None]
            return 2.0 * jnp.cos(jnp.pi * (2.0 * n + 1.0) * k / (2.0 * N))
        b = x.shape[0]
        xp = x.reshape(b, C, HP, P, HP, P).transpose(0, 2, 4, 1, 3, 5)
        D = dct_basis(P, xp.dtype)
        y = jnp.einsum('bhwcnm,kn,lm->bhwckl', xp, D, D)
        y = y.reshape(b, HP, HP, C * P * P)
        y = jnp.einsum('bhwf,ef->bhwe', y, W)
        return y.reshape(b, HP * HP, EMBED)

    def _L0_attn_ref(x, e, p, ln_w, W_qk, W_o, wte):
        import jax, jax.numpy as jnp
        import numpy as np
        import math
        B, S, E = (2, 512, 192)
        H = 12
        V = 50257
        EPS = 1e-05

        def _layernorm(x, w):
            mu = jnp.mean(x, axis=-1, keepdims=True)
            var = jnp.mean(jnp.square(x - mu), axis=-1, keepdims=True)
            return (x - mu) * jax.lax.rsqrt(var + EPS) * w
        xb, sb, eb = x.shape
        xn = _layernorm(x, ln_w)
        avg_wte = jnp.mean(wte, axis=0)
        Q = xn[:, None, :, :] * W_qk[None, :, None, :]
        attn = jnp.einsum('bhse,bhte->bhst', Q, Q) / math.sqrt(eb)
        causal = jnp.tril(jnp.ones((sb, sb), dtype=bool))
        attn = jnp.where(causal[None, None], attn, -jnp.inf)
        attn = jax.nn.softmax(attn, axis=-1)
        Vv = xn[:, None, :, :] - avg_wte[None, None, None, :]
        out = jnp.einsum('bhst,bhte->bhse', attn, Vv)
        N_reg = 1.0 / jnp.arange(1, sb + 1, dtype=jnp.float32)
        out = out * N_reg[None, None, :, None]
        out = out.transpose(0, 2, 1, 3).reshape(xb, sb, H * eb)
        out = out @ W_o.T
        return out

    def _L0_ffn_ref(x, attn_q, attn_k, attn_v, attn_o, ffn_wi, ffn_wo, ln1, ln2, ln_f, rel_emb, gate_w, moe_w1, moe_w2):
        import jax, jax.numpy as jnp
        import numpy as np
        B, S, D, F = (2, 128, 192, 768)
        L, H, DK = (4, 12, 64)
        E, K = (8, 2)
        NB, MAXD = (32, 128)
        MOE_LAYERS = (1, 3)
        EPS = 1e-06

        def t5_layer_norm(x, w):
            var = jnp.mean(x * x, axis=-1, keepdims=True)
            return w * x * jax.lax.rsqrt(var + EPS)

        def relative_position_bias(rel_emb, seq_len):
            ctx = jnp.arange(seq_len)[:, None]
            mem = jnp.arange(seq_len)[None, :]
            rel = mem - ctx
            nb = NB // 2
            buckets = (rel > 0).astype(jnp.int32) * nb
            n = jnp.abs(rel)
            max_exact = nb // 2
            is_small = n < max_exact
            nf = jnp.maximum(n, 1).astype(jnp.float32)
            large = max_exact + (jnp.log(nf / max_exact) / np.log(MAXD / max_exact) * (nb - max_exact)).astype(jnp.int32)
            large = jnp.minimum(large, nb - 1)
            buckets = buckets + jnp.where(is_small, n, large)
            return rel_emb[buckets].transpose(2, 0, 1)[None]

        def moe_ffn(x2d, gw, w1, w2):
            logits = x2d @ gw
            vals, idx = jax.lax.top_k(logits, K)
            gsc = jax.nn.softmax(vals, axis=-1)
            T = x2d.shape[0]
            cw = jnp.zeros((T, E), x2d.dtype).at[jnp.arange(T)[:, None], idx].add(gsc)

            def body(acc, xs):
                w1e, w2e, cwe = xs
                y = jax.nn.gelu(x2d @ w1e, approximate=False) @ w2e
                return (acc + cwe[:, None] * y, None)
            out, _ = jax.lax.scan(body, jnp.zeros_like(x2d), (w1, w2, cw.T))
            return out
        b, s, d = x.shape
        bias = relative_position_bias(rel_emb, s)
        h = x
        mi = 0
        for i in range(L):
            nx = t5_layer_norm(h, ln1[i])
            q = (nx @ attn_q[i]).reshape(b, s, H, DK)
            k = (nx @ attn_k[i]).reshape(b, s, H, DK)
            v = (nx @ attn_v[i]).reshape(b, s, H, DK)
            scores = jnp.einsum('bqhd,bkhd->bhqk', q, k) + bias
            attn = jax.nn.softmax(scores, axis=-1)
            ctx = jnp.einsum('bhqk,bkhd->bqhd', attn, v).reshape(b, s, H * DK)
            h = h + ctx @ attn_o[i]
            nx = t5_layer_norm(h, ln2[i])
            y = jax.nn.relu(nx @ ffn_wi[i]) @ ffn_wo[i]
            if i in MOE_LAYERS:
                y = y + moe_ffn(nx.reshape(-1, d), gate_w[mi], moe_w1[mi], moe_w2[mi]).reshape(b, s, d)
                mi += 1
            h = h + y
        return t5_layer_norm(h, ln_f)

    def _L1_attn_ref(u, A_real, A_imag, B, C):
        import jax, jax.numpy as jnp
        import numpy as np
        DT = 0.01
        DAMP_MIN = 0.0005
        dt = jnp.float32(DT)
        lam = jax.lax.complex(A_real, A_imag)
        denom = 1.0 - dt / 2 * lam
        a_d = (1.0 + dt / 2 * lam) / denom
        B_d = jnp.sqrt(dt) * B.astype(jnp.complex64) / denom[:, None]
        Bu = jnp.einsum('bsd,nd->bsn', u.astype(jnp.complex64), B_d)
        a_full = jnp.broadcast_to(a_d, Bu.shape)

        def combine(c1, c2):
            a1, b1 = c1
            a2, b2 = c2
            return (a1 * a2, a2 * b1 + b2)
        _, h = jax.lax.associative_scan(combine, (a_full, Bu), axis=1)
        y = jnp.einsum('bsn,dn->bsd', h.real, C)
        return y

    def _L1_ffn_ref(x, wr, w1, b1, w2, b2):
        import jax, jax.numpy as jnp
        import numpy as np
        B, L, D, E, F, K = (2, 256, 192, 16, 768, 2)
        logits = jnp.einsum('bld,ed->ble', x, wr)
        probs = jax.nn.softmax(logits, axis=-1)
        top_p, ix = jax.lax.top_k(probs, K)
        gate = jnp.sum(jax.nn.one_hot(ix, E, dtype=x.dtype) * top_p[..., None], axis=-2)
        h = jnp.einsum('bld,efd->blef', x, w1) + b1
        h = jax.nn.gelu(h, approximate=False)
        y = jnp.einsum('blef,edf->bled', h, w2) + b2
        out = x + jnp.einsum('bled,ble->bld', y, gate)
        return out
    h = _L0_tok_ref(x, L0_tok_W)
    h = jnp.concatenate([jnp.broadcast_to(cls_tok, (h.shape[0], 1, h.shape[2])), h], axis=1)
    h = h + _L0_attn_ref(_layernorm(h, axis=-1), L0_attn_e, L0_attn_p, L0_attn_ln_w, L0_attn_W_qk, L0_attn_W_o, L0_attn_wte)
    h = h + _L0_ffn_ref(_layernorm(h, axis=-1), L0_ffn_attn_q, L0_ffn_attn_k, L0_ffn_attn_v, L0_ffn_attn_o, L0_ffn_ffn_wi, L0_ffn_ffn_wo, L0_ffn_ln1, L0_ffn_ln2, L0_ffn_ln_f, L0_ffn_rel_emb, L0_ffn_gate_w, L0_ffn_moe_w1, L0_ffn_moe_w2)
    h = h + _L1_attn_ref(_layernorm(h, axis=-1), L1_attn_A_real, L1_attn_A_imag, L1_attn_B, L1_attn_C)
    h = h + _L1_ffn_ref(_layernorm(h, axis=-1), L1_ffn_wr, L1_ffn_w1, L1_ffn_b1, L1_ffn_w2, L1_ffn_b2)
    return h

_drawn_inputs = setup_inputs


def setup_inputs(seed=0):
    import zlib

    import numpy as np

    out = dict(_drawn_inputs(seed))
    spreads = {'L0_attn_ln_w': (1.0, 0.6),
     'L0_ffn_ln1': (1.0, 0.6),
     'L0_ffn_ln2': (1.0, 0.6),
     'L0_ffn_ln_f': (1.0, 0.6),
     'L1_ffn_b1': (0.0, 0.8),
     'L1_ffn_b2': (0.0, 2.0)}
    factors = {'cls_tok': 3.707,
     'L0_attn_W_qk': 200.0,
     'L0_attn_W_o': 3.725,
     'L0_attn_wte': 200.0,
     'L0_ffn_attn_q': 8.0,
     'L0_ffn_attn_k': 8.0,
     'L0_ffn_attn_v': 8.0,
     'L0_ffn_attn_o': 8.0,
     'L0_ffn_ffn_wi': 8.0,
     'L0_ffn_ffn_wo': 7.832,
     'L0_ffn_rel_emb': 8.0,
     'L0_ffn_gate_w': 8.0,
     'L0_ffn_moe_w1': 8.0,
     'L0_ffn_moe_w2': 8.0,
     'L1_attn_A_real': 200.0,
     'L1_attn_A_imag': 200.0,
     'L1_attn_B': 24.69,
     'L1_attn_C': 24.556,
     'L1_ffn_wr': 8.0,
     'L1_ffn_w1': 8.0,
     'L1_ffn_w2': 8.0}
    for name, (base, spread) in spreads.items():
        noise = np.random.default_rng([zlib.crc32(name.encode()), seed]).standard_normal(out[name].shape)
        drawn = base * np.exp(spread * noise) if base else spread * noise
        out[name] = jnp.asarray(drawn.astype(out[name].dtype))
    for name, factor in factors.items():
        out[name] = (out[name] * factor).astype(out[name].dtype)
    return out
```

```python
from contextlib import ExitStack

import numpy as np

import concourse.bass as bass
from concourse import mybir

F32 = mybir.dt.float32
U32 = mybir.dt.uint32
ALU = mybir.AluOpType
ACT = mybir.ActivationFunctionType
AX = mybir.AxisListType

BATCH, SEQ, D = 32, 17, 192
TOK = BATCH * SEQ
IMGS = 7
TT = IMGS * SEQ
NT = 5
TPAD = NT * TT
LAST = TOK - (NT - 1) * TT
KD = D // 2
CH = TOK // 2
H = 12
DK = 64
HD = H * DK
FF = 768
FT = FF // 128
E0, E1 = 8, 16
LAYERS = 4
NPIX = 768
VOCAB = 50257
WROWS = 14
WCH = VOCAB // 128 // WROWS
WTAIL = VOCAB - WCH * WROWS * 128
WBUF = 4
NEG = -1.0e30
DT = 0.01
NSTATE = 64


def rows(g):
    return TT if g < NT - 1 else LAST


class Chain:

    def __init__(self, eng, sem):
        self.eng, self.sem, self.base, self.n = eng, sem, 0, 0

    def link(self, ins):
        self.n += 1
        ins.then_inc(self.sem, 1)
        self.eng.wait_ge(self.sem, self.base + self.n)


def build(nc, xst, w_tok, k2, cls, wte_main, wte_tail, ln_w, wqk, wot, causal, nreg, clsmask,
          wq, wk, wv, wo, fw1, fw2, ln1, ln2, ln_f, onehot, rel_emb, block_mask, gate_w,
          ew1, ew2, eb1, a_real, a_imag, bt, ct, wr, b2, ident, iota, out):
    ctx = ExitStack()
    with ctx:
        def sb(name, shape, dt=F32):
            return ctx.enter_context(nc.sbuf_tensor(name, shape, dt))

        def sem(name):
            return ctx.enter_context(nc.semaphore(name))

        ps = ctx.enter_context(nc.psum_tensor("ps", [128, 8, 512], F32))

        res = sb("res", [TT, NT, D])
        hid = sb("hid", [TT, NT, D])
        xs = sb("xs", [TT, NT, D])
        xT = sb("xT", [KD, 2, TPAD])
        idn = sb("idn", [128, 128])
        mask_sb = sb("mask_sb", [TT, TT])
        biasM = sb("biasM", [TT, 12, TT])
        lnw_sb = sb("lnw_sb", [KD, 2, 1])
        ln1_sb = sb("ln1_sb", [KD, 2, LAYERS])
        ln2_sb = sb("ln2_sb", [KD, 2, LAYERS])
        lnc = [sb(f"lnc{i}", [KD, 2, 1]) for i in range(2)]
        idle = sb("idle", [TT, 1])
        stats = sb("stats", [TT, NT, 6])
        mv = sb("mv", [TT, NT, 2])
        rstd = sb("rstd", [TT, NT])
        mhalf = sb("mhalf", [TT, NT])
        prob = [sb(f"prob{i}", [TT, 12, TT]) for i in range(2)]
        probT = sb("probT", [TT, 12, TT])
        mx = [sb(f"mx{i}", [TT, H]) for i in range(2)]
        nmx = [sb(f"nmx{i}", [TT, H]) for i in range(2)]
        rsum = [sb(f"rsum{i}", [TT, H]) for i in range(2)]
        rinv = sb("rinv", [TT, H])
        ctxn = sb("ctxn", [TT, HD])
        ctxT = sb("ctxT", [128, 6, TT])
        wreg = sb("wreg", [128, 4 * 2 * HD + 2 * FT * D])

        def w_part(i, *shape):
            n = shape[1] * shape[2]
            return wreg[0:shape[0], i:i + n].rearrange("p (a b) -> p a b", a=shape[1]), i + n

        wq_sb, at = w_part(0, KD, 2, HD)
        wk_sb, at = w_part(at, KD, 2, HD)
        wv_sb, at = w_part(at, KD, 2, HD)
        wo_sb, at = w_part(at, 128, 6, D)
        fw1_sb, at = w_part(at, KD, 2, FF)
        fw2_sb, at = w_part(at, 128, FT, D)
        part, at = w_part(0, 128, WCH + 1, D)
        wtok_sb, at = w_part(at, 128, 6, D)
        wfold, at = w_part(at, 128, 6, D)
        k2_sb, at = w_part(at, 128, 2, 256)
        big = sb("big", [128, 3, 6 * TPAD])
        qT = big[:, 0, :].rearrange("p (m t) -> p m t", m=6)
        kT = [big[:, 1 + i, :].rearrange("p (m t) -> p m t", m=6) for i in range(2)]
        xp = qT
        xstage = big[:, 1, 0:6 * BATCH * 16].rearrange("p (m b t) -> p m b t", m=6, b=BATCH)
        big2 = sb("big2", [128, WBUF * WROWS * D])
        hidden = [big2[:, i * FT * TOK:(i + 1) * FT * TOK].rearrange("p (f t) -> p f t", f=FT)
                  for i in range(2)]
        wte_sb = big2[:, :].rearrange("p (s r d) -> p s r d", s=WBUF, r=WROWS)
        vbuf = sb("vbuf", [128, NT * HD])
        v_sb = vbuf[0:TT, :].rearrange("p (g n) -> p g n", g=NT)
        ering = sb("ering", [128, 2 * (2 * FF + FT * D)])
        esz = 2 * FF + FT * D
        ew1_sb = [ering[0:KD, i * esz:i * esz + 2 * FF].rearrange("p (k f) -> p k f", k=2) for i in range(2)]
        ew2_sb = [ering[:, i * esz + 2 * FF:(i + 1) * esz].rearrange("p (f d) -> p f d", f=FT)
                  for i in range(2)]
        wot_sb = ering[0:KD, 0:2 * H * D].rearrange("p (k h d) -> p k h d", k=2, h=H)
        po_sb = vbuf[0:TT, 0:H * D].rearrange("p (h d) -> p h d", h=H)
        eb1_sb = [sb(f"eb1_sb{i}", [128, FT]) for i in range(2)]
        cls_sb = sb("cls_sb", [TT, D])
        lnf_sb = sb("lnf_sb", [TT, D])
        wqk_sb = sb("wqk_sb", [KD, 2, H])
        qs = [prob_q.rearrange("p (k h t) -> p k h t", k=2, h=H) for prob_q in
              (big[0:KD, 1, 0:2 * H * TT], big[0:KD, 2, 0:2 * H * TT])]
        psum_all = sb("psum_all", [128, D])
        onesv = sb("onesv", [128, TT])
        avgB = sb("avgB", [KD, 2, TT])
        nreg_sb = sb("nreg_sb", [TT, 2])
        cmask_sb = sb("cmask_sb", [TT, 1])
        oh_sb = big[0:32, 2, 0:SEQ * TT].rearrange("p (s t) -> p s t", s=SEQ)
        rel_sb = sb("rel_sb", [32, H])
        R_sb = ctxn[:, 0:SEQ * H].rearrange("p (t h) -> p t h", t=SEQ)
        bmask_sb = sb("bmask_sb", [TT, TT])
        gw_sb = sb("gw_sb", [KD, 2, E0])
        wr_sb = sb("wr_sb", [KD, 2, E1])
        b2_sb = sb("b2_sb", [E1, D])
        iota_sb = sb("iota_sb", [TT, E1])
        logit = sb("logit", [TT, NT, E1])
        top = sb("top", [TT, NT, 8])
        idx = sb("idx", [TT, NT, 8], U32)
        idf = sb("idf", [TT, NT, 2])
        gsm = sb("gsm", [TT, 6, NT])
        cw = sb("cw", [TT, NT, E1])
        cwb = sb("cwb", [TT, E1])
        cwT = ctxT[0:E1, :, :].rearrange("p m t -> p (m t)")[:, 0:TPAD]
        lam = sb("lam", [NSTATE, 16])
        bt_sb = sb("bt_sb", [KD, 2, NSTATE])
        ct_sb = sb("ct_sb", [NSTATE, D])
        hst = big[0:NSTATE, 0, 0:2 * TOK].rearrange("p (c t) -> p c t", c=2)

        s_in = sem("inputs_tok")
        s_const = sem("inputs_const")
        s_cn2 = sem("inputs_const2")
        s_wte = [sem(f"wte_in{i}") for i in range(WBUF)]
        s_wtail = sem("wte_tail_in")
        s_wot = sem("wot_in")
        wte_used = sem("wte_used")
        zeroed = sem("zeroed")
        xp_ready = sem("xp_ready")
        fold_ready = sem("fold_ready")
        fold_out = sem("fold_out")
        tok_ready = sem("tok_ready")
        tok_out = sem("tok_out")
        n_stats = sem("norm_stats")
        n_rstd = sem("norm_rstd")
        n_scaled = sem("norm_scaled")
        n_T = sem("norm_transposed")
        n_outA = sem("norm_out_act")
        n_outD = sem("norm_out_dve")
        qs_ready = sem("qs_ready")
        a_s = sem("a_scores")
        a_masked = sem("a_masked")
        a_exp = sem("a_exp")
        a_norm = sem("a_normed")
        a_T = sem("a_probT")
        a_Tout = sem("a_probT_out")
        a_p = sem("a_p")
        a_pout = sem("a_p_out")
        a_y = sem("a_y")
        a_yout = sem("a_y_out")
        r_ready = sem("rel_ready")
        r_out = sem("rel_out")
        biasm_ready = sem("biasm_ready")
        avg_sum = sem("avg_sum")
        avg_T = sem("avg_T")
        avg_out = sem("avg_out")
        rbc_ready = sem("rbc_ready")
        zero_kv = sem("zero_kv")
        w_in = {n: sem(f"{n}_in") for n in ("wq", "wk", "wv", "wo", "f1", "f2")}
        e1_in = [sem(f"ew1_in{i}") for i in range(2)]
        e2_in = [sem(f"ew2_in{i}") for i in range(2)]
        eb_in = [sem(f"eb1_in{i}") for i in range(2)]
        gw_in = sem("gate_w_in")
        qk_ready = sem("qk_ready")
        q_out = sem("q_out")
        k_out = sem("k_out")
        v_ready = sem("v_ready")
        v_outA = sem("v_out_act")
        v_outD = sem("v_out_dve")
        s_ready = sem("s_ready")
        s_masked = sem("s_masked")
        s_max = sem("s_max")
        e_ready = sem("e_ready")
        at_ready = sem("at_ready")
        at_out = sem("at_out")
        ctx_ready = sem("ctx_ready")
        ctx_out = sem("ctx_out")
        ctxT_ready = sem("ctxT_ready")
        ctxT_out = sem("ctxT_out")
        o_ready = sem("o_ready")
        o_out = sem("o_out")
        up_ready = [sem(f"up_ready{i}") for i in range(2)]
        hid_out = sem("hid_out")
        down_ready = [sem(f"down_ready{i}") for i in range(2)]
        y_out = sem("y_out")
        lg_ready = sem("logits_ready")
        lg_out = sem("logits_out")
        g_mx = sem("gate_max")
        g_exp = sem("gate_exp")
        cw_ready = sem("cw_ready")
        cwT_ready = sem("cwT_ready")
        cwT_out = sem("cwT_out")
        b2_ready = sem("b2_ready")
        b2_out = sem("b2_out")
        ss_bu = sem("ss_bu")
        ss_h = sem("ss_h")
        ss_y = sem("ss_y")
        ss_yout = sem("ss_yout")
        d_chain = sem("dve_chain")
        p_chain = sem("pool_chain")
        fin = sem("fin")
        s_out = sem("out_stored")

        N_CONST = 15
        SCALE = 1.0 / float(np.sqrt(np.float32(D)))
        NORM_L = 3
        NORM_F = NORM_L + 2 * LAYERS

        def pos(h):
            return 6 * (h % 2) + h // 2

        block = ctx.enter_context(nc.Block())

        @block.sync
        def _(sp):
            sp.dma_start(wtok_sb[:, :, :], w_tok).then_inc(s_in, 16)
            sp.dma_start(k2_sb[:, :, :], k2).then_inc(s_in, 16)
            sp.dma_start(xstage.rearrange("p m b t -> p (m b t)"), xst).then_inc(s_in, 16)
            small = [(idn[:, :], ident), (cls_sb[:, :], cls.to_broadcast([TT, D])),
                     (cmask_sb[:, :], clsmask), (lnw_sb[:, :, :], ln_w), (wqk_sb[:, :, :], wqk),
                     (mask_sb[:, :], causal), (nreg_sb[:, :], nreg), (bmask_sb[:, :], block_mask),
                     (oh_sb[:, :, :], onehot), (rel_sb[:, :], rel_emb), (ln1_sb[:, :, :], ln1),
                     (ln2_sb[:, :, :], ln2), (lam[:, 0:1], a_real), (lam[:, 1:2], a_imag),
                     (iota_sb[:, :], iota)]
            assert len(small) == N_CONST
            for dst, src in small:
                sp.dma_start(dst, src).then_inc(s_const, 16)
            for j in range(WCH):
                if j == 2:
                    sp.dma_start(wot_sb, wot).then_inc(s_wot, 16)
                if j >= WBUF:
                    sp.wait_ge(wte_used, j - WBUF + 1)
                sp.dma_start(wte_sb[:, j % WBUF, :, :], wte_main[j]).then_inc(s_wte[j % WBUF], 16)
                if j == 6:
                    for dst, src in ((lnf_sb[:, :], ln_f.to_broadcast([TT, D])),
                                     (wr_sb[:, :, :], wr), (b2_sb[:, :], b2), (bt_sb[:, :, :], bt),
                                     (ct_sb[:, :], ct)):
                        sp.dma_start(dst, src).then_inc(s_cn2, 16)
            sp.wait_ge(zeroed, 2)
            sp.dma_start(part[0:WTAIL, WCH, :], wte_tail).then_inc(s_wtail, 16)
            sp.wait_ge(rbc_ready, 1)
            for L in range(LAYERS):
                lp, odd = divmod(L, 2)

                def load(dst, src, arrived, used, count):
                    if L:
                        sp.wait_ge(used, count)
                    sp.dma_start(dst, src[L]).then_inc(arrived, 16)

                load(wq_sb[:, :, :], wq, w_in["wq"], qk_ready, 12 * L)
                load(wk_sb[:, :, :], wk, w_in["wk"], qk_ready, 12 * L)
                load(wv_sb[:, :, :], wv, w_in["wv"], v_ready, NT * L)
                load(wo_sb[:, :, :], wo, w_in["wo"], o_ready, NT * L)
                u, passes = (0, 5 * lp + 1) if odd else (1, 5 * (lp - 1) + 1)
                load(fw1_sb[:, :, :], fw1, w_in["f1"], up_ready[u], FT * passes)
                load(fw2_sb[:, :, :], fw2, w_in["f2"], down_ready[u], NT * passes)
                if odd:
                    if lp:
                        sp.wait_ge(lg_ready, lp)
                    sp.dma_start(gw_sb[:, :, :], gate_w[lp]).then_inc(gw_in, 16)
                    with sp.Fori(0, E0 // 2) as ep:
                        for u in range(2):
                            e = E0 * lp + 2 * ep + u
                            sp.wait_ge(up_ready[u], FT * (5 * lp + 1 + ep))
                            sp.dma_start(ew1_sb[u], ew1[bass.ds(e, 1)].rearrange("a p k f -> (a p) k f")).then_inc(e1_in[u], 16)
                            sp.wait_ge(down_ready[u], NT * (5 * lp + 1 + ep))
                            sp.dma_start(ew2_sb[u], ew2[bass.ds(e, 1)].rearrange("a p k f -> (a p) k f")).then_inc(e2_in[u], 16)
            with sp.Fori(0, E1 // 2) as ep:
                for u in range(2):
                    e = 2 * E0 + 2 * ep + u
                    sp.wait_ge(up_ready[u], FT * (5 * LAYERS // 2 + ep))
                    sp.dma_start(ew1_sb[u], ew1[bass.ds(e, 1)].rearrange("a p k f -> (a p) k f")).then_inc(e1_in[u], 16)
                    sp.wait_ge(down_ready[u], NT * (5 * LAYERS // 2 + ep))
                    sp.dma_start(eb1_sb[u][:, :], eb1[bass.ds(2 * ep + u, 1)].rearrange("a p f -> (a p) f")).then_inc(eb_in[u], 16)
                    sp.dma_start(ew2_sb[u], ew2[bass.ds(e, 1)].rearrange("a p k f -> (a p) k f")).then_inc(e2_in[u], 16)
            sp.wait_ge(fin, 1)
            for g in range(NT):
                sp.dma_start(out[g * TT:g * TT + rows(g), :], res[0:rows(g), g, :]).then_inc(s_out, 16)
            sp.wait_ge(s_out, 16 * NT)

        @block.gpsimd
        def _(pool):
            link = Chain(pool, p_chain)

            def norm_rstd(n):
                pool.wait_ge(n_stats, n + 1)
                nc.gpsimd.tensor_tensor(rstd[:, :], rstd[:, :], mhalf[:, :], ALU.pow).then_inc(n_rstd, 1)

            nc.gpsimd.memset(xp[:, :, :], 0.0).then_inc(zeroed, 1)
            nc.gpsimd.memset(part[:, WCH, :], 0.0).then_inc(zeroed, 1)
            nc.gpsimd.memset(mhalf[:, :], -0.5).then_inc(zeroed, 1)
            nc.gpsimd.memset(onesv[:, :], 1.0 / VOCAB).then_inc(zeroed, 1)
            pool.wait_ge(s_in, 48)
            pool.wait_ge(zeroed, 4)
            for m in range(6):
                nc.gpsimd.tensor_copy(
                    xp[:, m, 0:TOK].rearrange("p (b s) -> p b s", s=SEQ)[:, :, 1:SEQ],
                    xstage[:, m, :, :]).then_inc(xp_ready, 1)
            norm_rstd(0)
            norm_rstd(1)
            pool.wait_ge(s_const, 16 * N_CONST)
            pool.wait_ge(xp_ready, 6)
            for g in range(NT):
                if g == 0:
                    pool.wait_ge(n_outA, NT)
                    pool.wait_ge(n_outD, NT)
                if g == 1:
                    pool.wait_ge(r_ready, 1)
                if g >= 2:
                    pool.wait_ge(a_s, g - 1)
                for k in range(2):
                    nc.gpsimd.tensor_tensor(
                        qs[g % 2][:, k, :, :],
                        xT[:, k, g * TT:(g + 1) * TT].unsqueeze(1).to_broadcast([KD, H, TT]),
                        wqk_sb[:, k, :].unsqueeze(2).to_broadcast([KD, H, TT]), ALU.mult).then_inc(qs_ready, 1)
            pool.wait_ge(r_out, 1)
            for h in range(H):
                last = nc.gpsimd.tensor_tensor(
                    biasM[:, pos(h), :].rearrange("p (b t) -> p b t", b=IMGS),
                    bmask_sb[:, :].rearrange("p (b t) -> p b t", b=IMGS),
                    R_sb[:, :, h].unsqueeze(1).to_broadcast([TT, IMGS, SEQ]), ALU.add)
                last.then_inc(biasm_ready, 1)
            pool.wait_ge(biasm_ready, H)
            pool.wait_ge(a_s, NT)
            for n, room in enumerate((kT[0][64:128, :, :], kT[1][0:64, :, :], qT[:, :, TOK:TPAD],
                                      kT[0][0:64, :, TOK:TPAD], kT[1][64:128, :, TOK:TPAD])):
                nc.gpsimd.memset(room, 0.0).then_inc(zero_kv, 1)
                pool.wait_ge(zero_kv, n + 1)
            norm_rstd(2)
            with pool.Fori(0, LAYERS) as L:
                norm_rstd(NORM_L + 2 * L)
                norm_rstd(NORM_L + 1 + 2 * L)
            for n in range(NORM_F, NORM_F + 3):
                norm_rstd(n)

        @block.scalar
        def _(act):
            def norm_out(v, col=None):
                for g in range(NT):
                    act.wait_ge(n_T, NT * v + g + 1)
                    src = ps[0:KD, 4 + g % 2, 0:TT]
                    dst = xT[:, 0, g * TT:(g + 1) * TT]
                    if col is None:
                        nc.scalar.activation(dst, src, ACT.Copy).then_inc(n_outA, 1)
                    else:
                        nc.scalar.activation(dst, src, ACT.Copy, scale=col[:, 0, :]).then_inc(n_outA, 1)

            def exps(i, scale):
                for h in range(H):
                    last = nc.scalar.activation(prob[i][:, pos(h), :], prob[i][:, pos(h), :], ACT.Exp,
                                                bias=nmx[i][:, h:h + 1], scale=scale,
                                                accum_out=rsum[i][:, h:h + 1])
                return last

            for f in range(6):
                act.wait_ge(fold_ready, f + 1)
                nc.scalar.activation(wfold[:, f, :], ps[:, f % 4, 0:D],
                                     ACT.Copy).then_inc(fold_out, 1)
            act.wait_ge(s_const, 16 * N_CONST)
            norm_out(0, lnw_sb)
            for g in range(NT):
                act.wait_ge(a_masked, g + 1)
                exps(g % 2, SCALE).then_inc(a_exp, 1)
                for b in range(6):
                    act.wait_ge(a_p, 6 * g + b + 1)
                    nc.scalar.activation(po_sb[:, 2 * b:2 * b + 2, :].rearrange("p h d -> p (h d)"),
                                         ps[0:TT, 6 + b % 2, 0:2 * D], ACT.Copy).then_inc(a_pout, 1)
                for r in range(3):
                    act.wait_ge(a_T, 3 * g + r + 1)
                    nc.scalar.activation(probT[:, 4 * r:4 * r + 4, :].rearrange("p h t -> p (h t)"),
                                         ps[0:TT, 4 + r % 2, 0:4 * TT], ACT.Copy).then_inc(a_Tout, 1)
            act.wait_ge(avg_T, 1)
            nc.scalar.activation(avgB[:, :, :], ps[0:KD, 4, 0:2 * TT].rearrange("p (k t) -> p k t", k=2),
                                 ACT.Copy).then_inc(avg_out, 1)

            def hidden_out(j, u, func, bias=None):
                for f in range(FT):
                    act.wait_ge(up_ready[u], FT * j + f + 1)
                    b = 0.0 if bias is None else bias[:, f:f + 1]
                    nc.scalar.activation(hidden[u][:, f, :].rearrange("p (c n) -> p c n", c=2),
                                         ps[:, 2 * (f % 2):2 * (f % 2) + 2, 0:CH], func, bias=b).then_inc(hid_out, 1)

            act.wait_ge(zero_kv, 5)
            with act.Fori(0, LAYERS // 2) as lp:
                for odd in range(2):
                    L = 2 * lp + odd
                    norm_out(1 + 2 * L, lnc[0])
                    for m in range(6):
                        act.wait_ge(qk_ready, 12 * L + 2 * m + 1)
                        nc.scalar.activation(qT[:, m, 0:TOK].rearrange("p (c n) -> p c n", c=2),
                                             ps[:, 0:2, 0:CH], ACT.Copy).then_inc(q_out, 1)
                    for g in range(0, NT, 2):
                        act.wait_ge(v_ready, NT * L + g + 1)
                        nc.scalar.activation(v_sb[:, g, :].rearrange("p (c n) -> p c n", c=2),
                                             ps[0:TT, 4:6, 0:HD // 2], ACT.Copy).then_inc(v_outA, 1)

                    def ctx_transposed_out(g):
                        if g >= 1:
                            act.wait_ge(o_ready, NT * L + g)
                        for c, (m0, m1) in enumerate(((0, 4), (4, 6))):
                            bank = 4 + (25 * odd + 5 * g + 3 + c) % 2
                            act.wait_ge(ctxT_ready, 2 * (NT * L + g) + c + 1)
                            nc.scalar.activation(ctxT[:, m0:m1, :].rearrange("p m t -> p (m t)"),
                                                 ps[:, bank, 0:(m1 - m0) * TT], ACT.Copy).then_inc(ctxT_out, 1)

                    for g in range(-2, NT):
                        if g >= 1:
                            ctx_transposed_out(g - 1)
                        if g + 2 < NT:
                            act.wait_ge(s_max, NT * L + g + 3)
                            exps(g % 2, 1.0).then_inc(e_ready, 1)
                    ctx_transposed_out(NT - 1)
                    norm_out(2 + 2 * L, lnc[1])
                    if odd:
                        act.wait_ge(g_mx, lp + 1)
                        nc.scalar.activation(gsm[:, 1, :], gsm[:, 0, :], ACT.Exp).then_inc(g_exp, 1)
                    hidden_out(5 * lp, odd, ACT.Relu)
                with act.Fori(0, E0 // 2) as ep:
                    for u in range(2):
                        hidden_out(5 * lp + 1 + ep, u, ACT.Gelu)
            norm_out(1 + 2 * LAYERS)
            norm_out(2 + 2 * LAYERS)
            act.wait_ge(g_mx, LAYERS // 2 + 1)
            for g in range(NT):
                nc.scalar.activation(cw[:, g, :], logit[:, g, :], ACT.Exp, bias=gsm[:, 0, g:g + 1],
                                     accum_out=gsm[:, 1, g:g + 1]).then_inc(g_exp, 1)
            act.wait_ge(cwT_ready, NT)
            nc.scalar.activation(cwT[:, 0:4 * TT], ps[0:E1, 2, 0:4 * TT], ACT.Copy).then_inc(cwT_out, 1)
            nc.scalar.activation(cwT[:, 4 * TT:], ps[0:E1, 3, 0:TT], ACT.Copy).then_inc(cwT_out, 1)
            with act.Fori(0, E1 // 2) as ep:
                for u in range(2):
                    act.wait_ge(eb_in[u], 16 * (ep + 1))
                    hidden_out(5 * LAYERS // 2 + ep, u, ACT.Gelu, eb1_sb[u])

        @block.vector
        def _(dve):
            chain = Chain(dve, d_chain)
            link = chain.link
            V = nc.vector

            def layer_norm(n, src, dst, eps, signal):
                for g in range(NT):
                    last = V.bn_stats(stats[:, g, :], src[:, g, :])
                link(last)
                for g in range(NT):
                    last = V.bn_aggr(mv[:, g, :], stats[:, g, :])
                link(last)
                V.tensor_scalar(rstd[:, :], mv[:, :, 1], eps, None, ALU.add).then_inc(n_stats, 1)
                dve.wait_ge(n_rstd, n + 1)
                for g in range(NT):
                    ins = V.tensor_scalar(dst[:, g, :], src[:, g, :], mv[:, g, 0:1], rstd[:, g:g + 1],
                                          ALU.subtract, ALU.mult)
                    if signal:
                        ins.then_inc(n_scaled, 1)
                    elif g == NT - 1:
                        link(ins)

            def t5_norm(n, src, dst, signal):
                for g in range(NT):
                    last = V.tensor_tensor_reduce(out=dst[:, g, :], in0=src[:, g, :], in1=src[:, g, :], scale=1.0 / D,
                                                  scalar=0.0, op0=ALU.mult, op1=ALU.add, accum_out=mv[:, g, 1:2])
                link(last)
                V.tensor_scalar(rstd[:, :], mv[:, :, 1], 1e-6, None, ALU.add).then_inc(n_stats, 1)
                dve.wait_ge(n_rstd, n + 1)
                for g in range(NT):
                    ins = V.tensor_scalar(dst[:, g, :], src[:, g, :], rstd[:, g:g + 1], None, ALU.mult)
                    if signal:
                        ins.then_inc(n_scaled, 1)
                    elif g == NT - 1:
                        link(ins)

            def norm_out(v, col=None):
                for g in range(NT):
                    dve.wait_ge(n_T, NT * v + g + 1)
                    src = ps[0:KD, 6 + g % 2, 0:TT]
                    dst = xT[:, 1, g * TT:(g + 1) * TT]
                    if col is None:
                        V.tensor_copy(dst, src).then_inc(n_outD, 1)
                    else:
                        V.tensor_scalar(dst, src, col[:, 1, :], None, ALU.mult).then_inc(n_outD, 1)

            dve.wait_ge(s_const, 16 * N_CONST)
            c = lambda i: lam[:, i:i + 1]
            link(V.tensor_scalar(c(2), c(0), -DT / 2, 1.0, ALU.mult, ALU.add))
            link(V.tensor_scalar(c(3), c(0), DT / 2, 1.0, ALU.mult, ALU.add))
            link(V.tensor_scalar(c(4), c(1), DT / 2, None, ALU.mult))
            link(V.tensor_tensor(c(5), c(2), c(2), ALU.mult))
            link(V.tensor_tensor(c(6), c(4), c(4), ALU.mult))
            link(V.tensor_tensor(c(5), c(5), c(6), ALU.add))
            link(V.reciprocal(c(6), c(5)))
            link(V.tensor_tensor(c(7), c(2), c(6), ALU.mult))
            link(V.tensor_tensor(c(8), c(4), c(6), ALU.mult))
            link(V.tensor_tensor(c(9), c(3), c(7), ALU.mult))
            link(V.tensor_tensor(c(10), c(4), c(8), ALU.mult))
            link(V.tensor_tensor(c(9), c(9), c(10), ALU.subtract))
            link(V.tensor_tensor(c(10), c(3), c(8), ALU.mult))
            link(V.tensor_tensor(c(11), c(4), c(7), ALU.mult))
            link(V.tensor_tensor(c(10), c(10), c(11), ALU.add))
            link(V.tensor_scalar(c(11), c(10), -1.0, None, ALU.mult))
            rt = float(np.sqrt(np.float32(DT)))
            link(V.tensor_scalar(c(12), c(7), rt, None, ALU.mult))
            link(V.tensor_scalar(c(13), c(8), rt, None, ALU.mult))
            for g in range(NT):
                dve.wait_ge(tok_ready, g + 1)
                V.scalar_tensor_tensor(
                    out=res[:, g, :], in0=cls_sb[:, :], scalar=cmask_sb[:, 0:1],
                    in1=ps[0:TT, 4 + g % 4, 0:D], op0=ALU.mult, op1=ALU.add).then_inc(tok_out, 1)
            dve.wait_ge(tok_out, NT)
            layer_norm(0, res, xs, 1e-5, False)
            layer_norm(1, xs, xs, 1e-5, True)
            norm_out(0, lnw_sb)
            dve.wait_ge(r_ready, 1)
            V.tensor_copy(R_sb[:, :, :].rearrange("p t h -> p (t h)"), ps[0:TT, 7, 0:SEQ * H]).then_inc(r_out, 1)

            def sum_wte(j):
                dve.wait_ge(s_wte[j % WBUF], 16 * (j // WBUF + 1))
                V.tensor_reduce(part[:, j, :], wte_sb[:, j % WBUF, :, :].rearrange("p r d -> p d r"),
                                AX.X, ALU.add).then_inc(wte_used, 1)

            for g in range(NT):
                i = g % 2
                dve.wait_ge(a_s, g + 1)
                if g >= 2:
                    dve.wait_ge(a_T, 3 * (g - 1))
                link(V.tensor_tensor(
                    prob[i][:, :, :].rearrange("p (c h) t -> p c h t", c=4),
                    ps[0:TT, 0:4, 0:3 * TT].rearrange("p c (h t) -> p c h t", h=3),
                    mask_sb[:, :].unsqueeze(1).unsqueeze(1).to_broadcast([TT, 4, 3, TT]), ALU.add))
                link(V.tensor_reduce(mx[i][:, :].rearrange("p (h c) -> p c h", c=2),
                                     prob[i][:, :, :].rearrange("p (c h) t -> p c h t", c=2), AX.X, ALU.max))
                V.tensor_scalar(nmx[i][:, :], mx[i][:, :], -SCALE, None, ALU.mult).then_inc(a_masked, 1)
                for j in range(4 * g, 4 * g + 4):
                    sum_wte(j)
                dve.wait_ge(a_exp, g + 1)
                link(V.reciprocal(rinv[:, :], rsum[i][:, :]))
                link(V.tensor_scalar(rinv[:, :], rinv[:, :], nreg_sb[:, 0:1], None, ALU.mult))
                V.tensor_tensor(prob[i][:, :, :].rearrange("p (c h) t -> p c h t", c=2),
                                prob[i][:, :, :].rearrange("p (c h) t -> p c h t", c=2),
                                rinv[:, :].rearrange("p (h c) -> p c h", c=2).unsqueeze(3).to_broadcast([TT, 2, 6, TT]),
                                ALU.mult).then_inc(a_norm, 1)
                dve.wait_ge(a_y, g + 1)
                V.tensor_tensor(res[:, g, :], res[:, g, :], ps[0:TT, 5, 0:D], ALU.add).then_inc(a_yout, 1)
            for j in range(4 * NT, WCH):
                sum_wte(j)
            dve.wait_ge(wte_used, WCH)
            dve.wait_ge(s_wtail, 16)
            V.tensor_reduce(psum_all[:, :], part[:, :, :].rearrange("p j d -> p d j"), AX.X, ALU.add).then_inc(avg_sum, 1)
            dve.wait_ge(rbc_ready, 1)
            dve.wait_ge(a_yout, NT)
            for g in range(NT):
                last = V.scalar_tensor_tensor(out=res[:, g, :], in0=ps[0:TT, 5, 0:D], scalar=nreg_sb[:, 1:2],
                                              in1=res[:, g, :], op0=ALU.mult, op1=ALU.add)
            link(last)
            layer_norm(2, res, hid, 1e-5, False)
            dve.wait_ge(biasm_ready, H)
            dve.wait_ge(zero_kv, 5)

            def gate_weights(v, width):
                for g in range(NT):
                    link(V.tensor_scalar(cwb[:, 0:width], iota_sb[:, 0:width], idf[:, g, 0:1], gsm[:, 2, g:g + 1],
                                         ALU.is_equal, ALU.mult))
                    link(V.tensor_scalar(cw[:, g, 0:width], iota_sb[:, 0:width], idf[:, g, 1:2], gsm[:, 3, g:g + 1],
                                         ALU.is_equal, ALU.mult))
                    ins = V.tensor_tensor(cw[:, g, 0:width], cw[:, g, 0:width], cwb[:, 0:width], ALU.add)
                    if g == NT - 1:
                        ins.then_inc(cw_ready, 1)
                        dve.wait_ge(cw_ready, v + 1)
                    else:
                        link(ins)

            def top2(src, width):
                V.memset(idle[:, :], 0.0)
                for g in range(NT):
                    last = V.max(top[:, g, :], src[:, g, 0:width])
                link(last)
                V.memset(idle[:, :], 0.0)
                for g in range(NT):
                    last = V.max_index(idx[:, g, :], top[:, g, :], src[:, g, 0:width])
                link(last)
                link(V.tensor_copy(idf[:, :, :], idx[:, :, 0:2]))

            def layer(lp, odd, base, per):
                L = 2 * lp + odd
                chain.base, chain.n = base, 0
                for w, src in enumerate((ln1_sb, ln2_sb)):
                    last = V.tensor_copy(lnc[w][:, :, :], src[:, :, bass.ds(L, 1)])
                link(last)
                t5_norm(NORM_L + 2 * L, hid, xs, True)
                norm_out(1 + 2 * L, lnc[0])
                for m in range(6):
                    dve.wait_ge(qk_ready, 12 * L + 2 * m + 2)
                    V.tensor_copy(kT[0][0:64, m, 0:TOK].rearrange("p (c n) -> p c n", c=2), ps[0:64, 2:4, 0:CH])
                    V.tensor_copy(kT[1][64:128, m, 0:TOK].rearrange("p (c n) -> p c n", c=2),
                                  ps[64:128, 2:4, 0:CH]).then_inc(k_out, 1)
                for g in range(1, NT, 2):
                    dve.wait_ge(v_ready, NT * L + g + 1)
                    V.tensor_copy(v_sb[:, g, :].rearrange("p (c n) -> p c n", c=2),
                                  ps[0:TT, 6:8, 0:HD // 2]).then_inc(v_outD, 1)

                def masked_max(g):
                    i = g % 2
                    dve.wait_ge(s_ready, NT * L + g + 1)
                    ins = V.tensor_tensor(
                        prob[i][:, :, :].rearrange("p (c h) t -> p c (h t)", c=4), ps[0:TT, 0:4, 0:3 * TT],
                        biasM[:, :, :].rearrange("p (c h) t -> p c (h t)", c=4), ALU.add)
                    ins.then_inc(s_masked, 1)
                    dve.wait_ge(s_masked, NT * L + g + 1)
                    link(V.tensor_reduce(mx[i][:, :].rearrange("p (h c) -> p c h", c=2),
                                         prob[i][:, :, :].rearrange("p (c h) t -> p c h t", c=2), AX.X, ALU.max))
                    V.tensor_scalar(nmx[i][:, :], mx[i][:, :], -1.0, None, ALU.mult).then_inc(s_max, 1)

                def add_o(g):
                    dve.wait_ge(o_ready, NT * L + g + 1)
                    V.tensor_tensor(hid[:, g, :], hid[:, g, :], ps[0:TT, 7, 0:D], ALU.add).then_inc(o_out, 1)

                for g in range(-2, NT):
                    if g >= 0:
                        for r in range(3):
                            bank = 4 + (25 * odd + 5 * g + r) % 2
                            dve.wait_ge(at_ready, 3 * (NT * L + g) + r + 1)
                            V.tensor_copy(probT[:, 4 * r:4 * r + 4, :].rearrange("p h t -> p (h t)"),
                                          ps[0:TT, bank, 0:4 * TT]).then_inc(at_out, 1)
                        link(V.reciprocal(rinv[:, :], rsum[g % 2][:, :]))
                        dve.wait_ge(ctx_ready, NT * L + g + 1)
                        V.tensor_tensor(ctxn[:, :].rearrange("p (h d) -> p h d", h=H),
                                        ps[0:TT, 6:8, :].rearrange("p c n -> p (c n)")[:, 0:HD].rearrange(
                                            "p (h d) -> p h d", h=H),
                                        rinv[:, :].unsqueeze(2).to_broadcast([TT, H, DK]), ALU.mult).then_inc(ctx_out, 1)
                    if g + 2 < NT:
                        masked_max(g + 2)
                    if g >= 1:
                        add_o(g - 1)
                add_o(NT - 1)
                dve.wait_ge(o_out, NT * (L + 1))
                t5_norm(NORM_L + 1 + 2 * L, hid, xs, True)
                norm_out(2 + 2 * L, lnc[1])
                if odd:
                    dve.wait_ge(lg_ready, lp + 1)
                    V.tensor_copy(logit[:, :, 0:E0], ps[0:TT, 7, 0:NT * E0].rearrange(
                        "p (g e) -> p g e", g=NT)).then_inc(lg_out, 1)
                    dve.wait_ge(lg_out, lp + 1)
                    top2(logit, E0)
                    V.tensor_tensor(gsm[:, 0, :], top[:, :, 1], top[:, :, 0], ALU.subtract).then_inc(g_mx, 1)
                    dve.wait_ge(g_exp, lp + 1)
                    link(V.tensor_scalar(gsm[:, 4, :], gsm[:, 1, :], 1.0, None, ALU.add))
                    link(V.reciprocal(gsm[:, 2, :], gsm[:, 4, :]))
                    link(V.tensor_tensor(gsm[:, 3, :], gsm[:, 1, :], gsm[:, 2, :], ALU.mult))
                    gate_weights(lp, E0)
                add_ffn(10 * lp + odd, 5 * lp, odd)
                assert chain.n == per, (odd, chain.n)

            def add_ffn(t, j, u):
                for g in range(NT):
                    dve.wait_ge(down_ready[u], NT * j + g + 1)
                    r = rows(g)
                    V.tensor_tensor(hid[0:r, g, :], hid[0:r, g, :],
                                    ps[0:r, 4 + g % 4, 0:D], ALU.add).then_inc(y_out, 1)
                dve.wait_ge(y_out, NT * (t + 1))
                V.memset(idle[:, :], 0.0)

            def add_expert(t, j, u, e, dst):
                dve.wait_ge(y_out, NT * t)
                for g in range(NT):
                    dve.wait_ge(down_ready[u], NT * j + g + 1)
                    r = rows(g)
                    V.scalar_tensor_tensor(out=dst[0:r, g, :],
                                           in0=ps[0:r, 4 + g % 4, 0:D],
                                           scalar=cw[0:r, g, bass.ds(e, 1)], in1=dst[0:r, g, :],
                                           op0=ALU.mult, op1=ALU.add).then_inc(y_out, 1)

            base = chain.n
            PER = [2 + NT + NT + 1, 2 + NT + NT + 1 + 3 + 3 + 3 * NT - 1]
            with dve.Fori(0, LAYERS // 2) as lp:
                for odd in range(2):
                    layer(lp, odd, base + (PER[0] + PER[1]) * lp + PER[0] * odd, PER[odd])
                with dve.Fori(0, E0 // 2) as ep:
                    for u in range(2):
                        add_expert(10 * lp + 2 + 2 * ep + u, 5 * lp + 1 + ep, u, 2 * ep + u, hid)
            chain.base, chain.n = 0, base + (PER[0] + PER[1]) * (LAYERS // 2)
            dve.wait_ge(y_out, NT * 20)
            t5_norm(NORM_F, hid, xs, False)
            dve.wait_ge(s_cn2, 16 * 5)
            for g in range(NT):
                last = V.tensor_tensor(xs[:, g, :], xs[:, g, :], lnf_sb[:, :], ALU.mult)
            link(last)
            for g in range(NT):
                last = V.tensor_tensor(res[:, g, :], res[:, g, :], xs[:, g, :], ALU.add)
            link(last)
            layer_norm(NORM_F + 1, res, xs, 1e-5, True)
            norm_out(1 + 2 * LAYERS)
            dve.wait_ge(ss_bu, 1)
            for k in range(2):
                last = V.tensor_scalar(hst[:, k, :].rearrange("p (c n) -> p c n", c=2), ps[0:NSTATE, 0:2, 0:CH],
                                       c(12 + k), None, ALU.mult)
            link(last)
            hv = hst.rearrange("p c (b s) -> p c b s", s=SEQ)
            for t in range(1, SEQ):
                link(V.scalar_tensor_tensor(out=hv[:, :, :, t], in0=hv[:, :, :, t - 1], scalar=c(9),
                                            in1=hv[:, :, :, t], op0=ALU.mult, op1=ALU.add))
                V.scalar_tensor_tensor(out=hv[:, 0, :, t], in0=hv[:, 1, :, t - 1], scalar=c(11),
                                       in1=hv[:, 0, :, t], op0=ALU.mult, op1=ALU.add)
                link(V.scalar_tensor_tensor(out=hv[:, 1, :, t], in0=hv[:, 0, :, t - 1], scalar=c(10),
                                            in1=hv[:, 1, :, t], op0=ALU.mult, op1=ALU.add))
            V.tensor_copy(lam[:, 14:15], lam[:, 13:14]).then_inc(ss_h, 1)
            for g in range(NT):
                dve.wait_ge(ss_y, g + 1)
                r = rows(g)
                V.tensor_tensor(res[0:r, g, :], res[0:r, g, :],
                                ps[0:r, 4 + g % 4, 0:D], ALU.add).then_inc(ss_yout, 1)
            dve.wait_ge(ss_yout, NT)
            layer_norm(NORM_F + 2, res, xs, 1e-5, True)
            norm_out(2 + 2 * LAYERS)
            dve.wait_ge(n_scaled, NT * (3 + 2 * LAYERS))
            for g in range(NT):
                last = V.tensor_tensor(res[:, g, :], res[:, g, :], xs[:, g, :], ALU.add)
            link(last)
            dve.wait_ge(lg_ready, LAYERS // 2 + 1)
            link(V.tensor_copy(logit[:, :, :], ps[0:TT, 0, 0:NT * E1].rearrange("p (g e) -> p g e", g=NT)))
            link(V.tensor_reduce(gsm[:, 5, :], logit[:, :, :], AX.X, ALU.max))
            V.tensor_scalar(gsm[:, 0, :], gsm[:, 5, :], -1.0, None, ALU.mult).then_inc(g_mx, 1)
            dve.wait_ge(g_exp, LAYERS // 2 + NT)
            link(V.reciprocal(gsm[:, 4, :], gsm[:, 1, :]))
            link(V.tensor_tensor(logit[:, :, :], cw[:, :, :],
                                 gsm[:, 4, :].unsqueeze(2).to_broadcast([TT, NT, E1]), ALU.mult))
            top2(logit, E1)
            for k in range(2):
                last = V.tensor_copy(gsm[:, 2 + k, :], top[:, :, k])
            link(last)
            gate_weights(LAYERS // 2, E1)
            for g in range(NT):
                dve.wait_ge(b2_ready, g + 1)
                r = rows(g)
                V.tensor_tensor(res[0:r, g, :], res[0:r, g, :], ps[0:r, 4 + g % 4, 0:D], ALU.add).then_inc(b2_out, 1)
            dve.wait_ge(b2_out, NT)
            with dve.Fori(0, E1 // 2) as ep:
                for u in range(2):
                    add_expert(20 + 2 * ep + u, 5 * LAYERS // 2 + ep, u, 2 * ep + u, res)
            dve.wait_ge(y_out, NT * 36)
            V.tensor_copy(lam[:, 14:15], lam[:, 13:14]).then_inc(fin, 1)

        @block.tensor
        def _(pe):
            T = nc.tensor

            def slot(g, n=TT):
                return ps[0:n, 4 + g % 4, 0:D]

            def tile(g, r=TT):
                return slice(g * TT, g * TT + r)

            def norm_transposes(v):
                for g in range(NT):
                    pe.wait_ge(n_scaled, NT * v + g + 1)
                    if g >= 2:
                        pe.wait_ge(n_outA, NT * v + g - 1)
                        pe.wait_ge(n_outD, NT * v + g - 1)
                    for k in range(2):
                        last = T.transpose(ps[0:KD, 4 + 2 * k + g % 2, 0:TT],
                                           xs[:, g, k * KD:(k + 1) * KD], idn[0:TT, 0:TT])
                    last.then_inc(n_T, 1)

            def normed(v):
                pe.wait_ge(n_outA, NT * (v + 1))
                pe.wait_ge(n_outD, NT * (v + 1))

            pe.wait_ge(s_in, 48)
            for f in range(6):
                if f >= 4:
                    pe.wait_ge(fold_out, f - 3)
                for i in range(2):
                    last = T.matmul(ps[:, f % 4, 0:D],
                                    k2_sb[:, i, (f % 2) * 128:(f % 2) * 128 + 128], wtok_sb[:, 2 * (f // 2) + i, :],
                                    start=(i == 0), stop=(i == 1))
                last.then_inc(fold_ready, 1)
            pe.wait_ge(fold_out, 6)
            pe.wait_ge(xp_ready, 6)
            for g in range(NT):
                if g == NT - 1:
                    pe.wait_ge(tok_out, 1)
                for k in range(6):
                    last = T.matmul(slot(g), xp[:, k, tile(g)], wfold[:, k, :], start=(k == 0), stop=(k == 5))
                last.then_inc(tok_ready, 1)
            pe.wait_ge(s_const, 16 * N_CONST)
            norm_transposes(0)
            normed(0)
            for t in range(SEQ):
                last = T.matmul(ps[0:TT, 7, t * H:(t + 1) * H], oh_sb[:, t, :], rel_sb[:, :], start=True, stop=True)
            last.then_inc(r_ready, 1)
            def scores(g):
                pe.wait_ge(qs_ready, 2 * (g + 1))
                if g >= 1:
                    pe.wait_ge(a_masked, g)
                for h in range(H):
                    p = pos(h)
                    for k in range(2):
                        last = T.matmul(ps[0:TT, p // 3, (p % 3) * TT:(p % 3 + 1) * TT], qs[g % 2][:, k, h, :],
                                        qs[g % 2][:, k, h, :], start=(k == 0), stop=(k == 1))
                last.then_inc(a_s, 1)

            scores(0)
            pe.wait_ge(s_wot, 16)
            pe.wait_ge(r_out, 1)
            for g in range(NT):
                for b in range(6):
                    n = 6 * g + b
                    if n >= 2:
                        pe.wait_ge(a_pout, n - 1)
                    for k in range(2):
                        last = T.matmul(ps[0:TT, 6 + b % 2, 0:2 * D], xT[:, k, tile(g)],
                                        wot_sb[:, k, 2 * b:2 * b + 2, :].rearrange("p h d -> p (h d)"),
                                        start=(k == 0), stop=(k == 1))
                    last.then_inc(a_p, 1)
                if g + 1 < NT:
                    scores(g + 1)
                pe.wait_ge(a_norm, g + 1)
                for r in range(3):
                    if r == 1 and g >= 1:
                        pe.wait_ge(a_yout, g)
                    if r == 2:
                        pe.wait_ge(a_Tout, 3 * g + 1)
                    for q in range(4):
                        last = T.transpose(ps[0:TT, 4 + r % 2, q * TT:(q + 1) * TT], prob[g % 2][:, 4 * r + q, :],
                                           idn[0:TT, 0:TT])
                    last.then_inc(a_T, 1)
                pe.wait_ge(a_Tout, 3 * (g + 1))
                pe.wait_ge(a_pout, 6 * (g + 1))
                for h in range(H):
                    last = T.matmul(ps[0:TT, 5, 0:D], probT[:, pos(h), :], po_sb[:, h, :], start=(h == 0), stop=(h == H - 1))
                last.then_inc(a_y, 1)
            pe.wait_ge(avg_sum, 1)
            pe.wait_ge(zeroed, 4)
            for k in range(2):
                last = T.matmul(ps[0:KD, 4, k * TT:(k + 1) * TT], psum_all[:, k * KD:(k + 1) * KD], onesv[:, :],
                                start=True, stop=True)
            last.then_inc(avg_T, 1)
            pe.wait_ge(avg_out, 1)
            for h in range(H):
                for k in range(2):
                    last = T.matmul(ps[0:TT, 5, 0:D], avgB[:, k, :], wot_sb[:, k, h, :],
                                    start=(h == 0 and k == 0), stop=(h == H - 1 and k == 1))
            last.then_inc(rbc_ready, 1)
            pe.wait_ge(zero_kv, 5)

            def up(t, u, w1):
                for f in range(FT):
                    if f >= 2:
                        pe.wait_ge(hid_out, FT * t + f - 1)
                    for c in range(2):
                        for k in range(2):
                            last = T.matmul(ps[:, 2 * (f % 2) + c, 0:CH], w1[:, k, f * 128:(f + 1) * 128],
                                            xT[:, k, c * CH:(c + 1) * CH], start=(k == 0), stop=(k == 1))
                    last.then_inc(up_ready[u], 1)

            def down(t, u, w2, first=False):
                if not first:
                    pe.wait_ge(y_out, NT * t)
                for g in range(NT):
                    if g == NT - 1:
                        pe.wait_ge(y_out, NT * t + 1)
                    for f in range(FT):
                        if g == 0:
                            pe.wait_ge(hid_out, FT * t + f + 1)
                        last = T.matmul(slot(g, rows(g)), hidden[u][:, f, tile(g, rows(g))], w2[:, f, :],
                                        start=(f == 0), stop=(f == FT - 1))
                    last.then_inc(down_ready[u], 1)

            with pe.Fori(0, LAYERS // 2) as lp:
                for odd in range(2):
                    L = 2 * lp + odd
                    norm_transposes(1 + 2 * L)
                    pe.wait_ge(w_in["wq"], 16 * (L + 1))
                    pe.wait_ge(w_in["wk"], 16 * (L + 1))
                    normed(1 + 2 * L)
                    for m in range(6):
                        for b, w, read in ((0, wq_sb, q_out), (2, wk_sb, k_out)):
                            if m >= 1:
                                pe.wait_ge(read, 6 * L + m)
                            for c in range(2):
                                for k in range(2):
                                    last = T.matmul(ps[:, b + c, 0:CH], w[:, k, m * 128:(m + 1) * 128],
                                                    xT[:, k, c * CH:(c + 1) * CH], start=(k == 0), stop=(k == 1))
                            last.then_inc(qk_ready, 1)
                    pe.wait_ge(w_in["wv"], 16 * (L + 1))
                    for g in range(NT):
                        if g >= 2:
                            if g % 2 == 0:
                                pe.wait_ge(v_outA, 3 * L + g // 2)
                            else:
                                pe.wait_ge(v_outD, 2 * L + g // 2)
                        for c in range(2):
                            for k in range(2):
                                last = T.matmul(ps[0:TT, 4 + 2 * (g % 2) + c, 0:HD // 2], xT[:, k, tile(g)],
                                                wv_sb[:, k, c * (HD // 2):(c + 1) * (HD // 2)],
                                                start=(k == 0), stop=(k == 1))
                        last.then_inc(v_ready, 1)

                    def scores2(g):
                        if g == 0:
                            pe.wait_ge(q_out, 6 * (L + 1))
                            pe.wait_ge(k_out, 6 * (L + 1))
                        else:
                            pe.wait_ge(s_masked, NT * L + g)
                        for h in range(H):
                            p = pos(h)
                            last = T.matmul(ps[0:TT, p // 3, (p % 3) * TT:(p % 3 + 1) * TT], qT[:, h // 2, tile(g)],
                                            kT[h % 2][:, h // 2, tile(g)], start=True, stop=True)
                        last.then_inc(s_ready, 1)

                    def ctx_transposes(g):
                        pe.wait_ge(ctx_out, NT * L + g + 1)
                        for c, (m0, m1) in enumerate(((0, 4), (4, 6))):
                            use = 5 * g + 3 + c
                            wait_bank(use)
                            for m in range(m0, m1):
                                last = T.transpose(ps[:, 4 + (25 * odd + use) % 2, (m - m0) * TT:(m - m0 + 1) * TT],
                                                   ctxn[:, m * 128:(m + 1) * 128], idn[0:TT, 0:TT])
                            last.then_inc(ctxT_ready, 1)

                    order = []

                    def wait_bank(use):
                        order.append(use)
                        same = [o for o in order[:-1] if o % 2 == use % 2]
                        if same:
                            g, k = divmod(same[-1], 5)
                            if k < 3:
                                pe.wait_ge(at_out, 3 * (NT * L + g) + k + 1)
                            else:
                                pe.wait_ge(ctxT_out, 2 * (NT * L + g) + k - 2)

                    def project(g):
                        if g == 0:
                            pe.wait_ge(w_in["wo"], 16 * (L + 1))
                        pe.wait_ge(ctxT_out, 2 * (NT * L + g + 1))
                        pe.wait_ge(ctx_out, NT * L + min(g + 2, NT))
                        if g >= 1:
                            pe.wait_ge(o_out, NT * L + g)
                        for m in range(6):
                            last = T.matmul(ps[0:TT, 7, 0:D], ctxT[:, m, :], wo_sb[:, m, :],
                                            start=(m == 0), stop=(m == 5))
                        last.then_inc(o_ready, 1)

                    scores2(0)
                    scores2(1)
                    pe.wait_ge(v_outA, 3 * (L + 1))
                    pe.wait_ge(v_outD, 2 * (L + 1))
                    for g in range(NT):
                        pe.wait_ge(e_ready, NT * L + g + 1)
                        for r in range(3):
                            use = 5 * g + r
                            wait_bank(use)
                            for q in range(4):
                                last = T.transpose(ps[0:TT, 4 + (25 * odd + use) % 2, q * TT:(q + 1) * TT],
                                                   prob[g % 2][:, 4 * r + q, :], idn[0:TT, 0:TT])
                            last.then_inc(at_ready, 1)
                        if g >= 1:
                            ctx_transposes(g - 1)
                        pe.wait_ge(at_out, 3 * (NT * L + g + 1))
                        if g >= 2:
                            pe.wait_ge(o_out, NT * L + g - 1)
                        for h in range(H):
                            last = T.matmul(ps[0:TT, 6 + h // 8, (h % 8) * DK:(h % 8 + 1) * DK], probT[:, pos(h), :],
                                            v_sb[:, g, h * DK:(h + 1) * DK], start=True, stop=True)
                        last.then_inc(ctx_ready, 1)
                        if g + 2 < NT:
                            scores2(g + 2)
                        if g >= 1:
                            project(g - 1)
                    ctx_transposes(NT - 1)
                    project(NT - 1)
                    norm_transposes(2 + 2 * L)
                    normed(2 + 2 * L)
                    if odd:
                        pe.wait_ge(gw_in, 16 * (lp + 1))
                        for g in range(NT):
                            for k in range(2):
                                last = T.matmul(ps[0:TT, 7, g * E0:(g + 1) * E0], xT[:, k, tile(g)],
                                                gw_sb[:, k, :], start=(k == 0), stop=(k == 1))
                        last.then_inc(lg_ready, 1)
                    pe.wait_ge(w_in["f1"], 16 * (L + 1))
                    up(10 * lp + odd, odd, fw1_sb)
                    pe.wait_ge(w_in["f2"], 16 * (L + 1))
                    if odd:
                        pe.wait_ge(lg_out, lp + 1)
                    down(10 * lp + odd, odd, fw2_sb, first=True)
                with pe.Fori(0, E0 // 2) as ep:
                    for u in range(2):
                        pe.wait_ge(e1_in[u], 64 * lp + 16 * (ep + 1))
                        up(10 * lp + 2 + 2 * ep + u, u, ew1_sb[u])
                        pe.wait_ge(e2_in[u], 64 * lp + 16 * (ep + 1))
                        down(10 * lp + 2 + 2 * ep + u, u, ew2_sb[u])
            norm_transposes(1 + 2 * LAYERS)
            normed(1 + 2 * LAYERS)
            for c in range(2):
                for k in range(2):
                    last = T.matmul(ps[0:NSTATE, c, 0:CH], bt_sb[:, k, :], xT[:, k, c * CH:(c + 1) * CH],
                                    start=(k == 0), stop=(k == 1))
            last.then_inc(ss_bu, 1)
            pe.wait_ge(ss_h, 1)
            for g in range(NT):
                if g == NT - 1:
                    pe.wait_ge(ss_yout, 1)
                T.matmul(slot(g, rows(g)), hst[:, 0, tile(g, rows(g))], ct_sb[:, :], start=True, stop=True).then_inc(ss_y, 1)
            norm_transposes(2 + 2 * LAYERS)
            normed(2 + 2 * LAYERS)
            for g in range(NT):
                for k in range(2):
                    last = T.matmul(ps[0:TT, 0, g * E1:(g + 1) * E1], xT[:, k, tile(g)], wr_sb[:, k, :],
                                    start=(k == 0), stop=(k == 1))
            last.then_inc(lg_ready, 1)
            pe.wait_ge(cw_ready, LAYERS // 2 + 1)
            for g in range(NT):
                T.transpose(ps[0:E1, 2 + g // 4, (g % 4) * TT:(g % 4 + 1) * TT], cw[:, g, :],
                            idn[0:TT, 0:TT]).then_inc(cwT_ready, 1)
            pe.wait_ge(cwT_out, 2)
            for g in range(NT):
                if g == NT - 1:
                    pe.wait_ge(b2_out, 1)
                T.matmul(slot(g, rows(g)), cwT[:, tile(g, rows(g))], b2_sb[:, :], start=True, stop=True).then_inc(b2_ready, 1)
            pe.wait_ge(b2_out, NT)
            with pe.Fori(0, E1 // 2) as ep:
                for u in range(2):
                    pe.wait_ge(e1_in[u], 16 * E0 + 16 * (ep + 1))
                    up(20 + 2 * ep + u, u, ew1_sb[u])
                    pe.wait_ge(e2_in[u], 16 * E0 + 16 * (ep + 1))
                    down(20 + 2 * ep + u, u, ew2_sb[u])


def tables():
    n = np.arange(16, dtype=np.float32)
    dct = (2.0 * np.cos(np.float32(np.pi) * (2.0 * n[None, :] + 1.0) * n[:, None] / np.float32(32.0))).astype(np.float32)
    k2 = np.kron(dct, dct).astype(np.float32)
    tok = np.arange(TT)
    img, s = tok // SEQ, tok % SEQ
    same = img[:, None] == img[None, :]
    causal = np.where(same & (s[None, :] <= s[:, None]), 0.0, NEG).astype(np.float32)
    block = np.where(same, 0.0, NEG).astype(np.float32)
    nreg = (1.0 / (s + 1).astype(np.float32)).astype(np.float32)
    nreg = np.stack([nreg, -nreg], 1)
    clsmask = (s == 0).astype(np.float32)[:, None]
    rel = np.arange(SEQ)[None, :] - s[:, None]
    dist = np.abs(rel)
    large = 8 + (np.log(np.maximum(dist, 1).astype(np.float32) / np.float32(8)) / np.float32(np.log(128 / 8))
                 * np.float32(8)).astype(np.int32)
    bucket = (rel > 0) * 16 + np.where(dist < 8, dist, np.minimum(large, 15))
    onehot = (bucket.T[None, :, :] == np.arange(32)[:, None, None]).astype(np.float32)
    iota = np.tile(np.arange(E1, dtype=np.float32), (TT, 1))
    return dict(k2=k2.reshape(2, 128, 256).transpose(1, 0, 2), causal=causal, nreg=nreg, clsmask=clsmask,
                onehot=onehot, block_mask=block, ident=np.eye(128, dtype=np.float32), iota=iota)


def kernel(x, cls_tok, L0_tok_W, L0_attn_e, L0_attn_p, L0_attn_ln_w, L0_attn_W_qk, L0_attn_W_o, L0_attn_wte,
           L0_ffn_attn_q, L0_ffn_attn_k, L0_ffn_attn_v, L0_ffn_attn_o, L0_ffn_ffn_wi, L0_ffn_ffn_wo, L0_ffn_ln1,
           L0_ffn_ln2, L0_ffn_ln_f, L0_ffn_rel_emb, L0_ffn_gate_w, L0_ffn_moe_w1, L0_ffn_moe_w2, L1_attn_A_real,
           L1_attn_A_imag, L1_attn_B, L1_attn_C, L1_ffn_wr, L1_ffn_w1, L1_ffn_b1, L1_ffn_w2, L1_ffn_b2):
    import numpy as _np
    import concourse.bacc as _bacc
    from concourse import mybir as _mybir
    from concourse.bass_utils import run_bass_kernel_spmd as _run

    a = _np.asarray

    def halves(w):
        w = a(w)
        w = w.reshape(w.shape[:-2] + (2, KD, w.shape[-1]))
        return w.swapaxes(-3, -2)

    def sixths(w):
        w = a(w)
        w = w.reshape(w.shape[:-2] + (6, 128, w.shape[-1]))
        return w.swapaxes(-3, -2)

    ins = dict(tables())
    xb = a(x).reshape(BATCH, 3, 4, 16, 4, 16).transpose(1, 3, 5, 0, 2, 4).reshape(6, 128, BATCH * 16)
    ins["xst"] = xb.transpose(1, 0, 2).reshape(128, 6 * BATCH * 16)
    ins["w_tok"] = sixths(a(L0_tok_W).T)
    ins["cls"] = a(cls_tok).reshape(1, D)
    wte = a(L0_attn_wte)
    ins["wte_main"] = wte[:WCH * WROWS * 128].reshape(WCH, 128, WROWS, D)
    ins["wte_tail"] = wte[WCH * WROWS * 128:]
    ins["ln_w"] = halves(a(L0_attn_ln_w)[:, None])
    ins["wqk"] = halves(a(L0_attn_W_qk).T)
    ins["wot"] = a(L0_attn_W_o).reshape(D, H, 2, KD).transpose(3, 2, 1, 0)
    ins["wq"], ins["wk"], ins["wv"] = halves(L0_ffn_attn_q), halves(L0_ffn_attn_k), halves(L0_ffn_attn_v)
    ins["wo"] = sixths(L0_ffn_attn_o)
    ins["fw1"], ins["fw2"] = halves(L0_ffn_ffn_wi), sixths(L0_ffn_ffn_wo)
    ins["ln1"], ins["ln2"] = halves(a(L0_ffn_ln1).T), halves(a(L0_ffn_ln2).T)
    ins["ln_f"] = a(L0_ffn_ln_f).reshape(1, D)
    ins["rel_emb"] = a(L0_ffn_rel_emb)
    ins["gate_w"] = halves(L0_ffn_gate_w)
    m1 = halves(L0_ffn_moe_w1).reshape(2 * E0, KD, 2, FF)
    m2 = sixths(L0_ffn_moe_w2).reshape(2 * E0, 128, FT, D)
    ins["ew1"] = _np.concatenate([m1, halves(a(L1_ffn_w1).transpose(0, 2, 1))])
    ins["ew2"] = _np.concatenate([m2, sixths(a(L1_ffn_w2).transpose(0, 2, 1))])
    ins["eb1"] = a(L1_ffn_b1).reshape(E1, FT, 128).transpose(0, 2, 1)
    ins["a_real"], ins["a_imag"] = a(L1_attn_A_real)[:, None], a(L1_attn_A_imag)[:, None]
    ins["bt"] = halves(a(L1_attn_B).T)
    ins["ct"] = a(L1_attn_C).T
    ins["wr"] = halves(a(L1_ffn_wr).T)
    ins["b2"] = a(L1_ffn_b2)

    nc = _bacc.Bacc("TRN2", target_bir_lowering=False, num_devices=1)
    arrays, args = {}, {}
    for name, v in ins.items():
        v = _np.ascontiguousarray(v)
        arrays[f"in_{name}"] = v
        args[name] = nc.dram_tensor(f"in_{name}", v.shape, _mybir.dt.from_np(v.dtype), kind="ExternalInput").ap()
    out = nc.dram_tensor("out", [TOK, D], _mybir.dt.float32, kind="ExternalOutput").ap()
    build(nc, out=out, **args)
    r = _run(nc, [arrays], core_ids=[0])
    return r.results[0]["out"].reshape(BATCH, SEQ, D)
```

```python
from contextlib import ExitStack

import numpy as np

import concourse.bass as bass
from concourse import mybir

F32 = mybir.dt.float32
U32 = mybir.dt.uint32
ALU = mybir.AluOpType
ACT = mybir.ActivationFunctionType
AX = mybir.AxisListType

BATCH, SEQ, D = 32, 17, 192
TOK = BATCH * SEQ
IMGS = 7
TT = IMGS * SEQ
NT = 5
TPAD = NT * TT
LAST = TOK - (NT - 1) * TT
KD = D // 2
CH = TOK // 2
H = 12
DK = 64
HD = H * DK
FF = 768
FT = FF // 128
E0, E1 = 8, 16
LAYERS = 4
NPIX = 768
VOCAB = 50257
WROWS = 14
WCH = VOCAB // 128 // WROWS
WTAIL = VOCAB - WCH * WROWS * 128
WBUF = 4
W_PE = range(5, 8)
W_DVE = [j for j in range(WCH) if j not in W_PE]
NEG = -1.0e30
DT = 0.01
NSTATE = 64
CAP = 112
MAXR = -(-TOK // CAP)


def rows(g):
    return TT if g < NT - 1 else LAST


class Chain:

    def __init__(self, eng, sem):
        self.eng, self.sem, self.base, self.n = eng, sem, 0, 0

    def link(self, ins):
        self.n += 1
        ins.then_inc(self.sem, 1)
        self.eng.wait_ge(self.sem, self.base + self.n)


def build(nc, xst, w_tok, k2, cls, wte_main, wte_tail, ln_w, wqk, wot, causal, nreg, clsmask,
          wq, wk, wv, wo, fw1, fw2, ln1, ln2, ln_f, onehot, rel_emb, block_mask, gate_w,
          ew1, ew2, eb1, a_real, a_imag, bt, ct, wr, b2, ident, iota, tri, slots, valid, out):
    ctx = ExitStack()
    with ctx:
        def sb(name, shape, dt=F32):
            return ctx.enter_context(nc.sbuf_tensor(name, shape, dt))

        def sem(name):
            return ctx.enter_context(nc.semaphore(name))

        ps = ctx.enter_context(nc.psum_tensor("ps", [128, 8, 512], F32))

        res = sb("res", [TT, NT, D])
        hid = sb("hid", [TT, NT, D])
        xs = sb("xs", [TT, NT, D])
        xT = sb("xT", [KD, 2, TPAD])
        idn = sb("idn", [128, 128])
        mask_sb = sb("mask_sb", [TT, TT])
        biasM = sb("biasM", [TT, 12, TT])
        lnw_sb = sb("lnw_sb", [KD, 2, 1])
        ln1_sb = sb("ln1_sb", [KD, 2, LAYERS])
        ln2_sb = sb("ln2_sb", [KD, 2, LAYERS])
        lnc = [sb(f"lnc{i}", [KD, 2, 1]) for i in range(4)]
        idle = sb("idle", [TT, 1])
        stats = sb("stats", [TT, NT, 6])
        mv = sb("mv", [TT, NT, 2])
        rstd = sb("rstd", [TT, NT])
        mhalf = sb("mhalf", [TT, NT])
        prob = [sb(f"prob{i}", [TT, 12, TT]) for i in range(2)]
        probT = sb("probT", [TT, 12, TT])
        mx = [sb(f"mx{i}", [TT, H]) for i in range(2)]
        nmx = [sb(f"nmx{i}", [TT, H]) for i in range(2)]
        rsum = [sb(f"rsum{i}", [TT, H]) for i in range(2)]
        rinv = sb("rinv", [TT, H])
        ctxT = sb("ctxT", [128, 6, TT])
        wreg = sb("wreg", [128, 4 * 2 * HD + 2 * FT * D])

        def w_part(i, *shape):
            n = shape[1] * shape[2]
            return wreg[0:shape[0], i:i + n].rearrange("p (a b) -> p a b", a=shape[1]), i + n

        wq_sb, at = w_part(0, KD, 2, HD)
        wk_sb, at = w_part(at, KD, 2, HD)
        wv_sb, at = w_part(at, KD, 2, HD)
        wo_sb, at = w_part(at, 128, 6, D)
        fw1_sb, at = w_part(at, KD, 2, FF)
        fw2_sb, at = w_part(at, 128, FT, D)
        part, at = w_part(0, 128, len(W_DVE) + 1, D)
        wtok_sb, at = w_part(at, 128, 6, D)
        wfold, at = w_part(at, 128, 6, D)
        k2_sb, at = w_part(at, 128, 2, 256)
        big = sb("big", [128, 3, 6 * TPAD])
        qT = big[:, 0, :].rearrange("p (m t) -> p m t", m=6)
        kT = [big[:, 1 + i, :].rearrange("p (m t) -> p m t", m=6) for i in range(2)]
        xp = qT
        xstage = big[:, 1, 0:6 * BATCH * 16].rearrange("p (m b t) -> p m b t", m=6, b=BATCH)
        big2 = sb("big2", [128, WBUF * WROWS * D])
        hidden = [big2[:, i * FT * TOK:(i + 1) * FT * TOK].rearrange("p (f t) -> p f t", f=FT)
                  for i in range(2)]
        wte_sb = big2[:, :].rearrange("p (s r d) -> p s r d", s=WBUF, r=WROWS)
        vbuf = sb("vbuf", [128, NT * HD])
        v_sb = vbuf[0:TT, :].rearrange("p (g n) -> p g n", g=NT)
        ering = sb("ering", [128, 2 * (2 * FF + FT * D)])
        esz = 2 * FF + FT * D
        ew1_sb = [ering[0:KD, i * esz:i * esz + 2 * FF].rearrange("p (k f) -> p k f", k=2) for i in range(2)]
        ew2_sb = [ering[:, i * esz + 2 * FF:(i + 1) * esz].rearrange("p (f d) -> p f d", f=FT)
                  for i in range(2)]
        wot_sb = ering[0:KD, 0:2 * H * D].rearrange("p (k h d) -> p k h d", k=2, h=H)
        po_sb = vbuf[0:TT, 0:H * D].rearrange("p (h d) -> p h d", h=H)
        eb1_sb = [sb(f"eb1_sb{i}", [128, FT]) for i in range(2)]
        cls_sb = sb("cls_sb", [TT, D])
        lnf_sb = sb("lnf_sb", [TT, D])
        wqk_sb = sb("wqk_sb", [KD, 2, H])
        qs = [prob_q.rearrange("p (k h t) -> p k h t", k=2, h=H) for prob_q in
              (big[0:KD, 1, 0:2 * H * TT], big[0:KD, 2, 0:2 * H * TT])]
        psum_all = sb("psum_all", [128, D])
        onesv = sb("onesv", [128, TT])
        pe_sum = sb("pe_sum", [1, 2 * D])
        ones = sb("ones", [128, 128])
        avgB = sb("avgB", [KD, 2, TT])
        nreg_sb = sb("nreg_sb", [TT, 2])
        cmask_sb = sb("cmask_sb", [TT, 1])
        oh_sb = big[0:32, 2, 0:SEQ * TT].rearrange("p (s t) -> p s t", s=SEQ)
        rel_sb = sb("rel_sb", [32, H])
        R_sb = sb("R_sb", [TT, SEQ, H])
        bmask_sb = sb("bmask_sb", [TT, TT])
        gw_sb = sb("gw_sb", [KD, 2, E0])
        wr_sb = sb("wr_sb", [KD, 2, E1])
        b2_sb = sb("b2_sb", [E1, D])
        iota_sb = sb("iota_sb", [TT, E1])
        logit = sb("logit", [TT, NT, E1])
        top = sb("top", [TT, NT, 8])
        idx = sb("idx", [TT, NT, 8], U32)
        idf = sb("idf", [TT, NT, 2])
        gsm = sb("gsm", [TT, 6, NT])
        cw = sb("cw", [TT, NT, E1])
        cwb = sb("cwb", [TT, E1])
        tri_sb = mask_sb
        slots_sb = bmask_sb[:, 0:CAP]
        valid_sb = sb("valid_sb", [TT, NT])
        asg = logit
        place = sb("place", [TT, NT, E1])
        most = sb("most", [TT, 2])
        rounds_sb = sb("rounds_sb", [1, 1], mybir.dt.int32)
        flat = [prob[i][:, :, :].rearrange("p h t -> p (h t)") for i in range(2)]
        pick = [f[:, 0:NT * CAP].rearrange("p (g c) -> p g c", g=NT) for f in flat]
        put = [f[:, NT * CAP:2 * NT * CAP].rearrange("p (g c) -> p g c", g=NT) for f in flat]
        xg = [probT[0:KD, :, :].rearrange("p h t -> p (h t)")[:, 2 * CAP * i:2 * CAP * (i + 1)].rearrange(
            "p (k c) -> p k c", k=2) for i in range(2)]
        putT = [biasM[0:CAP, :, :].rearrange("p h t -> p (h t)")[:, TPAD * i:TPAD * (i + 1)] for i in range(2)]
        yg = [wreg[0:CAP, D * i:D * (i + 1)] for i in range(2)]
        cwT = ctxT[0:E1, :, :].rearrange("p m t -> p (m t)")[:, 0:TPAD]
        lam = sb("lam", [NSTATE, 16])
        bt_sb = sb("bt_sb", [KD, 2, NSTATE])
        ct_sb = sb("ct_sb", [NSTATE, D])
        hst = big[0:NSTATE, 0, 0:2 * TOK].rearrange("p (c t) -> p c t", c=2)

        s_in = sem("inputs_tok")
        s_const = sem("inputs_const")
        s_cn2 = sem("inputs_const2")
        s_wte = [sem(f"wte_in{i}") for i in range(WBUF)]
        s_wtail = sem("wte_tail_in")
        s_wot = sem("wot_in")
        wte_used = sem("wte_summed_dve")
        wte_used_pe = sem("wte_summed_pe")
        pe_sum_out = sem("pe_sum_out")
        zeroed = sem("zeroed")
        xp_ready = sem("xp_ready")
        fold_ready = sem("fold_ready")
        fold_out = sem("fold_out")
        tok_ready = sem("tok_ready")
        tok_out = sem("tok_out")
        n_stats = sem("norm_stats")
        n_rstd = sem("norm_rstd")
        t_stats = sem("tile_norm_stats")
        t_rstd = sem("tile_norm_rstd")
        n_scaled = sem("norm_scaled")
        n_T = sem("norm_transposed")
        n_outA = sem("norm_out_act")
        n_outD = sem("norm_out_dve")
        qs_ready = sem("qs_ready")
        a_s = sem("a_scores")
        a_masked = sem("a_masked")
        a_exp = sem("a_exp")
        a_norm = sem("a_normed")
        a_T = sem("a_probT")
        a_Tout = sem("a_probT_out")
        a_p = sem("a_p")
        a_pout = sem("a_p_out")
        a_y = sem("a_y")
        a_yout = sem("a_y_out")
        r_ready = sem("rel_ready")
        r_out = sem("rel_out")
        biasm_ready = sem("biasm_ready")
        avg_sum = sem("avg_sum")
        avg_T = sem("avg_T")
        avg_out = sem("avg_out")
        rbc_ready = sem("rbc_ready")
        zero_kv = sem("zero_kv")
        w_in = {n: sem(f"{n}_in") for n in ("wq", "wk", "wv", "wo", "f1", "f2")}
        e1_in = [sem(f"ew1_in{i}") for i in range(2)]
        e2_in = [sem(f"ew2_in{i}") for i in range(2)]
        eb_in = [sem(f"eb1_in{i}") for i in range(2)]
        gw_in = sem("gate_w_in")
        qk_ready = sem("qk_ready")
        q_out = sem("q_out")
        k_out = sem("k_out")
        v_ready = sem("v_ready")
        v_outA = sem("v_out_act")
        v_outD = sem("v_out_dve")
        s_ready = sem("s_ready")
        s_masked = sem("s_masked")
        s_max = sem("s_max")
        e_ready = sem("e_ready")
        p_ready = sem("p_ready")
        at_ready = sem("at_ready")
        at_out = sem("at_out")
        ctx_ready = sem("ctx_ready")
        ctx_out = sem("ctx_out")
        o_ready = sem("o_ready")
        o_out = sem("o_out")
        up_ready = [sem(f"up_ready{i}") for i in range(2)]
        hid_out = sem("hid_out")
        down_ready = [sem(f"down_ready{i}") for i in range(2)]
        y_out = sem("y_out")
        lg_ready = sem("logits_ready")
        lg_out = sem("logits_out")
        g_mx = sem("gate_max")
        g_exp = sem("gate_exp")
        cw_ready = sem("cw_ready")
        cwT_ready = sem("cwT_ready")
        cwT_out = sem("cwT_out")
        b2_ready = sem("b2_ready")
        asg_ready = sem("asg_ready")
        pos_ready = sem("pos_ready")
        rounds_ready = sem("rounds_ready")
        route_in = sem("route_tables_in")
        x_pick = sem("x_pick")
        place_next = sem("place_next")
        x_gather = sem("x_gather")
        x_T = sem("x_put_transposed")
        x_gout = sem("x_gather_out")
        x_Tout = sem("x_put_out")
        x_up = sem("x_up")
        x_hout = sem("x_hidden_out")
        x_down = sem("x_down")
        x_ygout = sem("x_down_out")
        x_back = sem("x_put_back")
        x_yout = sem("x_added")
        ss_bu = sem("ss_bu")
        ss_h = sem("ss_h")
        ss_y = sem("ss_y")
        ss_yout = sem("ss_yout")
        d_chain = sem("dve_chain")
        p_chain = sem("pool_chain")
        fin = sem("fin")
        s_out = sem("out_stored")

        N_CONST = 15
        SCALE = 1.0 / float(np.sqrt(np.float32(D)))
        NORM_L = 3
        NORM_F = NORM_L + LAYERS // 2

        def pos(h):
            return 6 * (h % 2) + h // 2

        block = ctx.enter_context(nc.Block())

        @block.sync
        def _(sp):
            sp.dma_start(wtok_sb[:, :, :], w_tok).then_inc(s_in, 16)
            sp.dma_start(k2_sb[:, :, :], k2).then_inc(s_in, 16)
            sp.dma_start(xstage.rearrange("p m b t -> p (m b t)"), xst).then_inc(s_in, 16)
            small = [(idn[:, :], ident), (cls_sb[:, :], cls.to_broadcast([TT, D])),
                     (cmask_sb[:, :], clsmask), (lnw_sb[:, :, :], ln_w), (wqk_sb[:, :, :], wqk),
                     (mask_sb[:, :], causal), (nreg_sb[:, :], nreg), (bmask_sb[:, :], block_mask),
                     (oh_sb[:, :, :], onehot), (rel_sb[:, :], rel_emb), (ln1_sb[:, :, :], ln1),
                     (ln2_sb[:, :, :], ln2), (lam[:, 0:1], a_real), (lam[:, 1:2], a_imag),
                     (iota_sb[:, :], iota)]
            assert len(small) == N_CONST
            for dst, src in small:
                sp.dma_start(dst, src).then_inc(s_const, 16)
            for j in range(WCH):
                if j == 2:
                    sp.dma_start(wot_sb, wot).then_inc(s_wot, 16)
                if j >= WBUF:
                    if j - WBUF in W_PE:
                        sp.wait_ge(wte_used_pe, W_PE.index(j - WBUF) + 1)
                    else:
                        sp.wait_ge(wte_used, W_DVE.index(j - WBUF) + 1)
                sp.dma_start(wte_sb[:, j % WBUF, :, :], wte_main[j]).then_inc(s_wte[j % WBUF], 16)
                if j == 6:
                    for dst, src in ((lnf_sb[:, :], ln_f.to_broadcast([TT, D])),
                                     (wr_sb[:, :, :], wr), (b2_sb[:, :], b2), (bt_sb[:, :, :], bt),
                                     (ct_sb[:, :], ct)):
                        sp.dma_start(dst, src).then_inc(s_cn2, 16)
            sp.wait_ge(zeroed, 2)
            sp.dma_start(part[0:WTAIL, len(W_DVE), :], wte_tail).then_inc(s_wtail, 16)
            sp.wait_ge(rbc_ready, 1)
            sp.wait_ge(biasm_ready, H)
            for dst, src in ((tri_sb[:, :], tri), (slots_sb, slots), (valid_sb[:, :], valid)):
                sp.dma_start(dst, src).then_inc(route_in, 16)
            for L in range(LAYERS):
                lp, odd = divmod(L, 2)

                def load(dst, src, arrived, used, count):
                    if L:
                        sp.wait_ge(used, count)
                    sp.dma_start(dst, src[L]).then_inc(arrived, 16)

                load(wq_sb[:, :, :], wq, w_in["wq"], qk_ready, 12 * L)
                load(wk_sb[:, :, :], wk, w_in["wk"], qk_ready, 12 * L)
                load(wv_sb[:, :, :], wv, w_in["wv"], v_ready, NT * L)
                load(wo_sb[:, :, :], wo, w_in["wo"], o_ready, NT * L)
                u, passes = (0, 5 * lp + 1) if odd else (1, 5 * (lp - 1) + 1)
                load(fw1_sb[:, :, :], fw1, w_in["f1"], up_ready[u], FT * passes)
                load(fw2_sb[:, :, :], fw2, w_in["f2"], down_ready[u], NT * passes)
                if odd:
                    if lp:
                        sp.wait_ge(lg_ready, lp)
                    sp.dma_start(gw_sb[:, :, :], gate_w[lp]).then_inc(gw_in, 16)
                    with sp.Fori(0, E0 // 2) as ep:
                        for u in range(2):
                            e = E0 * lp + 2 * ep + u
                            sp.wait_ge(up_ready[u], FT * (5 * lp + 1 + ep))
                            sp.dma_start(ew1_sb[u], ew1[bass.ds(e, 1)].rearrange("a p k f -> (a p) k f")).then_inc(e1_in[u], 16)
                            sp.wait_ge(down_ready[u], NT * (5 * lp + 1 + ep))
                            sp.dma_start(ew2_sb[u], ew2[bass.ds(e, 1)].rearrange("a p k f -> (a p) k f")).then_inc(e2_in[u], 16)
            def load_expert(e, u):
                sp.dma_start(ew1_sb[u], ew1[bass.ds(2 * E0 + e, 1)].rearrange("a p k f -> (a p) k f")).then_inc(e1_in[u], 16)

            def load_expert2(e, u):
                sp.dma_start(eb1_sb[u][:, :], eb1[bass.ds(e, 1)].rearrange("a p f -> (a p) f")).then_inc(eb_in[u], 16)
                sp.dma_start(ew2_sb[u], ew2[bass.ds(2 * E0 + e, 1)].rearrange("a p k f -> (a p) k f")).then_inc(e2_in[u], 16)

            for u in range(2):
                sp.wait_ge(up_ready[u], FT * 5 * LAYERS // 2)
                load_expert(u, u)
                sp.wait_ge(down_ready[u], NT * 5 * LAYERS // 2)
                load_expert2(u, u)
            sp.wait_ge(rounds_ready, 1)
            rounds = sp.value_load(rounds_sb[0:1, 0:1], min_val=1, max_val=MAXR)

            def load_next(i, e, u):
                sp.wait_ge(x_up, 2 * FT * i + FT * (u + 1))
                load_expert(e, u)
                sp.wait_ge(x_down, 2 * i + u + 1)
                load_expert2(e, u)

            with sp.Fori(0, rounds) as rd:
                with sp.Fori(0, E1 // 2 - 1) as ep:
                    for u in range(2):
                        load_next(8 * rd + ep, 2 * ep + 2 + u, u)
                for u in range(2):
                    load_next(8 * rd + 7, u, u)
            sp.wait_ge(fin, 1)
            last_loads = [(arrived[u], before + 16) for u in range(2)
                          for arrived, before in ((e1_in, 16 * E0), (e2_in, 16 * E0), (eb_in, 0))]
            parts = [(g, 0, rows(g)) for g in range(NT - 1)]
            parts += [(NT - 1, 0, rows(NT - 1) // 2), (NT - 1, rows(NT - 1) // 2, rows(NT - 1))]
            for (arrived, before), (g, lo, hi) in zip(last_loads, parts, strict=True):
                sp.wait_ge(arrived, before + 128 * rounds)
                sp.dma_start(out[g * TT + lo:g * TT + hi, :], res[lo:hi, g, :]).then_inc(s_out, 16)
            sp.wait_ge(s_out, 16 * len(parts))

        @block.gpsimd
        def _(pool):
            link = Chain(pool, p_chain)

            def norm_rstd(n):
                pool.wait_ge(n_stats, n + 1)
                nc.gpsimd.tensor_tensor(rstd[:, :], rstd[:, :], mhalf[:, :], ALU.pow).then_inc(n_rstd, 1)

            nc.gpsimd.memset(xp[:, :, :], 0.0).then_inc(zeroed, 1)
            nc.gpsimd.memset(part[:, len(W_DVE), :], 0.0).then_inc(zeroed, 1)
            nc.gpsimd.memset(mhalf[:, :], -0.5).then_inc(zeroed, 1)
            nc.gpsimd.memset(onesv[:, :], 1.0 / VOCAB).then_inc(zeroed, 1)
            nc.gpsimd.memset(ones[:, :], 1.0).then_inc(zeroed, 1)
            pool.wait_ge(s_in, 48)
            pool.wait_ge(zeroed, 5)
            for m in range(6):
                nc.gpsimd.tensor_copy(
                    xp[:, m, 0:TOK].rearrange("p (b s) -> p b s", s=SEQ)[:, :, 1:SEQ],
                    xstage[:, m, :, :]).then_inc(xp_ready, 1)
            norm_rstd(0)
            norm_rstd(1)
            pool.wait_ge(s_const, 16 * N_CONST)
            pool.wait_ge(xp_ready, 6)
            for g in range(NT):
                if g == 0:
                    pool.wait_ge(n_outA, NT)
                    pool.wait_ge(n_outD, NT)
                if g == 1:
                    pool.wait_ge(r_ready, 1)
                if g >= 2:
                    pool.wait_ge(a_s, g - 1)
                for k in range(2):
                    nc.gpsimd.tensor_tensor(
                        qs[g % 2][:, k, :, :],
                        xT[:, k, g * TT:(g + 1) * TT].unsqueeze(1).to_broadcast([KD, H, TT]),
                        wqk_sb[:, k, :].unsqueeze(2).to_broadcast([KD, H, TT]), ALU.mult).then_inc(qs_ready, 1)
            pool.wait_ge(r_out, 1)
            for h in range(H):
                last = nc.gpsimd.tensor_tensor(
                    biasM[:, pos(h), :].rearrange("p (b t) -> p b t", b=IMGS),
                    bmask_sb[:, :].rearrange("p (b t) -> p b t", b=IMGS),
                    R_sb[:, :, h].unsqueeze(1).to_broadcast([TT, IMGS, SEQ]), ALU.add)
                last.then_inc(biasm_ready, 1)
            pool.wait_ge(biasm_ready, H)
            pool.wait_ge(a_s, NT)
            for n, room in enumerate((kT[0][64:128, :, :], kT[1][0:64, :, :], qT[:, :, TOK:TPAD],
                                      kT[0][0:64, :, TOK:TPAD], kT[1][64:128, :, TOK:TPAD])):
                nc.gpsimd.memset(room, 0.0).then_inc(zero_kv, 1)
                pool.wait_ge(zero_kv, n + 1)
            norm_rstd(2)
            with pool.Fori(0, LAYERS // 2) as lp:
                norm_rstd(NORM_L + lp)
                for q in range(3):
                    for g in range(NT):
                        pool.wait_ge(t_stats, NT * (3 * lp + q) + g + 1)
                        nc.gpsimd.tensor_tensor(rstd[:, g:g + 1], rstd[:, g:g + 1], mhalf[:, g:g + 1],
                                                ALU.pow).then_inc(t_rstd, 1)
            for n in range(NORM_F, NORM_F + 3):
                norm_rstd(n)

        @block.scalar
        def _(act):
            def norm_out(v, col=None):
                for g in range(NT):
                    act.wait_ge(n_T, NT * v + g + 1)
                    src = ps[0:KD, g % 2, 0:TT]
                    dst = xT[:, 0, g * TT:(g + 1) * TT]
                    if col is None:
                        nc.scalar.activation(dst, src, ACT.Copy).then_inc(n_outA, 1)
                    else:
                        nc.scalar.activation(dst, src, ACT.Copy, scale=col[:, 0, :]).then_inc(n_outA, 1)

            def exps(i, scale):
                for h in range(H):
                    last = nc.scalar.activation(prob[i][:, pos(h), :], prob[i][:, pos(h), :], ACT.Exp,
                                                bias=nmx[i][:, h:h + 1], scale=scale,
                                                accum_out=rsum[i][:, h:h + 1])
                return last

            for f in range(6):
                act.wait_ge(fold_ready, f + 1)
                nc.scalar.activation(wfold[:, f, :], ps[:, f % 4, 0:D],
                                     ACT.Copy).then_inc(fold_out, 1)
            act.wait_ge(wte_used_pe, len(W_PE))
            nc.scalar.activation(pe_sum[:, :], ps[0:1, 0, 0:2 * D], ACT.Copy).then_inc(pe_sum_out, 1)
            act.wait_ge(s_const, 16 * N_CONST)
            norm_out(0, lnw_sb)
            def project0_out(g):
                for b in range(6):
                    act.wait_ge(a_p, 6 * g + b + 1)
                    nc.scalar.activation(po_sb[:, 2 * b:2 * b + 2, :].rearrange("p h d -> p (h d)"),
                                         ps[0:TT, 6 + b % 2, 0:2 * D], ACT.Copy).then_inc(a_pout, 1)

            project0_out(0)
            act.wait_ge(a_masked, 1)
            exps(0, SCALE).then_inc(a_exp, 1)
            for g in range(NT):
                for r in range(3):
                    act.wait_ge(a_T, 3 * g + r + 1)
                    nc.scalar.activation(probT[:, 4 * r:4 * r + 4, :].rearrange("p h t -> p (h t)"),
                                         ps[0:TT, 4 + r % 2, 0:4 * TT], ACT.Copy).then_inc(a_Tout, 1)
                if g + 1 < NT:
                    act.wait_ge(a_masked, g + 2)
                    exps((g + 1) % 2, SCALE).then_inc(a_exp, 1)
                    project0_out(g + 1)
            act.wait_ge(avg_T, 1)
            nc.scalar.activation(avgB[:, :, :], ps[0:KD, 4, 0:2 * TT].rearrange("p (k t) -> p k t", k=2),
                                 ACT.Copy).then_inc(avg_out, 1)

            def hidden_out(j, u, func, bias=None):
                for f in range(FT):
                    act.wait_ge(up_ready[u], FT * j + f + 1)
                    b = 0.0 if bias is None else bias[:, f:f + 1]
                    nc.scalar.activation(hidden[u][:, f, :].rearrange("p (c n) -> p c n", c=2),
                                         ps[:, 2 * (f % 2):2 * (f % 2) + 2, 0:CH], func, bias=b).then_inc(hid_out, 1)

            act.wait_ge(zero_kv, 5)
            with act.Fori(0, LAYERS // 2) as lp:
                for odd in range(2):
                    L = 2 * lp + odd
                    norm_out(1 + 2 * L, lnc[2 * odd])
                    for m in range(6):
                        act.wait_ge(qk_ready, 12 * L + 2 * m + 1)
                        nc.scalar.activation(qT[:, m, 0:TOK].rearrange("p (c n) -> p c n", c=2),
                                             ps[:, 0:2, 0:CH], ACT.Copy).then_inc(q_out, 1)
                    for g in range(0, NT, 2):
                        act.wait_ge(v_ready, NT * L + g + 1)
                        nc.scalar.activation(v_sb[:, g, :].rearrange("p (c n) -> p c n", c=2),
                                             ps[0:TT, 4:6, 0:HD // 2], ACT.Copy).then_inc(v_outA, 1)

                    for g in range(-2, NT):
                        if g >= 0:
                            act.wait_ge(ctx_ready, NT * L + g + 1)
                            if g >= 1:
                                act.wait_ge(o_ready, NT * L + g)
                            nc.scalar.activation(
                                ctxT[:, :, :].rearrange("p m t -> p (m t)")[:, 0:4 * TT], ps[:, 6, 0:4 * TT],
                                ACT.Copy)
                            nc.scalar.activation(
                                ctxT[:, :, :].rearrange("p m t -> p (m t)")[:, 4 * TT:], ps[:, 7, 0:2 * TT],
                                ACT.Copy).then_inc(ctx_out, 1)
                        if g + 2 < NT:
                            act.wait_ge(s_max, NT * L + g + 3)
                            exps(g % 2, 1.0).then_inc(e_ready, 1)
                    norm_out(2 + 2 * L, lnc[2 * odd + 1])
                    if odd:
                        act.wait_ge(g_mx, lp + 1)
                        nc.scalar.activation(gsm[:, 1, :], gsm[:, 0, :], ACT.Exp).then_inc(g_exp, 1)
                    hidden_out(5 * lp, odd, ACT.Relu)
                with act.Fori(0, E0 // 2) as ep:
                    for u in range(2):
                        hidden_out(5 * lp + 1 + ep, u, ACT.Gelu)
            norm_out(1 + 2 * LAYERS)
            norm_out(2 + 2 * LAYERS)
            act.wait_ge(g_mx, LAYERS // 2 + 1)
            for g in range(NT):
                nc.scalar.activation(cw[:, g, :], logit[:, g, :], ACT.Exp, bias=gsm[:, 0, g:g + 1],
                                     accum_out=gsm[:, 1, g:g + 1]).then_inc(g_exp, 1)
            act.wait_ge(cwT_ready, NT)
            nc.scalar.activation(cwT[:, 0:4 * TT], ps[0:E1, 2, 0:4 * TT], ACT.Copy).then_inc(cwT_out, 1)
            nc.scalar.activation(cwT[:, 4 * TT:], ps[0:E1, 3, 0:TT], ACT.Copy).then_inc(cwT_out, 1)
            act.wait_ge(rounds_ready, 1)
            rounds = act.value_load(rounds_sb[0:1, 0:1], min_val=1, max_val=MAXR)
            with act.Fori(0, rounds) as rd:
                with act.Fori(0, E1 // 2) as ep:
                    i = 8 * rd + ep
                    for u in range(2):
                        act.wait_ge(x_gather, 2 * i + u + 1)
                        nc.scalar.activation(xg[u], ps[0:KD, u, 0:2 * CAP].rearrange("p (k c) -> p k c", k=2),
                                             ACT.Copy).then_inc(x_gout, 1)
                        nc.scalar.activation(putT[u][:, 4 * TT:], ps[0:CAP, u, 256:256 + TT], ACT.Copy)
                        act.wait_ge(x_T, 2 * i + u + 1)
                        nc.scalar.activation(putT[u][:, 0:4 * TT], ps[0:CAP, 2 + u, 0:4 * TT], ACT.Copy).then_inc(x_Tout, 1)
                    for u in range(2):
                        act.wait_ge(eb_in[u], 16 * (i + 1))
                        for f in range(FT):
                            act.wait_ge(x_up, 2 * FT * i + FT * u + f + 1)
                            nc.scalar.activation(hidden[u][:, f, 0:CAP], ps[:, 4 + f % 2, 0:CAP], ACT.Gelu,
                                                 bias=eb1_sb[u][:, f:f + 1]).then_inc(x_hout, 1)
                    for u in range(2):
                        act.wait_ge(x_down, 2 * i + u + 1)
                        nc.scalar.activation(yg[u], ps[0:CAP, 6 + u, 0:D], ACT.Copy).then_inc(x_ygout, 1)

        @block.vector
        def _(dve):
            chain = Chain(dve, d_chain)
            link = chain.link
            V = nc.vector

            def layer_norm(n, src, dst, eps, signal):
                for g in range(NT):
                    last = V.bn_stats(stats[:, g, :], src[:, g, :])
                link(last)
                for g in range(NT):
                    last = V.bn_aggr(mv[:, g, :], stats[:, g, :])
                link(last)
                V.tensor_scalar(rstd[:, :], mv[:, :, 1], eps, None, ALU.add).then_inc(n_stats, 1)
                dve.wait_ge(n_rstd, n + 1)
                for g in range(NT):
                    ins = V.tensor_scalar(dst[:, g, :], src[:, g, :], mv[:, g, 0:1], rstd[:, g:g + 1],
                                          ALU.subtract, ALU.mult)
                    if signal:
                        ins.then_inc(n_scaled, 1)
                    elif g == NT - 1:
                        link(ins)

            def mean_square(src, dst, g):
                return V.tensor_tensor_reduce(out=dst[:, g, :], in0=src[:, g, :], in1=src[:, g, :], scale=1.0 / D,
                                              scalar=1e-6, op0=ALU.mult, op1=ALU.add, accum_out=rstd[:, g:g + 1])

            def tile_stats(g):
                mean_square(hid, xs, g).then_inc(t_stats, 1)

            def tile_scale(q, g):
                dve.wait_ge(t_rstd, NT * q + g + 1)
                V.tensor_scalar(xs[:, g, :], hid[:, g, :], rstd[:, g:g + 1], None, ALU.mult).then_inc(n_scaled, 1)

            def t5_norm(n, src, dst, signal):
                for g in range(NT):
                    last = mean_square(src, dst, g)
                last.then_inc(n_stats, 1)
                dve.wait_ge(n_rstd, n + 1)
                for g in range(NT):
                    ins = V.tensor_scalar(dst[:, g, :], src[:, g, :], rstd[:, g:g + 1], None, ALU.mult)
                    if signal:
                        ins.then_inc(n_scaled, 1)
                    elif g == NT - 1:
                        link(ins)

            def norm_out(v, col=None):
                for g in range(NT):
                    dve.wait_ge(n_T, NT * v + g + 1)
                    src = ps[0:KD, 2 + g % 2, 0:TT]
                    dst = xT[:, 1, g * TT:(g + 1) * TT]
                    if col is None:
                        V.tensor_copy(dst, src).then_inc(n_outD, 1)
                    else:
                        V.tensor_scalar(dst, src, col[:, 1, :], None, ALU.mult).then_inc(n_outD, 1)

            dve.wait_ge(s_const, 16 * N_CONST)
            c = lambda i: lam[:, i:i + 1]
            link(V.tensor_scalar(c(2), c(0), -DT / 2, 1.0, ALU.mult, ALU.add))
            link(V.tensor_scalar(c(3), c(0), DT / 2, 1.0, ALU.mult, ALU.add))
            link(V.tensor_scalar(c(4), c(1), DT / 2, None, ALU.mult))
            link(V.tensor_tensor(c(5), c(2), c(2), ALU.mult))
            link(V.tensor_tensor(c(6), c(4), c(4), ALU.mult))
            link(V.tensor_tensor(c(5), c(5), c(6), ALU.add))
            link(V.reciprocal(c(6), c(5)))
            link(V.tensor_tensor(c(7), c(2), c(6), ALU.mult))
            link(V.tensor_tensor(c(8), c(4), c(6), ALU.mult))
            link(V.tensor_tensor(c(9), c(3), c(7), ALU.mult))
            link(V.tensor_tensor(c(10), c(4), c(8), ALU.mult))
            link(V.tensor_tensor(c(9), c(9), c(10), ALU.subtract))
            link(V.tensor_tensor(c(10), c(3), c(8), ALU.mult))
            link(V.tensor_tensor(c(11), c(4), c(7), ALU.mult))
            link(V.tensor_tensor(c(10), c(10), c(11), ALU.add))
            link(V.tensor_scalar(c(11), c(10), -1.0, None, ALU.mult))
            rt = float(np.sqrt(np.float32(DT)))
            link(V.tensor_scalar(c(12), c(7), rt, None, ALU.mult))
            link(V.tensor_scalar(c(13), c(8), rt, None, ALU.mult))
            def sum_wte(j):
                dve.wait_ge(s_wte[j % WBUF], 16 * (j // WBUF + 1))
                V.tensor_reduce(part[:, W_DVE.index(j), :], wte_sb[:, j % WBUF, :, :].rearrange("p r d -> p d r"),
                                AX.X, ALU.add).then_inc(wte_used, 1)

            for j in W_DVE[:5]:
                sum_wte(j)
            for g in range(NT):
                dve.wait_ge(tok_ready, g + 1)
                V.scalar_tensor_tensor(
                    out=res[:, g, :], in0=cls_sb[:, :], scalar=cmask_sb[:, 0:1],
                    in1=ps[0:TT, 4 + g % 4, 0:D], op0=ALU.mult, op1=ALU.add).then_inc(tok_out, 1)
            dve.wait_ge(tok_out, NT)
            layer_norm(0, res, xs, 1e-5, False)
            layer_norm(1, xs, xs, 1e-5, True)
            norm_out(0, lnw_sb)
            dve.wait_ge(r_ready, 1)
            V.tensor_copy(R_sb[:, :, :].rearrange("p t h -> p (t h)"), ps[0:TT, 7, 0:SEQ * H]).then_inc(r_out, 1)

            def masked_max0(g):
                i = g % 2
                dve.wait_ge(a_s, g + 1)
                if g >= 2:
                    dve.wait_ge(a_T, 3 * (g - 1))
                link(V.tensor_tensor(
                    prob[i][:, :, :].rearrange("p (c h) t -> p c h t", c=4),
                    ps[0:TT, 0:4, 0:3 * TT].rearrange("p c (h t) -> p c h t", h=3),
                    mask_sb[:, :].unsqueeze(1).unsqueeze(1).to_broadcast([TT, 4, 3, TT]), ALU.add))
                link(V.tensor_reduce(mx[i][:, :].rearrange("p (h c) -> p c h", c=2),
                                     prob[i][:, :, :].rearrange("p (c h) t -> p c h t", c=2), AX.X, ALU.max))
                V.tensor_scalar(nmx[i][:, :], mx[i][:, :], -SCALE, None, ALU.mult).then_inc(a_masked, 1)

            later = iter(W_DVE[5:])
            masked_max0(0)
            for g in range(NT):
                i = g % 2
                sum_wte(next(later))
                dve.wait_ge(a_exp, g + 1)
                link(V.reciprocal(rinv[:, :], rsum[i][:, :]))
                link(V.tensor_scalar(rinv[:, :], rinv[:, :], nreg_sb[:, 0:1], None, ALU.mult))
                V.tensor_tensor(prob[i][:, :, :].rearrange("p (c h) t -> p c h t", c=2),
                                prob[i][:, :, :].rearrange("p (c h) t -> p c h t", c=2),
                                rinv[:, :].rearrange("p (h c) -> p c h", c=2).unsqueeze(3).to_broadcast([TT, 2, 6, TT]),
                                ALU.mult).then_inc(a_norm, 1)
                sum_wte(next(later))
                if g + 1 < NT:
                    masked_max0(g + 1)
                sum_wte(next(later))
                dve.wait_ge(a_y, g + 1)
                V.tensor_tensor(res[:, g, :], res[:, g, :], ps[0:TT, 5, 0:D], ALU.add).then_inc(a_yout, 1)
            for j in later:
                sum_wte(j)
            dve.wait_ge(wte_used, len(W_DVE))
            dve.wait_ge(s_wtail, 16)
            link(V.tensor_reduce(psum_all[:, :], part[:, :, :].rearrange("p j d -> p d j"), AX.X, ALU.add))
            dve.wait_ge(pe_sum_out, 1)
            link(V.tensor_tensor(psum_all[0:1, :], psum_all[0:1, :], pe_sum[:, 0:D], ALU.add))
            V.tensor_tensor(psum_all[0:1, :], psum_all[0:1, :], pe_sum[:, D:2 * D], ALU.add).then_inc(avg_sum, 1)
            dve.wait_ge(rbc_ready, 1)
            dve.wait_ge(a_yout, NT)
            for g in range(NT):
                last = V.scalar_tensor_tensor(out=res[:, g, :], in0=ps[0:TT, 5, 0:D], scalar=nreg_sb[:, 1:2],
                                              in1=res[:, g, :], op0=ALU.mult, op1=ALU.add)
            link(last)
            layer_norm(2, res, hid, 1e-5, False)
            dve.wait_ge(biasm_ready, H)
            dve.wait_ge(zero_kv, 5)

            def gate_weights(v, width):
                for g in range(NT):
                    link(V.tensor_scalar(cwb[:, 0:width], iota_sb[:, 0:width], idf[:, g, 0:1], gsm[:, 2, g:g + 1],
                                         ALU.is_equal, ALU.mult))
                    link(V.tensor_scalar(cw[:, g, 0:width], iota_sb[:, 0:width], idf[:, g, 1:2], gsm[:, 3, g:g + 1],
                                         ALU.is_equal, ALU.mult))
                    ins = V.tensor_tensor(cw[:, g, 0:width], cw[:, g, 0:width], cwb[:, 0:width], ALU.add)
                    if g == NT - 1:
                        ins.then_inc(cw_ready, 1)
                        dve.wait_ge(cw_ready, v + 1)
                    else:
                        link(ins)

            def top2(src, width):
                V.memset(idle[:, :], 0.0)
                for g in range(NT):
                    last = V.max(top[:, g, :], src[:, g, 0:width])
                link(last)
                V.memset(idle[:, :], 0.0)
                for g in range(NT):
                    last = V.max_index(idx[:, g, :], top[:, g, :], src[:, g, 0:width])
                link(last)
                link(V.tensor_copy(idf[:, :, :], idx[:, :, 0:2]))

            def layer(lp, odd, base, per):
                L = 2 * lp + odd
                chain.base, chain.n = base, 0
                if not odd:
                    for w, src in enumerate((ln1_sb, ln2_sb)):
                        for o in range(2):
                            last = V.tensor_copy(lnc[2 * o + w][:, :, :], src[:, :, bass.ds(L + o, 1)])
                    link(last)
                if not odd:
                    t5_norm(NORM_L + lp, hid, xs, True)
                norm_out(1 + 2 * L, lnc[2 * odd])
                for m in range(6):
                    dve.wait_ge(qk_ready, 12 * L + 2 * m + 2)
                    V.tensor_copy(kT[0][0:64, m, 0:TOK].rearrange("p (c n) -> p c n", c=2), ps[0:64, 2:4, 0:CH])
                    V.tensor_copy(kT[1][64:128, m, 0:TOK].rearrange("p (c n) -> p c n", c=2),
                                  ps[64:128, 2:4, 0:CH]).then_inc(k_out, 1)
                for g in range(1, NT, 2):
                    dve.wait_ge(v_ready, NT * L + g + 1)
                    V.tensor_copy(v_sb[:, g, :].rearrange("p (c n) -> p c n", c=2),
                                  ps[0:TT, 6:8, 0:HD // 2]).then_inc(v_outD, 1)

                def masked_max(g):
                    i = g % 2
                    dve.wait_ge(s_ready, NT * L + g + 1)
                    ins = V.tensor_tensor(
                        prob[i][:, :, :].rearrange("p (c h) t -> p c (h t)", c=4), ps[0:TT, 0:4, 0:3 * TT],
                        biasM[:, :, :].rearrange("p (c h) t -> p c (h t)", c=4), ALU.add)
                    ins.then_inc(s_masked, 1)
                    dve.wait_ge(s_masked, NT * L + g + 1)
                    link(V.tensor_reduce(mx[i][:, :].rearrange("p (h c) -> p c h", c=2),
                                         prob[i][:, :, :].rearrange("p (c h) t -> p c h t", c=2), AX.X, ALU.max))
                    V.tensor_scalar(nmx[i][:, :], mx[i][:, :], -1.0, None, ALU.mult).then_inc(s_max, 1)

                def add_o(g):
                    dve.wait_ge(o_ready, NT * L + g + 1)
                    V.tensor_tensor(hid[:, g, :], hid[:, g, :], ps[0:TT, 7, 0:D], ALU.add).then_inc(o_out, 1)
                    dve.wait_ge(o_out, NT * L + g + 1)

                def normalise(g):
                    i = g % 2
                    dve.wait_ge(e_ready, NT * L + g + 1)
                    link(V.reciprocal(rinv[:, :], rsum[i][:, :]))
                    V.tensor_tensor(prob[i][:, :, :].rearrange("p (c h) t -> p c h t", c=2),
                                    prob[i][:, :, :].rearrange("p (c h) t -> p c h t", c=2),
                                    rinv[:, :].rearrange("p (h c) -> p c h", c=2).unsqueeze(3).to_broadcast([TT, 2, 6, TT]),
                                    ALU.mult).then_inc(p_ready, 1)

                masked_max(0)
                masked_max(1)
                normalise(0)
                for g in range(NT):
                    for r in range(3):
                        if r == 2 and g >= 1:
                            add_o(g - 1)
                            tile_stats(g - 1)
                        dve.wait_ge(at_ready, 3 * (NT * L + g) + r + 1)
                        V.tensor_copy(probT[:, 4 * r:4 * r + 4, :].rearrange("p h t -> p (h t)"),
                                      ps[0:TT, 4 + (15 * odd + 3 * g + r) % 2, 0:4 * TT]).then_inc(at_out, 1)
                    if g >= 1:
                        tile_scale(3 * lp + 2 * odd, g - 1)
                    if g + 1 < NT:
                        normalise(g + 1)
                    if g + 2 < NT:
                        masked_max(g + 2)
                add_o(NT - 1)
                tile_stats(NT - 1)
                tile_scale(3 * lp + 2 * odd, NT - 1)
                norm_out(2 + 2 * L, lnc[2 * odd + 1])
                if odd:
                    dve.wait_ge(lg_ready, lp + 1)
                    V.tensor_copy(logit[:, :, 0:E0], ps[0:TT, 7, 0:NT * E0].rearrange(
                        "p (g e) -> p g e", g=NT)).then_inc(lg_out, 1)
                    dve.wait_ge(lg_out, lp + 1)
                    top2(logit, E0)
                    V.tensor_tensor(gsm[:, 0, :], top[:, :, 1], top[:, :, 0], ALU.subtract).then_inc(g_mx, 1)
                    dve.wait_ge(g_exp, lp + 1)
                    link(V.tensor_scalar(gsm[:, 4, :], gsm[:, 1, :], 1.0, None, ALU.add))
                    link(V.reciprocal(gsm[:, 2, :], gsm[:, 4, :]))
                    link(V.tensor_tensor(gsm[:, 3, :], gsm[:, 1, :], gsm[:, 2, :], ALU.mult))
                    gate_weights(lp, E0)
                add_ffn(10 * lp + odd, 5 * lp, odd, 3 * lp + 1)
                assert chain.n == per, (odd, chain.n)

            def add_ffn(t, j, u, q):
                for g in range(NT):
                    dve.wait_ge(down_ready[u], NT * j + g + 1)
                    r = rows(g)
                    V.tensor_tensor(hid[0:r, g, :], hid[0:r, g, :], ps[0:r, 4 + g % 4, 0:D], ALU.add).then_inc(y_out, 1)
                    if u == 0:
                        dve.wait_ge(y_out, NT * t + g + 1)
                        tile_stats(g)
                        if g >= 1:
                            tile_scale(q, g - 1)
                if u == 0:
                    tile_scale(q, NT - 1)
                V.memset(idle[:, :], 0.0)

            def add_expert(t, j, u, e, dst):
                dve.wait_ge(y_out, NT * t)
                for g in range(NT):
                    dve.wait_ge(down_ready[u], NT * j + g + 1)
                    r = rows(g)
                    V.scalar_tensor_tensor(out=dst[0:r, g, :],
                                           in0=ps[0:r, 4 + g % 4, 0:D],
                                           scalar=cw[0:r, g, bass.ds(e, 1)], in1=dst[0:r, g, :],
                                           op0=ALU.mult, op1=ALU.add).then_inc(y_out, 1)

            base = chain.n
            PER = [1 + NT + NT, NT + NT + 3 + 3 + 3 * NT - 1]
            with dve.Fori(0, LAYERS // 2) as lp:
                for odd in range(2):
                    layer(lp, odd, base + (PER[0] + PER[1]) * lp + PER[0] * odd, PER[odd])
                with dve.Fori(0, E0 // 2) as ep:
                    for u in range(2):
                        add_expert(10 * lp + 2 + 2 * ep + u, 5 * lp + 1 + ep, u, 2 * ep + u, hid)
            chain.base, chain.n = 0, base + (PER[0] + PER[1]) * (LAYERS // 2)
            dve.wait_ge(y_out, NT * 20)
            t5_norm(NORM_F, hid, xs, False)
            dve.wait_ge(s_cn2, 16 * 5)
            for g in range(NT):
                last = V.tensor_tensor(xs[:, g, :], xs[:, g, :], lnf_sb[:, :], ALU.mult)
            link(last)
            for g in range(NT):
                last = V.tensor_tensor(res[:, g, :], res[:, g, :], xs[:, g, :], ALU.add)
            link(last)
            layer_norm(NORM_F + 1, res, xs, 1e-5, True)
            norm_out(1 + 2 * LAYERS)
            dve.wait_ge(ss_bu, 1)
            for k in range(2):
                last = V.tensor_scalar(hst[:, k, :].rearrange("p (c n) -> p c n", c=2), ps[0:NSTATE, 0:2, 0:CH],
                                       c(12 + k), None, ALU.mult)
            link(last)
            hv = hst.rearrange("p c (b s) -> p c b s", s=SEQ)
            for t in range(1, SEQ):
                link(V.scalar_tensor_tensor(out=hv[:, :, :, t], in0=hv[:, :, :, t - 1], scalar=c(9),
                                            in1=hv[:, :, :, t], op0=ALU.mult, op1=ALU.add))
                V.scalar_tensor_tensor(out=hv[:, 0, :, t], in0=hv[:, 1, :, t - 1], scalar=c(11),
                                       in1=hv[:, 0, :, t], op0=ALU.mult, op1=ALU.add)
                link(V.scalar_tensor_tensor(out=hv[:, 1, :, t], in0=hv[:, 0, :, t - 1], scalar=c(10),
                                            in1=hv[:, 1, :, t], op0=ALU.mult, op1=ALU.add))
            V.tensor_copy(lam[:, 14:15], lam[:, 13:14]).then_inc(ss_h, 1)
            for g in range(NT):
                dve.wait_ge(ss_y, g + 1)
                r = rows(g)
                V.tensor_tensor(res[0:r, g, :], res[0:r, g, :],
                                ps[0:r, 4 + g % 4, 0:D], ALU.add).then_inc(ss_yout, 1)
            dve.wait_ge(ss_yout, NT)
            layer_norm(NORM_F + 2, res, xs, 1e-5, True)
            norm_out(2 + 2 * LAYERS)
            dve.wait_ge(n_scaled, NT * (3 + 2 * LAYERS))
            for g in range(NT):
                last = V.tensor_tensor(res[:, g, :], res[:, g, :], xs[:, g, :], ALU.add)
            link(last)
            dve.wait_ge(lg_ready, LAYERS // 2 + 1)
            link(V.tensor_copy(logit[:, :, :], ps[0:TT, 0, 0:NT * E1].rearrange("p (g e) -> p g e", g=NT)))
            link(V.tensor_reduce(gsm[:, 5, :], logit[:, :, :], AX.X, ALU.max))
            V.tensor_scalar(gsm[:, 0, :], gsm[:, 5, :], -1.0, None, ALU.mult).then_inc(g_mx, 1)
            dve.wait_ge(g_exp, LAYERS // 2 + NT)
            link(V.reciprocal(gsm[:, 4, :], gsm[:, 1, :]))
            link(V.tensor_tensor(logit[:, :, :], cw[:, :, :],
                                 gsm[:, 4, :].unsqueeze(2).to_broadcast([TT, NT, E1]), ALU.mult))
            top2(logit, E1)
            for k in range(2):
                last = V.tensor_copy(gsm[:, 2 + k, :], top[:, :, k])
            link(last)
            gate_weights(LAYERS // 2, E1)
            dve.wait_ge(route_in, 16 * 3)
            V.scalar_tensor_tensor(out=asg[:, :, :], in0=cw[:, :, :], scalar=0.0,
                                   in1=valid_sb[:, :].unsqueeze(2).to_broadcast([TT, NT, E1]),
                                   op0=ALU.is_gt, op1=ALU.mult).then_inc(asg_ready, 1)
            dve.wait_ge(pos_ready, 1)
            link(V.scalar_tensor_tensor(out=place[:, :, :].rearrange("p g e -> p (g e)"), in0=ps[0:TT, 1, 0:NT * E1],
                                        scalar=1.0, in1=asg[:, :, :].rearrange("p g e -> p (g e)"),
                                        op0=ALU.add, op1=ALU.mult))
            V.memset(most[:, 1:2], 1.0)
            link(V.tensor_reduce(most[:, 0:1], ps[0:TT, 1, NT * E1:(NT + 1) * E1], AX.X, ALU.max))
            for m in range(1, MAXR):
                link(V.scalar_tensor_tensor(out=most[:, 1:2], in0=most[:, 0:1], scalar=float(m * CAP),
                                            in1=most[:, 1:2], op0=ALU.is_gt, op1=ALU.add))
            V.tensor_copy(rounds_sb[:, :], most[0:1, 1:2]).then_inc(rounds_ready, 1)

            def one_hots(e, u):
                for g in range(NT):
                    V.tensor_scalar(pick[u][:, g, :], slots_sb, place[:, g, e], None, ALU.is_equal)
                    last = V.tensor_scalar(put[u][:, g, :], slots_sb, place[:, g, e], cw[:, g, e],
                                           ALU.is_equal, ALU.mult)
                last.then_inc(x_pick, 1)

            for u in range(2):
                one_hots(slice(u, u + 1), u)
            for g in range(NT):
                dve.wait_ge(b2_ready, g + 1)
                r = rows(g)
                V.tensor_tensor(res[0:r, g, :], res[0:r, g, :], ps[0:r, 4 + g % 4, 0:D], ALU.add).then_inc(x_yout, 1)
            dve.wait_ge(x_yout, NT)
            dve.wait_ge(rounds_ready, 1)
            rounds = dve.value_load(rounds_sb[0:1, 0:1], min_val=1, max_val=MAXR)

            def add_back(i):
                for u in range(2):
                    dve.wait_ge(x_yout, NT + 2 * NT * i + NT * u)
                    for g in range(NT):
                        n = NT * u + g
                        dve.wait_ge(x_back, 2 * NT * i + n + 1)
                        r = rows(g)
                        V.tensor_tensor(res[0:r, g, :], res[0:r, g, :], ps[0:r, n % 4, 0:D], ALU.add).then_inc(x_yout, 1)

            with dve.Fori(0, rounds) as rd:
                with dve.Fori(0, E1 // 2 - 1) as ep:
                    for u in range(2):
                        dve.wait_ge(x_T, 2 * (8 * rd + ep) + u + 1)
                        one_hots(bass.ds(2 * ep + 2 + u, 1), u)
                    add_back(8 * rd + ep)
                dve.wait_ge(x_T, 2 * (8 * rd + 7) + 2)
                V.tensor_scalar(place[:, :, :], place[:, :, :], -float(CAP), None, ALU.add).then_inc(place_next, 1)
                dve.wait_ge(place_next, rd + 1)
                for u in range(2):
                    one_hots(slice(u, u + 1), u)
                add_back(8 * rd + 7)
            dve.wait_ge(x_yout, NT + 2 * NT * 8 * rounds)
            V.tensor_copy(lam[:, 14:15], lam[:, 13:14]).then_inc(fin, 1)

        @block.tensor
        def _(pe):
            T = nc.tensor

            def slot(g, n=TT):
                return ps[0:n, 4 + g % 4, 0:D]

            def tile(g, r=TT):
                return slice(g * TT, g * TT + r)

            def norm_transposes(v):
                for g in range(NT):
                    pe.wait_ge(n_scaled, NT * v + g + 1)
                    if g >= 2:
                        pe.wait_ge(n_outA, NT * v + g - 1)
                        pe.wait_ge(n_outD, NT * v + g - 1)
                    for k in range(2):
                        last = T.transpose(ps[0:KD, 2 * k + g % 2, 0:TT],
                                           xs[:, g, k * KD:(k + 1) * KD], idn[0:TT, 0:TT])
                    last.then_inc(n_T, 1)

            def normed(v):
                pe.wait_ge(n_outA, NT * (v + 1))
                pe.wait_ge(n_outD, NT * (v + 1))

            pe.wait_ge(s_in, 48)
            for f in range(6):
                if f >= 4:
                    pe.wait_ge(fold_out, f - 3)
                for i in range(2):
                    last = T.matmul(ps[:, f % 4, 0:D],
                                    k2_sb[:, i, (f % 2) * 128:(f % 2) * 128 + 128], wtok_sb[:, 2 * (f // 2) + i, :],
                                    start=(i == 0), stop=(i == 1))
                last.then_inc(fold_ready, 1)
            pe.wait_ge(fold_out, 6)
            pe.wait_ge(xp_ready, 6)
            pe.wait_ge(zeroed, 5)
            for g in range(NT):
                if g == NT - 1:
                    pe.wait_ge(tok_out, 1)
                for k in range(6):
                    last = T.matmul(slot(g), xp[:, k, tile(g)], wfold[:, k, :], start=(k == 0), stop=(k == 5))
                last.then_inc(tok_ready, 1)
            for j in W_PE:
                pe.wait_ge(s_wte[j % WBUF], 16 * (j // WBUF + 1))
                for row in range(0, WROWS, 2):
                    last = T.matmul(ps[:, 0, 0:2 * D], ones[:, :],
                                    wte_sb[:, j % WBUF, row:row + 2, :].rearrange("p r d -> p (r d)"),
                                    start=(j == W_PE[0] and row == 0), stop=(j == W_PE[-1] and row == WROWS - 2))
                last.then_inc(wte_used_pe, 1)
            pe.wait_ge(s_const, 16 * N_CONST)
            pe.wait_ge(pe_sum_out, 1)
            norm_transposes(0)
            normed(0)
            for t in range(SEQ):
                last = T.matmul(ps[0:TT, 7, t * H:(t + 1) * H], oh_sb[:, t, :], rel_sb[:, :], start=True, stop=True)
            last.then_inc(r_ready, 1)
            def scores(g):
                pe.wait_ge(qs_ready, 2 * (g + 1))
                if g >= 1:
                    pe.wait_ge(a_masked, g)
                for h in range(H):
                    p = pos(h)
                    for k in range(2):
                        last = T.matmul(ps[0:TT, p // 3, (p % 3) * TT:(p % 3 + 1) * TT], qs[g % 2][:, k, h, :],
                                        qs[g % 2][:, k, h, :], start=(k == 0), stop=(k == 1))
                last.then_inc(a_s, 1)

            def project0(g):
                for b in range(6):
                    n = 6 * g + b
                    if n >= 2:
                        pe.wait_ge(a_pout, n - 1)
                    for k in range(2):
                        last = T.matmul(ps[0:TT, 6 + b % 2, 0:2 * D], xT[:, k, tile(g)],
                                        wot_sb[:, k, 2 * b:2 * b + 2, :].rearrange("p h d -> p (h d)"),
                                        start=(k == 0), stop=(k == 1))
                    last.then_inc(a_p, 1)

            pe.wait_ge(s_wot, 16)
            pe.wait_ge(r_out, 1)
            project0(0)
            scores(0)
            for g in range(NT):
                if g + 1 < NT:
                    scores(g + 1)
                pe.wait_ge(a_norm, g + 1)
                for r in range(3):
                    if r == 1 and g >= 1:
                        pe.wait_ge(a_yout, g)
                    if r == 2:
                        pe.wait_ge(a_Tout, 3 * g + 1)
                    for q in range(4):
                        last = T.transpose(ps[0:TT, 4 + r % 2, q * TT:(q + 1) * TT], prob[g % 2][:, 4 * r + q, :],
                                           idn[0:TT, 0:TT])
                    last.then_inc(a_T, 1)
                pe.wait_ge(a_Tout, 3 * (g + 1))
                pe.wait_ge(a_pout, 6 * (g + 1))
                for h in range(H):
                    last = T.matmul(ps[0:TT, 5, 0:D], probT[:, pos(h), :], po_sb[:, h, :], start=(h == 0), stop=(h == H - 1))
                last.then_inc(a_y, 1)
                if g + 1 < NT:
                    project0(g + 1)
            pe.wait_ge(avg_sum, 1)
            for k in range(2):
                last = T.matmul(ps[0:KD, 4, k * TT:(k + 1) * TT], psum_all[:, k * KD:(k + 1) * KD], onesv[:, :],
                                start=True, stop=True)
            last.then_inc(avg_T, 1)
            pe.wait_ge(avg_out, 1)
            for h in range(H):
                for k in range(2):
                    last = T.matmul(ps[0:TT, 5, 0:D], avgB[:, k, :], wot_sb[:, k, h, :],
                                    start=(h == 0 and k == 0), stop=(h == H - 1 and k == 1))
            last.then_inc(rbc_ready, 1)
            pe.wait_ge(zero_kv, 5)

            def up(t, u, w1):
                for f in range(FT):
                    if f >= 2:
                        pe.wait_ge(hid_out, FT * t + f - 1)
                    for c in range(2):
                        for k in range(2):
                            last = T.matmul(ps[:, 2 * (f % 2) + c, 0:CH], w1[:, k, f * 128:(f + 1) * 128],
                                            xT[:, k, c * CH:(c + 1) * CH], start=(k == 0), stop=(k == 1))
                    last.then_inc(up_ready[u], 1)

            def down(t, u, w2, first=False):
                if not first:
                    pe.wait_ge(y_out, NT * t)
                for g in range(NT):
                    if g == NT - 1:
                        pe.wait_ge(y_out, NT * t + 1)
                    for f in range(FT):
                        if g == 0:
                            pe.wait_ge(hid_out, FT * t + f + 1)
                        last = T.matmul(slot(g, rows(g)), hidden[u][:, f, tile(g, rows(g))], w2[:, f, :],
                                        start=(f == 0), stop=(f == FT - 1))
                    last.then_inc(down_ready[u], 1)

            with pe.Fori(0, LAYERS // 2) as lp:
                for odd in range(2):
                    L = 2 * lp + odd
                    norm_transposes(1 + 2 * L)
                    pe.wait_ge(w_in["wq"], 16 * (L + 1))
                    pe.wait_ge(w_in["wk"], 16 * (L + 1))
                    normed(1 + 2 * L)
                    for m in range(6):
                        for b, w, read in ((0, wq_sb, q_out), (2, wk_sb, k_out)):
                            if m >= 1:
                                pe.wait_ge(read, 6 * L + m)
                            for c in range(2):
                                for k in range(2):
                                    last = T.matmul(ps[:, b + c, 0:CH], w[:, k, m * 128:(m + 1) * 128],
                                                    xT[:, k, c * CH:(c + 1) * CH], start=(k == 0), stop=(k == 1))
                            last.then_inc(qk_ready, 1)
                    pe.wait_ge(w_in["wv"], 16 * (L + 1))
                    for g in range(NT):
                        if g >= 2:
                            if g % 2 == 0:
                                pe.wait_ge(v_outA, 3 * L + g // 2)
                            else:
                                pe.wait_ge(v_outD, 2 * L + g // 2)
                        for c in range(2):
                            for k in range(2):
                                last = T.matmul(ps[0:TT, 4 + 2 * (g % 2) + c, 0:HD // 2], xT[:, k, tile(g)],
                                                wv_sb[:, k, c * (HD // 2):(c + 1) * (HD // 2)],
                                                start=(k == 0), stop=(k == 1))
                        last.then_inc(v_ready, 1)

                    def scores2(g):
                        if g == 0:
                            pe.wait_ge(q_out, 6 * (L + 1))
                            pe.wait_ge(k_out, 6 * (L + 1))
                        else:
                            pe.wait_ge(s_masked, NT * L + g)
                        for h in range(H):
                            p = pos(h)
                            last = T.matmul(ps[0:TT, p // 3, (p % 3) * TT:(p % 3 + 1) * TT], qT[:, h // 2, tile(g)],
                                            kT[h % 2][:, h // 2, tile(g)], start=True, stop=True)
                        last.then_inc(s_ready, 1)

                    def project(g):
                        if g == 0:
                            pe.wait_ge(w_in["wo"], 16 * (L + 1))
                        pe.wait_ge(ctx_out, NT * L + g + 1)
                        if g >= 1:
                            pe.wait_ge(o_out, NT * L + g)
                        for m in range(6):
                            last = T.matmul(ps[0:TT, 7, 0:D], ctxT[:, m, :], wo_sb[:, m, :],
                                            start=(m == 0), stop=(m == 5))
                        last.then_inc(o_ready, 1)

                    scores2(0)
                    scores2(1)
                    pe.wait_ge(v_outA, 3 * (L + 1))
                    pe.wait_ge(v_outD, 2 * (L + 1))
                    for g in range(NT):
                        pe.wait_ge(p_ready, NT * L + g + 1)
                        for r in range(3):
                            use = 3 * g + r
                            if r == 2 and g >= 1:
                                project(g - 1)
                            if use >= 2:
                                pe.wait_ge(at_out, 3 * NT * L + use - 1)
                            for q in range(4):
                                last = T.transpose(ps[0:TT, 4 + (15 * odd + use) % 2, q * TT:(q + 1) * TT],
                                                   prob[g % 2][:, 4 * r + q, :], idn[0:TT, 0:TT])
                            last.then_inc(at_ready, 1)
                        if g + 2 < NT:
                            scores2(g + 2)
                        pe.wait_ge(at_out, 3 * (NT * L + g + 1))
                        if g >= 1:
                            pe.wait_ge(o_out, NT * L + g)
                        for h in range(H):
                            m = h // 2
                            last = T.matmul(ps[DK * (h % 2):DK * (h % 2 + 1), 6 + m // 4, (m % 4) * TT:(m % 4 + 1) * TT],
                                            v_sb[:, g, h * DK:(h + 1) * DK], probT[:, pos(h), :], start=True, stop=True)
                        last.then_inc(ctx_ready, 1)
                    project(NT - 1)
                    norm_transposes(2 + 2 * L)
                    normed(2 + 2 * L)
                    if odd:
                        pe.wait_ge(gw_in, 16 * (lp + 1))
                        for g in range(NT):
                            for k in range(2):
                                last = T.matmul(ps[0:TT, 7, g * E0:(g + 1) * E0], xT[:, k, tile(g)],
                                                gw_sb[:, k, :], start=(k == 0), stop=(k == 1))
                        last.then_inc(lg_ready, 1)
                    pe.wait_ge(w_in["f1"], 16 * (L + 1))
                    up(10 * lp + odd, odd, fw1_sb)
                    pe.wait_ge(w_in["f2"], 16 * (L + 1))
                    if odd:
                        pe.wait_ge(lg_out, lp + 1)
                    down(10 * lp + odd, odd, fw2_sb, first=True)
                with pe.Fori(0, E0 // 2) as ep:
                    for u in range(2):
                        pe.wait_ge(e1_in[u], 64 * lp + 16 * (ep + 1))
                        up(10 * lp + 2 + 2 * ep + u, u, ew1_sb[u])
                        pe.wait_ge(e2_in[u], 64 * lp + 16 * (ep + 1))
                        down(10 * lp + 2 + 2 * ep + u, u, ew2_sb[u])
            norm_transposes(1 + 2 * LAYERS)
            normed(1 + 2 * LAYERS)
            for c in range(2):
                for k in range(2):
                    last = T.matmul(ps[0:NSTATE, c, 0:CH], bt_sb[:, k, :], xT[:, k, c * CH:(c + 1) * CH],
                                    start=(k == 0), stop=(k == 1))
            last.then_inc(ss_bu, 1)
            pe.wait_ge(ss_h, 1)
            for g in range(NT):
                if g == NT - 1:
                    pe.wait_ge(ss_yout, 1)
                T.matmul(slot(g, rows(g)), hst[:, 0, tile(g, rows(g))], ct_sb[:, :], start=True, stop=True).then_inc(ss_y, 1)
            norm_transposes(2 + 2 * LAYERS)
            normed(2 + 2 * LAYERS)
            for g in range(NT):
                for k in range(2):
                    last = T.matmul(ps[0:TT, 0, g * E1:(g + 1) * E1], xT[:, k, tile(g)], wr_sb[:, k, :],
                                    start=(k == 0), stop=(k == 1))
            last.then_inc(lg_ready, 1)
            pe.wait_ge(cw_ready, LAYERS // 2 + 1)
            for g in range(NT):
                T.transpose(ps[0:E1, 2 + g // 4, (g % 4) * TT:(g % 4 + 1) * TT], cw[:, g, :],
                            idn[0:TT, 0:TT]).then_inc(cwT_ready, 1)
            pe.wait_ge(asg_ready, 1)
            for g in range(NT):
                for b in range(g + 1):
                    last = T.matmul(ps[0:TT, 1, g * E1:(g + 1) * E1], tri_sb[:, :] if b == g else ones[0:TT, 0:TT],
                                    asg[:, b, :], start=(b == 0), stop=(b == g))
            for b in range(NT):
                last = T.matmul(ps[0:TT, 1, NT * E1:(NT + 1) * E1], ones[0:TT, 0:TT], asg[:, b, :],
                                start=(b == 0), stop=(b == NT - 1))
            last.then_inc(pos_ready, 1)
            pe.wait_ge(cwT_out, 2)
            for g in range(NT):
                if g == NT - 1:
                    pe.wait_ge(x_yout, 1)
                T.matmul(slot(g, rows(g)), cwT[:, tile(g, rows(g))], b2_sb[:, :], start=True, stop=True).then_inc(b2_ready, 1)
            pe.wait_ge(x_yout, NT)
            pe.wait_ge(rounds_ready, 1)
            rounds = pe.value_load(rounds_sb[0:1, 0:1], min_val=1, max_val=MAXR)
            with pe.Fori(0, rounds) as rd:
                with pe.Fori(0, E1 // 2) as ep:
                    i = 8 * rd + ep
                    pe.wait_ge(x_yout, NT + 2 * NT * i)
                    for u in range(2):
                        pe.wait_ge(x_pick, 2 * i + u + 1)
                        for k in range(2):
                            for g in range(NT):
                                T.matmul(ps[0:KD, u, k * CAP:(k + 1) * CAP], xs[:, g, k * KD:(k + 1) * KD],
                                         pick[u][:, g, :], start=(g == 0), stop=(g == NT - 1))
                        T.transpose(ps[0:CAP, u, 256:256 + TT], put[u][:, 4, :], idn[0:TT, 0:TT]).then_inc(x_gather, 1)
                        for g in range(4):
                            last = T.transpose(ps[0:CAP, 2 + u, g * TT:(g + 1) * TT], put[u][:, g, :], idn[0:TT, 0:TT])
                        last.then_inc(x_T, 1)
                    for u in range(2):
                        pe.wait_ge(e1_in[u], 16 * E0 + 16 * (i + 1))
                        pe.wait_ge(x_gout, 2 * i + u + 1)
                        for f in range(FT):
                            n = FT * u + f
                            if n >= 2:
                                pe.wait_ge(x_hout, 2 * FT * i + n - 1)
                            for k in range(2):
                                last = T.matmul(ps[:, 4 + f % 2, 0:CAP], ew1_sb[u][:, k, f * 128:(f + 1) * 128],
                                                xg[u][:, k, :], start=(k == 0), stop=(k == 1))
                            last.then_inc(x_up, 1)
                    for u in range(2):
                        pe.wait_ge(e2_in[u], 16 * E0 + 16 * (i + 1))
                        pe.wait_ge(x_hout, 2 * FT * i + FT * (u + 1))
                        for f in range(FT):
                            last = T.matmul(ps[0:CAP, 6 + u, 0:D], hidden[u][:, f, 0:CAP], ew2_sb[u][:, f, :],
                                            start=(f == 0), stop=(f == FT - 1))
                        last.then_inc(x_down, 1)
                    for u in range(2):
                        pe.wait_ge(x_ygout, 2 * i + u + 1)
                        pe.wait_ge(x_Tout, 2 * i + u + 1)
                        for g in range(NT):
                            n = NT * u + g
                            if n >= 4:
                                pe.wait_ge(x_yout, NT + 2 * NT * i + n - 3)
                            T.matmul(ps[0:rows(g), n % 4, 0:D], putT[u][:, tile(g, rows(g))], yg[u],
                                     start=True, stop=True).then_inc(x_back, 1)


def tables():
    n = np.arange(16, dtype=np.float32)
    dct = (2.0 * np.cos(np.float32(np.pi) * (2.0 * n[None, :] + 1.0) * n[:, None] / np.float32(32.0))).astype(np.float32)
    k2 = np.kron(dct, dct).astype(np.float32)
    tok = np.arange(TT)
    img, s = tok // SEQ, tok % SEQ
    same = img[:, None] == img[None, :]
    causal = np.where(same & (s[None, :] <= s[:, None]), 0.0, NEG).astype(np.float32)
    block = np.where(same, 0.0, NEG).astype(np.float32)
    nreg = (1.0 / (s + 1).astype(np.float32)).astype(np.float32)
    nreg = np.stack([nreg, -nreg], 1)
    clsmask = (s == 0).astype(np.float32)[:, None]
    rel = np.arange(SEQ)[None, :] - s[:, None]
    dist = np.abs(rel)
    large = 8 + (np.log(np.maximum(dist, 1).astype(np.float32) / np.float32(8)) / np.float32(np.log(128 / 8))
                 * np.float32(8)).astype(np.int32)
    bucket = (rel > 0) * 16 + np.where(dist < 8, dist, np.minimum(large, 15))
    onehot = (bucket.T[None, :, :] == np.arange(32)[:, None, None]).astype(np.float32)
    tri = (tok[:, None] < tok[None, :]).astype(np.float32)
    slots = np.tile(np.arange(1, CAP + 1, dtype=np.float32), (TT, 1))
    valid = np.stack([(tok < rows(g)) for g in range(NT)], 1).astype(np.float32)
    iota = np.tile(np.arange(E1, dtype=np.float32), (TT, 1))
    return dict(k2=k2.reshape(2, 128, 256).transpose(1, 0, 2), causal=causal, nreg=nreg, clsmask=clsmask,
                onehot=onehot, block_mask=block, ident=np.eye(128, dtype=np.float32), iota=iota,
                tri=tri, slots=slots, valid=valid)


def kernel(x, cls_tok, L0_tok_W, L0_attn_e, L0_attn_p, L0_attn_ln_w, L0_attn_W_qk, L0_attn_W_o, L0_attn_wte,
           L0_ffn_attn_q, L0_ffn_attn_k, L0_ffn_attn_v, L0_ffn_attn_o, L0_ffn_ffn_wi, L0_ffn_ffn_wo, L0_ffn_ln1,
           L0_ffn_ln2, L0_ffn_ln_f, L0_ffn_rel_emb, L0_ffn_gate_w, L0_ffn_moe_w1, L0_ffn_moe_w2, L1_attn_A_real,
           L1_attn_A_imag, L1_attn_B, L1_attn_C, L1_ffn_wr, L1_ffn_w1, L1_ffn_b1, L1_ffn_w2, L1_ffn_b2):
    import numpy as _np
    import concourse.bacc as _bacc
    from concourse import mybir as _mybir
    from concourse.bass_utils import run_bass_kernel_spmd as _run

    a = _np.asarray

    def halves(w):
        w = a(w)
        w = w.reshape(w.shape[:-2] + (2, KD, w.shape[-1]))
        return w.swapaxes(-3, -2)

    def sixths(w):
        w = a(w)
        w = w.reshape(w.shape[:-2] + (6, 128, w.shape[-1]))
        return w.swapaxes(-3, -2)

    ins = dict(tables())
    xb = a(x).reshape(BATCH, 3, 4, 16, 4, 16).transpose(1, 3, 5, 0, 2, 4).reshape(6, 128, BATCH * 16)
    ins["xst"] = xb.transpose(1, 0, 2).reshape(128, 6 * BATCH * 16)
    ins["w_tok"] = sixths(a(L0_tok_W).T)
    ins["cls"] = a(cls_tok).reshape(1, D)
    wte = a(L0_attn_wte)
    ins["wte_main"] = wte[:WCH * WROWS * 128].reshape(WCH, 128, WROWS, D)
    ins["wte_tail"] = wte[WCH * WROWS * 128:]
    ins["ln_w"] = halves(a(L0_attn_ln_w)[:, None])
    ins["wqk"] = halves(a(L0_attn_W_qk).T)
    ins["wot"] = a(L0_attn_W_o).reshape(D, H, 2, KD).transpose(3, 2, 1, 0)
    ins["wq"], ins["wk"], ins["wv"] = halves(L0_ffn_attn_q), halves(L0_ffn_attn_k), halves(L0_ffn_attn_v)
    ins["wo"] = sixths(L0_ffn_attn_o)
    ins["fw1"], ins["fw2"] = halves(L0_ffn_ffn_wi), sixths(L0_ffn_ffn_wo)
    ins["ln1"], ins["ln2"] = halves(a(L0_ffn_ln1).T), halves(a(L0_ffn_ln2).T)
    ins["ln_f"] = a(L0_ffn_ln_f).reshape(1, D)
    ins["rel_emb"] = a(L0_ffn_rel_emb)
    ins["gate_w"] = halves(L0_ffn_gate_w)
    m1 = halves(L0_ffn_moe_w1).reshape(2 * E0, KD, 2, FF)
    m2 = sixths(L0_ffn_moe_w2).reshape(2 * E0, 128, FT, D)
    ins["ew1"] = _np.concatenate([m1, halves(a(L1_ffn_w1).transpose(0, 2, 1))])
    ins["ew2"] = _np.concatenate([m2, sixths(a(L1_ffn_w2).transpose(0, 2, 1))])
    ins["eb1"] = a(L1_ffn_b1).reshape(E1, FT, 128).transpose(0, 2, 1)
    ins["a_real"], ins["a_imag"] = a(L1_attn_A_real)[:, None], a(L1_attn_A_imag)[:, None]
    ins["bt"] = halves(a(L1_attn_B).T)
    ins["ct"] = a(L1_attn_C).T
    ins["wr"] = halves(a(L1_ffn_wr).T)
    ins["b2"] = a(L1_ffn_b2)

    nc = _bacc.Bacc("TRN2", target_bir_lowering=False, num_devices=1)
    arrays, args = {}, {}
    for name, v in ins.items():
        v = _np.ascontiguousarray(v)
        arrays[f"in_{name}"] = v
        args[name] = nc.dram_tensor(f"in_{name}", v.shape, _mybir.dt.from_np(v.dtype), kind="ExternalInput").ap()
    out = nc.dram_tensor("out", [TOK, D], _mybir.dt.float32, kind="ExternalOutput").ap()
    build(nc, out=out, **args)
    r = _run(nc, [arrays], core_ids=[0])
    return r.results[0]["out"].reshape(BATCH, SEQ, D)
```

```python
from contextlib import ExitStack

import numpy as np

import concourse.bass as bass
from concourse import mybir

F32 = mybir.dt.float32
U32 = mybir.dt.uint32
BF16 = mybir.dt.bfloat16
ALU = mybir.AluOpType
ACT = mybir.ActivationFunctionType
AX = mybir.AxisListType

BATCH, SEQ, D = 32, 17, 192
TOK = BATCH * SEQ
IMGS = 7
TT = IMGS * SEQ
NT = 5
TPAD = NT * TT
LAST = TOK - (NT - 1) * TT
KD = D // 2
CH = TOK // 2
H = 12
DK = 64
HD = H * DK
FF = 768
FT = FF // 128
E0, E1 = 8, 16
LAYERS = 4
NPIX = 768
VOCAB = 50257
WROWS = 14
WCH = VOCAB // 128 // WROWS
WTAIL = VOCAB - WCH * WROWS * 128
WBUF = 4
W_PE = range(2, 5)
W_DVE = [j for j in range(WCH) if j not in W_PE]
EARLY = len(W_DVE) - 2
NEG = -1.0e30
DT = 0.01
NSTATE = 64
CAP0, CAP1 = 128, 96
CMAX = max(CAP0, CAP1)
XMAX = -(-2 * TOK // min(CAP0, CAP1)) // 2 * 2
BEYOND = 65536.0


def rows(g):
    return TT if g < NT - 1 else LAST


class Chain:

    def __init__(self, eng, sem):
        self.eng, self.sem, self.base, self.n = eng, sem, 0, 0

    def link(self, ins):
        self.n += 1
        ins.then_inc(self.sem, 1)
        self.eng.wait_ge(self.sem, self.base + self.n)


def build(nc, xst, w_tok, k2, cls, wte_main, wte_tail, ln_w, wqk, wot, causal, nreg, clsmask,
          wq, wk, wv, wo, fw1, fw2, ln1, ln2, ln_f, onehot, rel_emb, block_mask, gate_w,
          ew1, ew2, eb1, a_real, a_imag, bt, ct, wr, b2, ident, iota, tri, slots, valid, out):
    ctx = ExitStack()
    with ctx:
        def sb(name, shape, dt=F32):
            return ctx.enter_context(nc.sbuf_tensor(name, shape, dt))

        def sem(name):
            return ctx.enter_context(nc.semaphore(name))

        ps = ctx.enter_context(nc.psum_tensor("ps", [128, 8, 512], F32))

        res = sb("res", [TT, NT, D])
        hid = sb("hid", [TT, NT, D])
        xs = sb("xs", [TT, NT, D])
        xT = sb("xT", [KD, 2, TPAD])
        idn = sb("idn", [128, 128])
        mask_sb = sb("mask_sb", [TT, TT])
        biasM = sb("biasM", [TT, 12, TT])
        lnw_sb = sb("lnw_sb", [KD, 2, 1])
        ln1_sb = sb("ln1_sb", [KD, 2, LAYERS])
        ln2_sb = sb("ln2_sb", [KD, 2, LAYERS])
        lnc = [sb(f"lnc{i}", [KD, 2, 1]) for i in range(4)]
        idle = sb("idle", [TT, 1])
        act_idle = sb("act_idle", [TT, 1])
        stats = sb("stats", [TT, NT, 6])
        mv = sb("mv", [TT, NT, 2])
        rstd = sb("rstd", [TT, NT])
        mhalf = sb("mhalf", [TT, NT])
        prob = [sb(f"prob{i}", [TT, 12, TT]) for i in range(2)]
        probT = sb("probT", [TT, 12, TT])
        mx = [sb(f"mx{i}", [TT, H]) for i in range(3)]
        nmx = [sb(f"nmx{i}", [TT, H]) for i in range(3)]
        rsum = [sb(f"rsum{i}", [TT, H]) for i in range(3)]
        rinv = sb("rinv", [TT, H])
        ctxT = sb("ctxT", [128, 6, TT])
        wreg = sb("wreg", [128, 4 * 2 * HD + 2 * FT * D])

        def w_part(i, *shape):
            n = shape[1] * shape[2]
            return wreg[0:shape[0], i:i + n].rearrange("p (a b) -> p a b", a=shape[1]), i + n

        wq_sb, at = w_part(0, KD, 2, HD)
        wk_sb, at = w_part(at, KD, 2, HD)
        wv_sb, at = w_part(at, KD, 2, HD)
        wo_sb, at = w_part(at, 128, 6, D)
        fw1_sb, at = w_part(at, KD, 2, FF)
        fw2_sb, at = w_part(at, 128, FT, D)
        part, at = w_part(0, 128, len(W_DVE) + 1, D)
        wtok_sb, at = w_part(at, 128, 6, D)
        wfold, at = w_part(at, 128, 6, D)
        k2_sb, at = w_part(at, 128, 2, 256)
        big = sb("big", [128, 3, 6 * TPAD])
        qT = big[:, 0, :].rearrange("p (m t) -> p m t", m=6)
        kT = [big[:, 1 + i, :].rearrange("p (m t) -> p m t", m=6) for i in range(2)]
        xp = qT
        xstage = big[:, 1, 0:6 * BATCH * 16].rearrange("p (m b t) -> p m b t", m=6, b=BATCH)
        big2 = sb("big2", [128, WBUF * WROWS * D])
        hidden = [big2[:, i * FT * TOK:(i + 1) * FT * TOK].rearrange("p (f t) -> p f t", f=FT)
                  for i in range(2)]
        prob.append(big2[0:TT, 2 * FT * TOK:2 * FT * TOK + 12 * TT].rearrange("p (h t) -> p h t", h=12))
        wte_sb = big2[:, :].rearrange("p (s r d) -> p s r d", s=WBUF, r=WROWS)
        vbuf = sb("vbuf", [128, NT * HD])
        v_sb = vbuf[0:TT, :].rearrange("p (g n) -> p g n", g=NT)
        ering = sb("ering", [128, 2 * (2 * FF + FT * D)])
        esz = 2 * FF + FT * D
        ew1_sb = [ering[0:KD, i * esz:i * esz + 2 * FF].rearrange("p (k f) -> p k f", k=2) for i in range(2)]
        ew2_sb = [ering[:, i * esz + 2 * FF:(i + 1) * esz].rearrange("p (f d) -> p f d", f=FT)
                  for i in range(2)]
        wot_sb = ering[0:KD, 0:2 * H * D].rearrange("p (k h d) -> p k h d", k=2, h=H)
        po_sb = vbuf[0:TT, 0:H * D].rearrange("p (h d) -> p h d", h=H)
        eb1_sb = [sb(f"eb1_sb{i}", [128, FT]) for i in range(2)]
        cls_sb = sb("cls_sb", [TT, D])
        lnf_sb = sb("lnf_sb", [TT, D])
        wqk_sb = sb("wqk_sb", [KD, 2, H])
        qs = [prob_q.rearrange("p (k h t) -> p k h t", k=2, h=H) for prob_q in
              (big[0:KD, 1, 0:2 * H * TT], big[0:KD, 2, 0:2 * H * TT])]
        psum_all = sb("psum_all", [128, D])
        pool_idle = psum_all[0:TT, 0:1]
        onesv = sb("onesv", [128, TT])
        pe_sum = sb("pe_sum", [1, 2 * D])
        ones = sb("ones", [128, 128])
        avgB = sb("avgB", [KD, 2, TT])
        wsum = vbuf[0:KD, H * D:(H + 2) * D].rearrange("p (k d) -> p k d", k=2)
        nreg_sb = sb("nreg_sb", [TT, 2])
        cmask_sb = sb("cmask_sb", [TT, 1])
        oh_sb = big[0:32, 2, 0:SEQ * TT].rearrange("p (s t) -> p s t", s=SEQ)
        rel_sb = sb("rel_sb", [32, H])
        R_sb = sb("R_sb", [TT, SEQ, H])
        bmask_sb = sb("bmask_sb", [TT, CMAX])
        gw_sb = sb("gw_sb", [KD, 2, E0])
        wr_sb = sb("wr_sb", [KD, 2, E1])
        b2_sb = sb("b2_sb", [E1, D])
        iota_sb = sb("iota_sb", [TT, E1])
        logit = sb("logit", [TT, NT, E1])
        top = sb("top", [TT, NT, 8])
        idx = sb("idx", [TT, NT, 8], U32)
        idf = sb("idf", [TT, NT, 2])
        gsm = sb("gsm", [TT, 6, NT])
        cw = sb("cw", [TT, NT, E1])
        tri_sb = mask_sb
        slots_sb = bmask_sb
        valid_sb = sb("valid_sb", [TT, NT])
        asg = logit
        place = sb("place", [TT, NT, E1])
        shift = sb("shift", [TT, 2, NT])
        cnt = sb("cnt", [TT, E1])
        more = [sb(f"more{i}", [TT, 8 + E1]) for i in range(3)]
        offs = sb("offs", [TT, 2 + XMAX])
        few = sb("few", [TT, XMAX + 3])
        pairs_f = sb("pairs_f", [TT, 1])
        pairs_sb = sb("pairs_sb", [1, 1], mybir.dt.int32)
        dyn_sb = sb("dyn_sb", [1, 1], mybir.dt.int32)
        ids_sb = sb("ids_sb", [1, 2 + XMAX], mybir.dt.int32)
        flat = [prob[i][:, :, :].rearrange("p h t -> p (h t)") for i in range(2)]
        flatT = probT[:, :, :].rearrange("p h t -> p (h t)")
        upto = flatT[:, 4 * CMAX:4 * CMAX + XMAX * E1]

        def unit_views(cap):
            return (flat[0][:, 0:NT * cap].bitcast(BF16).rearrange("p (g c) -> p g c", g=NT),
                    flat[1][:, 0:NT * 2 * cap].rearrange("p (g c) -> p g c", g=NT),
                    flatT[0:KD, 0:4 * cap].rearrange("p (k c) -> p k c", k=2))

        at = 2 * FT * TOK
        rest = big2[0:TT, at:at + NT * D].rearrange("p (g d) -> p g d", g=NT)
        parts = [big2[0:TT, at + NT * D + i * NT * D // 2:at + NT * D + (i + 1) * NT * D // 2].bitcast(BF16).rearrange(
            "p (g d) -> p g d", g=NT) for i in range(3)]
        putT = [vbuf[0:CMAX, TPAD * i:TPAD * (i + 1)] for i in range(2)]
        yg = [vbuf[0:CMAX, 2 * TPAD + D * i:2 * TPAD + D * (i + 1)] for i in range(2)]
        cwT = ctxT[0:E1, :, :].rearrange("p m t -> p (m t)")[:, 0:TPAD]
        lam = sb("lam", [NSTATE, 16])
        bt_sb = sb("bt_sb", [KD, 2, NSTATE])
        ct_sb = sb("ct_sb", [NSTATE, D])
        hst = big[0:NSTATE, 0, 0:2 * TOK].rearrange("p (c t) -> p c t", c=2)

        s_in = sem("inputs_tok")
        s_const = sem("inputs_const")
        s_cn2 = sem("inputs_const2")
        s_wte = [sem(f"wte_in{i}") for i in range(WBUF)]
        s_wtail = sem("wte_tail_in")
        s_wot = sem("wot_in")
        wte_used = sem("wte_summed_dve")
        wte_used_pe = sem("wte_summed_pe")
        pe_sum_out = sem("pe_sum_out")
        zeroed = sem("zeroed")
        xp_ready = sem("xp_ready")
        fold_ready = sem("fold_ready")
        fold_out = sem("fold_out")
        tok_ready = sem("tok_ready")
        tok_out = sem("tok_out")
        n_stats = sem("norm_stats")
        n_rstd = sem("norm_rstd")
        t_stats = sem("tile_norm_stats")
        t_rstd = sem("tile_norm_rstd")
        n_scaled = sem("norm_scaled")
        n_T = sem("norm_transposed")
        n_outA = sem("norm_out_act")
        n_outD = sem("norm_out_dve")
        qs_ready = sem("qs_ready")
        a_s = sem("a_scores")
        a_masked = sem("a_masked")
        a_exp = sem("a_exp")
        a_norm = sem("a_normed")
        a_T = sem("a_probT")
        a_Tout = sem("a_probT_out")
        a_p = sem("a_p")
        a_pout = sem("a_p_out")
        a_y = sem("a_y")
        a_yout = sem("a_y_out")
        r_ready = sem("rel_ready")
        r_out = sem("rel_out")
        biasm_ready = sem("biasm_ready")
        avg_sum = sem("avg_sum")
        avg_T = sem("avg_T")
        avg_out = sem("avg_out")
        rbc_ready = sem("rbc_ready")
        zero_kv = sem("zero_kv")
        w_in = {n: sem(f"{n}_in") for n in ("wq", "wk", "wv", "wo", "f1", "f2")}
        e1_in = [sem(f"ew1_in{i}") for i in range(2)]
        e2_in = [sem(f"ew2_in{i}") for i in range(2)]
        eb_in = [sem(f"eb1_in{i}") for i in range(2)]
        gw_in = sem("gate_w_in")
        qk_ready = sem("qk_ready")
        q_out = sem("q_out")
        k_out = sem("k_out")
        v_ready = sem("v_ready")
        v_outA = sem("v_out_act")
        v_outD = sem("v_out_dve")
        s_ready = sem("s_ready")
        s_masked = sem("s_masked")
        s_max = sem("s_max")
        e_ready = sem("e_ready")
        p_ready = sem("p_ready")
        at_ready = sem("at_ready")
        at_out = sem("at_out")
        ctx_ready = sem("ctx_ready")
        ctx_out = sem("ctx_out")
        o_ready = sem("o_ready")
        o_out = sem("o_out")
        up_ready = [sem(f"up_ready{i}") for i in range(2)]
        hid_out = sem("hid_out")
        down_ready = [sem(f"down_ready{i}") for i in range(2)]
        y_out = sem("y_out")
        lg_ready = sem("logits_ready")
        lg_out = sem("logits_out")
        g_mx = sem("gate_max")
        g_exp = sem("gate_exp")
        cw_ready = sem("cw_ready")
        cwT_ready = sem("cwT_ready")
        cwT_out = sem("cwT_out")
        b2_ready = sem("b2_ready")
        asg_ready = sem("asg_ready")
        pos_ready = sem("pos_ready")
        b2_added = sem("b2_added")
        pos_out = sem("pos_out")
        pairs_ready = sem("pairs_ready")
        sched_ready = sem("sched_ready")
        x_shift = sem("x_shift")
        x_parts = sem("x_parts")
        route_in = sem("route_tables_in")
        x_pick = sem("x_pick")
        x_gather = sem("x_gather")
        x_T = sem("x_put_transposed")
        x_gout = sem("x_gather_out")
        x_Ta = sem("x_put_out_act")
        x_Td = sem("x_put_out_dve")
        x_up = sem("x_up")
        x_hout = sem("x_hidden_out")
        x_down = sem("x_down")
        x_ygout = sem("x_down_out")
        x_back = sem("x_put_back")
        x_yout = sem("x_added")
        ss_bu = sem("ss_bu")
        ss_h = sem("ss_h")
        ss_y = sem("ss_y")
        ss_yout = sem("ss_yout")
        d_chain = sem("dve_chain")
        wsum_ready = sem("wsum_ready")
        fin = sem("fin")
        s_out = sem("out_stored")

        N_CONST = 15
        SCALE = 1.0 / float(np.sqrt(np.float32(D)))
        NORM_L = 3
        NORM_F = NORM_L + LAYERS // 2

        def pos(h):
            return 6 * (h % 2) + h // 2

        def norm_bank(g, k):
            return 5 + k if g == NT - 1 else 2 * k + g % 2

        BACK = (4, 5, 6, 7, 6)

        block = ctx.enter_context(nc.Block())

        @block.sync
        def _(sp):
            sp.dma_start(wtok_sb[:, :, :], w_tok).then_inc(s_in, 16)
            sp.dma_start(k2_sb[:, :, :], k2).then_inc(s_in, 16)
            sp.dma_start(xstage.rearrange("p m b t -> p (m b t)"), xst).then_inc(s_in, 16)
            small = [(idn[:, :], ident), (cls_sb[:, :], cls.to_broadcast([TT, D])),
                     (cmask_sb[:, :], clsmask), (lnw_sb[:, :, :], ln_w), (wqk_sb[:, :, :], wqk),
                     (mask_sb[:, :], causal), (nreg_sb[:, :], nreg), (bmask_sb[:, 0:TT], block_mask),
                     (oh_sb[:, :, :], onehot), (rel_sb[:, :], rel_emb), (ln1_sb[:, :, :], ln1),
                     (ln2_sb[:, :, :], ln2), (lam[:, 0:1], a_real), (lam[:, 1:2], a_imag),
                     (iota_sb[:, :], iota)]
            assert len(small) == N_CONST
            for dst, src in small:
                sp.dma_start(dst, src).then_inc(s_const, 16)
            for j in range(WCH):
                if j == 2:
                    sp.dma_start(wot_sb, wot).then_inc(s_wot, 16)
                if j >= WBUF:
                    if j - WBUF in W_PE:
                        sp.wait_ge(wte_used_pe, W_PE.index(j - WBUF) + 1)
                    else:
                        sp.wait_ge(wte_used, W_DVE.index(j - WBUF) + 1)
                sp.dma_start(wte_sb[:, j % WBUF, :, :], wte_main[j]).then_inc(s_wte[j % WBUF], 16)
                if j == 6:
                    for dst, src in ((lnf_sb[:, :], ln_f.to_broadcast([TT, D])),
                                     (wr_sb[:, :, :], wr), (b2_sb[:, :], b2), (bt_sb[:, :, :], bt),
                                     (ct_sb[:, :], ct)):
                        sp.dma_start(dst, src).then_inc(s_cn2, 16)
            sp.wait_ge(zeroed, 2)
            sp.dma_start(part[0:WTAIL, len(W_DVE), :], wte_tail).then_inc(s_wtail, 16)
            sp.wait_ge(rbc_ready, 1)
            sp.wait_ge(biasm_ready, H)
            for dst, src in ((tri_sb[:, :], tri), (slots_sb[:, :], slots), (valid_sb[:, :], valid)):
                sp.dma_start(dst, src).then_inc(route_in, 16)

            def load_expert(e, u):
                sp.dma_start(ew1_sb[u], ew1[bass.ds(e, 1)].rearrange("a p k f -> (a p) k f")).then_inc(e1_in[u], 16)

            def load_expert2(e, u):
                sp.dma_start(eb1_sb[u][:, :], eb1[bass.ds(e, 1)].rearrange("a p f -> (a p) f")).then_inc(eb_in[u], 16)
                sp.dma_start(ew2_sb[u], ew2[bass.ds(e, 1)].rearrange("a p k f -> (a p) k f")).then_inc(e2_in[u], 16)

            def mixture(v, n_experts, first):
                static = n_experts // 2 - 2

                def load_next(i, e, u):
                    sp.wait_ge(x_up, 2 * FT * i + FT * (u + 1))
                    load_expert(e, u)
                    sp.wait_ge(x_down, 2 * i + u + 1)
                    load_expert2(e, u)

                sp.wait_ge(pairs_ready, v + 1)
                before = sp.value_load(pairs_sb[0:1, 0:1], min_val=0, max_val=2 * E0)
                for u in range(2):
                    load_expert(first + u, u)
                    load_expert2(first + u, u)
                with sp.Fori(0, static) as p:
                    for u in range(2):
                        load_next(before + p, first + 2 + 2 * p + u, u)
                sp.wait_ge(sched_ready, v + 1)
                dyn = sp.value_load(dyn_sb[0:1, 0:1], min_val=1, max_val=XMAX // 2 + 1)
                with sp.Fori(0, dyn) as p:
                    for u in range(2):
                        e = sp.value_load(ids_sb[0:1, bass.ds(2 * p + u, 1)], min_val=0, max_val=n_experts - 1)
                        load_next(before + static + p, first + e, u)

            for L in range(LAYERS):
                lp, odd = divmod(L, 2)

                def load(dst, src, arrived, used, count):
                    if L:
                        sp.wait_ge(used, count)
                    sp.dma_start(dst, src[L]).then_inc(arrived, 16)

                load(wq_sb[:, :, :], wq, w_in["wq"], qk_ready, 12 * L)
                load(wk_sb[:, :, :], wk, w_in["wk"], qk_ready, 12 * L)
                load(wv_sb[:, :, :], wv, w_in["wv"], v_ready, NT * L)
                load(wo_sb[:, :, :], wo, w_in["wo"], o_ready, NT * L)
                u, passes = (0, lp + 1) if odd else (1, lp)
                load(fw1_sb[:, :, :], fw1, w_in["f1"], up_ready[u], FT * passes)
                load(fw2_sb[:, :, :], fw2, w_in["f2"], down_ready[u], NT * passes)
                if odd:
                    if lp:
                        sp.wait_ge(lg_ready, lp)
                    sp.dma_start(gw_sb[:, :, :], gate_w[lp]).then_inc(gw_in, 16)
                    mixture(lp, E0, E0 * lp)
            mixture(LAYERS // 2, E1, 2 * E0)
            sp.wait_ge(fin, 1)
            for g in range(NT):
                sp.dma_start(out[g * TT:g * TT + rows(g), :], res[0:rows(g), g, :]).then_inc(s_out, 16)
            sp.wait_ge(s_out, 16 * NT)

        @block.gpsimd
        def _(pool):
            link = Chain(pool, wsum_ready)

            def norm_rstd(n):
                pool.wait_ge(n_stats, n + 1)
                nc.gpsimd.tensor_tensor(rstd[:, :], rstd[:, :], mhalf[:, :], ALU.pow).then_inc(n_rstd, 1)

            nc.gpsimd.memset(xp[:, :, :], 0.0).then_inc(zeroed, 1)
            nc.gpsimd.memset(part[:, len(W_DVE), :], 0.0).then_inc(zeroed, 1)
            nc.gpsimd.memset(mhalf[:, :], -0.5).then_inc(zeroed, 1)
            nc.gpsimd.memset(onesv[:, :], 1.0 / VOCAB).then_inc(zeroed, 1)
            nc.gpsimd.memset(ones[:, :], 1.0).then_inc(zeroed, 1)
            pool.wait_ge(s_in, 48)
            pool.wait_ge(zeroed, 5)
            for m in range(6):
                nc.gpsimd.tensor_copy(
                    xp[:, m, 0:TOK].rearrange("p (b s) -> p b s", s=SEQ)[:, :, 1:SEQ],
                    xstage[:, m, :, :]).then_inc(xp_ready, 1)
            norm_rstd(0)
            norm_rstd(1)
            pool.wait_ge(s_const, 16 * N_CONST)
            pool.wait_ge(xp_ready, 6)
            for g in range(NT):
                if g == 0:
                    pool.wait_ge(n_outA, NT)
                    pool.wait_ge(n_outD, NT)
                if g == 1:
                    pool.wait_ge(r_ready, 1)
                if g >= 2:
                    pool.wait_ge(a_s, g - 1)
                for k in range(2):
                    nc.gpsimd.tensor_tensor(
                        qs[g % 2][:, k, :, :],
                        xT[:, k, g * TT:(g + 1) * TT].unsqueeze(1).to_broadcast([KD, H, TT]),
                        wqk_sb[:, k, :].unsqueeze(2).to_broadcast([KD, H, TT]), ALU.mult).then_inc(qs_ready, 1)
            pool.wait_ge(r_out, 1)
            for h in range(H):
                last = nc.gpsimd.tensor_tensor(
                    biasM[:, pos(h), :].rearrange("p (b t) -> p b t", b=IMGS),
                    bmask_sb[:, 0:TT].rearrange("p (b t) -> p b t", b=IMGS),
                    R_sb[:, :, h].unsqueeze(1).to_broadcast([TT, IMGS, SEQ]), ALU.add)
                last.then_inc(biasm_ready, 1)
            pool.wait_ge(s_wot, 16)
            for h in range(1, H):
                link.link(nc.gpsimd.tensor_tensor(wsum[:, :, :], wot_sb[:, :, 0, :] if h == 1 else wsum[:, :, :],
                                                  wot_sb[:, :, h, :], ALU.add))
            pool.wait_ge(biasm_ready, H)
            pool.wait_ge(a_s, NT)
            for n, room in enumerate((kT[0][64:128, :, :], kT[1][0:64, :, :], qT[:, :, TOK:TPAD],
                                      kT[0][0:64, :, TOK:TPAD], kT[1][64:128, :, TOK:TPAD])):
                nc.gpsimd.memset(room, 0.0).then_inc(zero_kv, 1)
                pool.wait_ge(zero_kv, n + 1)
            norm_rstd(2)
            def split(v):
                nc.gpsimd.tensor_copy(parts[0], xs[:, :, :]).then_inc(x_parts, 1)
                pool.wait_ge(x_parts, 4 * v + 1)
                nc.gpsimd.tensor_tensor(rest, xs[:, :, :], parts[0], ALU.subtract).then_inc(x_parts, 1)
                pool.wait_ge(x_parts, 4 * v + 2)
                nc.gpsimd.tensor_tensor(pool_idle, mhalf[:, 0:1], mhalf[:, 0:1], ALU.add)
                nc.gpsimd.tensor_copy(parts[1], rest).then_inc(x_parts, 1)
                pool.wait_ge(x_parts, 4 * v + 3)
                nc.gpsimd.tensor_tensor(parts[2], rest, parts[1], ALU.subtract).then_inc(x_parts, 1)

            with pool.Fori(0, LAYERS // 2) as lp:
                norm_rstd(NORM_L + lp)
                for q in range(3):
                    for g in range(NT):
                        pool.wait_ge(t_stats, NT * (3 * lp + q) + g + 1)
                        nc.gpsimd.tensor_tensor(rstd[:, g:g + 1], rstd[:, g:g + 1], mhalf[:, g:g + 1],
                                                ALU.pow).then_inc(t_rstd, 1)
                pool.wait_ge(n_scaled, NT * (4 * lp + 5))
                nc.gpsimd.tensor_tensor(pool_idle, mhalf[:, 0:1], mhalf[:, 0:1], ALU.add)
                split(lp)
            for n in range(NORM_F, NORM_F + 3):
                norm_rstd(n)
            pool.wait_ge(n_scaled, NT * (3 + 2 * LAYERS))
            split(LAYERS // 2)

        @block.scalar
        def _(act):
            def norm_out(v, col=None):
                for g in range(NT):
                    act.wait_ge(n_T, NT * v + g + 1)
                    src = ps[0:KD, norm_bank(g, 0), 0:TT]
                    dst = xT[:, 0, g * TT:(g + 1) * TT]
                    if col is None:
                        nc.scalar.activation(dst, src, ACT.Copy).then_inc(n_outA, 1)
                    else:
                        nc.scalar.activation(dst, src, ACT.Copy, scale=col[:, 0, :]).then_inc(n_outA, 1)

            def exps(i, scale):
                for h in range(H):
                    last = nc.scalar.activation(prob[i][:, pos(h), :], prob[i][:, pos(h), :], ACT.Exp,
                                                bias=nmx[i][:, h:h + 1], scale=scale,
                                                accum_out=rsum[i][:, h:h + 1])
                return last

            for f in range(6):
                act.wait_ge(fold_ready, f + 1)
                nc.scalar.activation(wfold[:, f, :], ps[:, f % 4, 0:D],
                                     ACT.Copy).then_inc(fold_out, 1)
            act.wait_ge(wte_used_pe, len(W_PE))
            nc.scalar.activation(pe_sum[:, :], ps[0:1, 0, 0:2 * D], ACT.Copy).then_inc(pe_sum_out, 1)
            act.wait_ge(s_const, 16 * N_CONST)
            norm_out(0, lnw_sb)
            def project0_out(g):
                for b in range(6):
                    act.wait_ge(a_p, 6 * g + b + 1)
                    nc.scalar.activation(po_sb[:, 2 * b:2 * b + 2, :].rearrange("p h d -> p (h d)"),
                                         ps[0:TT, 6 + b % 2, 0:2 * D], ACT.Copy).then_inc(a_pout, 1)

            project0_out(0)
            act.wait_ge(a_masked, 1)
            exps(0, SCALE).then_inc(a_exp, 1)
            for g in range(NT):
                for r in range(3):
                    act.wait_ge(a_T, 3 * g + r + 1)
                    nc.scalar.activation(probT[:, 4 * r:4 * r + 4, :].rearrange("p h t -> p (h t)"),
                                         ps[0:TT, 4 + r % 2, 0:4 * TT], ACT.Copy).then_inc(a_Tout, 1)
                if g + 1 < NT:
                    act.wait_ge(a_masked, g + 2)
                    exps((g + 1) % 2, SCALE).then_inc(a_exp, 1)
                    project0_out(g + 1)
            act.wait_ge(avg_T, 1)
            nc.scalar.activation(avgB[:, :, :], ps[0:KD, 4, 0:2 * TT].rearrange("p (k t) -> p k t", k=2),
                                 ACT.Copy).then_inc(avg_out, 1)

            def hidden_out(j, u):
                for f in range(FT):
                    act.wait_ge(up_ready[u], FT * j + f + 1)
                    nc.scalar.activation(hidden[u][:, f, :].rearrange("p (c n) -> p c n", c=2),
                                         ps[:, 2 * (f % 2):2 * (f % 2) + 2, 0:CH], ACT.Relu).then_inc(hid_out, 1)

            def mixture(v, n_experts, cap, col=None):
                static = n_experts // 2 - 2
                pick, put, xg = unit_views(cap)

                def gathered(i, first=False):
                    act.wait_ge(x_gather, i + 1)
                    for k in range(2):
                        last = nc.scalar.activation(xg[:, k, :], ps[0:KD, k, 0:2 * cap], ACT.Copy,
                                                    scale=1.0 if col is None else col[:, k, :])
                    last.then_inc(x_gout, 1)
                    if not first:
                        act.wait_ge(x_back, NT * i)
                    for u in range(2):
                        last = nc.scalar.activation(putT[u][0:cap, 4 * TT:TOK], ps[0:cap, u, 256:256 + LAST], ACT.Copy)
                    last.then_inc(x_Ta, 1)

                def units(i):
                    for u in range(2):
                        act.wait_ge(eb_in[u], 16 * (i + 1))
                        for f in range(FT):
                            act.wait_ge(x_up, 2 * FT * i + FT * u + f + 1)
                            nc.scalar.activation(hidden[u][:, f, 0:cap], ps[:, 4 + f % 2, 0:cap], ACT.Gelu,
                                                 bias=eb1_sb[u][:, f:f + 1]).then_inc(x_hout, 1)
                    for u in range(2):
                        act.wait_ge(x_down, 2 * i + u + 1)
                        nc.scalar.activation(yg[u][0:cap, :], ps[0:cap, 6 + u, 0:D], ACT.Copy).then_inc(x_ygout, 1)

                before = act.value_load(pairs_sb[0:1, 0:1], min_val=0, max_val=2 * E0)
                nc.scalar.activation(act_idle[:, :], mhalf[:, 0:1], ACT.Gelu)
                gathered(before, first=True)
                with act.Fori(0, static) as p:
                    units(before + p)
                    act.wait_ge(sched_ready, v + 1)
                    gathered(before + p + 1)
                dyn = act.value_load(dyn_sb[0:1, 0:1], min_val=1, max_val=XMAX // 2 + 1)
                with act.Fori(0, dyn) as p:
                    units(before + static + p)
                    gathered(before + static + p + 1)
                units(before + static + dyn)

            act.wait_ge(zero_kv, 5)
            with act.Fori(0, LAYERS // 2) as lp:
                for odd in range(2):
                    L = 2 * lp + odd
                    norm_out(1 + 2 * L, lnc[2 * odd])
                    for m in range(6):
                        act.wait_ge(qk_ready, 12 * L + 2 * m + 1)
                        nc.scalar.activation(qT[:, m, 0:TOK].rearrange("p (c n) -> p c n", c=2),
                                             ps[:, 0:2, 0:CH], ACT.Copy).then_inc(q_out, 1)

                    def values_out(g):
                        act.wait_ge(v_ready, NT * L + g + 1)
                        nc.scalar.activation(v_sb[:, g, :].rearrange("p (c n) -> p c n", c=2),
                                             ps[0:TT, 4:6, 0:HD // 2], ACT.Copy).then_inc(v_outA, 1)

                    def softmax(g):
                        act.wait_ge(s_max, NT * L + g + 1)
                        exps(g % 3, 1.0).then_inc(e_ready, 1)

                    values_out(0)
                    for g in range(-2, NT):
                        if g == -1:
                            values_out(2)
                        if g == 0:
                            values_out(4)
                            softmax(2)
                        if g >= 0:
                            act.wait_ge(ctx_ready, NT * L + g + 1)
                            if g >= 1:
                                act.wait_ge(o_ready, NT * L + g)
                            nc.scalar.activation(
                                ctxT[:, :, :].rearrange("p m t -> p (m t)")[:, 0:4 * TT], ps[:, 6, 0:4 * TT],
                                ACT.Copy)
                            nc.scalar.activation(
                                ctxT[:, :, :].rearrange("p m t -> p (m t)")[:, 4 * TT:], ps[:, 7, 0:2 * TT],
                                ACT.Copy).then_inc(ctx_out, 1)
                        if g + 2 < NT and g != 0:
                            softmax(g + 2)
                    norm_out(2 + 2 * L, lnc[2 * odd + 1])
                    if odd:
                        act.wait_ge(g_mx, lp + 1)
                        nc.scalar.activation(gsm[:, 1, :], gsm[:, 0, :], ACT.Exp).then_inc(g_exp, 1)
                    if odd:
                        act.wait_ge(pairs_ready, lp + 1)
                    hidden_out(lp, odd)
                mixture(lp, E0, CAP0, lnc[3])
            norm_out(1 + 2 * LAYERS)
            norm_out(2 + 2 * LAYERS)
            act.wait_ge(pairs_ready, LAYERS // 2 + 1)
            act.wait_ge(g_mx, LAYERS // 2 + 1)
            for g in range(NT):
                nc.scalar.activation(cw[:, g, :], logit[:, g, :], ACT.Exp, bias=gsm[:, 0, g:g + 1],
                                     accum_out=gsm[:, 1, g:g + 1]).then_inc(g_exp, 1)
            act.wait_ge(cwT_ready, NT)
            nc.scalar.activation(cwT[:, 0:4 * TT], ps[0:E1, 2, 0:4 * TT], ACT.Copy).then_inc(cwT_out, 1)
            nc.scalar.activation(cwT[:, 4 * TT:], ps[0:E1, 3, 0:TT], ACT.Copy).then_inc(cwT_out, 1)
            mixture(LAYERS // 2, E1, CAP1)

        @block.vector
        def _(dve):
            chain = Chain(dve, d_chain)
            link = chain.link
            V = nc.vector

            def layer_norm(n, src, dst, eps, signal):
                for g in range(NT):
                    last = V.bn_stats(stats[:, g, :], src[:, g, :])
                link(last)
                for g in range(NT):
                    last = V.bn_aggr(mv[:, g, :], stats[:, g, :])
                link(last)
                V.tensor_scalar(rstd[:, :], mv[:, :, 1], eps, None, ALU.add).then_inc(n_stats, 1)
                dve.wait_ge(n_rstd, n + 1)
                for g in range(NT):
                    ins = V.tensor_scalar(dst[:, g, :], src[:, g, :], mv[:, g, 0:1], rstd[:, g:g + 1],
                                          ALU.subtract, ALU.mult)
                    if signal:
                        ins.then_inc(n_scaled, 1)
                    elif g == NT - 1:
                        link(ins)

            def mean_square(src, dst, g):
                return V.tensor_tensor_reduce(out=dst[:, g, :], in0=src[:, g, :], in1=src[:, g, :], scale=1.0 / D,
                                              scalar=1e-6, op0=ALU.mult, op1=ALU.add, accum_out=rstd[:, g:g + 1])

            def tile_stats(g):
                mean_square(hid, xs, g).then_inc(t_stats, 1)

            def tile_scale(q, g):
                dve.wait_ge(t_rstd, NT * q + g + 1)
                V.tensor_scalar(xs[:, g, :], hid[:, g, :], rstd[:, g:g + 1], None, ALU.mult).then_inc(n_scaled, 1)

            def t5_norm(n, src, dst):
                for g in range(NT):
                    last = mean_square(src, dst, g)
                last.then_inc(n_stats, 1)
                dve.wait_ge(n_rstd, n + 1)
                for g in range(NT):
                    V.tensor_scalar(dst[:, g, :], src[:, g, :], rstd[:, g:g + 1], None, ALU.mult).then_inc(n_scaled, 1)

            def norm_out(v, col=None, tiles=range(NT)):
                for g in tiles:
                    dve.wait_ge(n_T, NT * v + g + 1)
                    src = ps[0:KD, norm_bank(g, 1), 0:TT]
                    dst = xT[:, 1, g * TT:(g + 1) * TT]
                    if col is None:
                        V.tensor_copy(dst, src).then_inc(n_outD, 1)
                    else:
                        V.tensor_scalar(dst, src, col[:, 1, :], None, ALU.mult).then_inc(n_outD, 1)

            for m in more:
                V.memset(m[:, 0:8], 0.0)
            V.memset(offs[:, 0:2], 0.0)
            link(V.memset(pairs_f[:, :], 0.0))
            V.tensor_copy(pairs_sb[:, :], pairs_f[0:1, :]).then_inc(pairs_ready, 1)
            for g in range(NT):
                V.memset(few[:, g:g + 1], 0.0).then_inc(x_yout, 1)
            dve.wait_ge(pairs_ready, 1)
            dve.wait_ge(s_const, 16 * N_CONST)
            c = lambda i: lam[:, i:i + 1]
            link(V.tensor_scalar(c(2), c(0), -DT / 2, 1.0, ALU.mult, ALU.add))
            link(V.tensor_scalar(c(3), c(0), DT / 2, 1.0, ALU.mult, ALU.add))
            link(V.tensor_scalar(c(4), c(1), DT / 2, None, ALU.mult))
            link(V.tensor_tensor(c(5), c(2), c(2), ALU.mult))
            link(V.tensor_tensor(c(6), c(4), c(4), ALU.mult))
            link(V.tensor_tensor(c(5), c(5), c(6), ALU.add))
            link(V.reciprocal(c(6), c(5)))
            link(V.tensor_tensor(c(7), c(2), c(6), ALU.mult))
            link(V.tensor_tensor(c(8), c(4), c(6), ALU.mult))
            link(V.tensor_tensor(c(9), c(3), c(7), ALU.mult))
            link(V.tensor_tensor(c(10), c(4), c(8), ALU.mult))
            link(V.tensor_tensor(c(9), c(9), c(10), ALU.subtract))
            link(V.tensor_tensor(c(10), c(3), c(8), ALU.mult))
            link(V.tensor_tensor(c(11), c(4), c(7), ALU.mult))
            link(V.tensor_tensor(c(10), c(10), c(11), ALU.add))
            link(V.tensor_scalar(c(11), c(10), -1.0, None, ALU.mult))
            rt = float(np.sqrt(np.float32(DT)))
            link(V.tensor_scalar(c(12), c(7), rt, None, ALU.mult))
            link(V.tensor_scalar(c(13), c(8), rt, None, ALU.mult))
            def sum_wte(j):
                dve.wait_ge(s_wte[j % WBUF], 16 * (j // WBUF + 1))
                V.tensor_reduce(part[:, W_DVE.index(j), :], wte_sb[:, j % WBUF, :, :].rearrange("p r d -> p d r"),
                                AX.X, ALU.add).then_inc(wte_used, 1)

            for j in W_DVE[:2]:
                sum_wte(j)
            for g in range(NT):
                dve.wait_ge(tok_ready, g + 1)
                V.scalar_tensor_tensor(
                    out=res[:, g, :], in0=cls_sb[:, :], scalar=cmask_sb[:, 0:1],
                    in1=ps[0:TT, 4 + g % 4, 0:D], op0=ALU.mult, op1=ALU.add).then_inc(tok_out, 1)
            dve.wait_ge(tok_out, NT)
            layer_norm(0, res, xs, 1e-5, False)
            layer_norm(1, xs, xs, 1e-5, True)
            norm_out(0, lnw_sb)
            dve.wait_ge(r_ready, 1)
            V.tensor_copy(R_sb[:, :, :].rearrange("p t h -> p (t h)"), ps[0:TT, 7, 0:SEQ * H]).then_inc(r_out, 1)

            def masked_max0(g):
                i = g % 2
                dve.wait_ge(a_s, g + 1)
                if g >= 2:
                    dve.wait_ge(a_T, 3 * (g - 1))
                link(V.tensor_tensor(
                    prob[i][:, :, :].rearrange("p (c h) t -> p c h t", c=4),
                    ps[0:TT, 0:4, 0:3 * TT].rearrange("p c (h t) -> p c h t", h=3),
                    mask_sb[:, :].unsqueeze(1).unsqueeze(1).to_broadcast([TT, 4, 3, TT]), ALU.add))
                link(V.tensor_reduce(mx[i][:, :].rearrange("p (h c) -> p c h", c=2),
                                     prob[i][:, :, :].rearrange("p (c h) t -> p c h t", c=2), AX.X, ALU.max))
                V.tensor_scalar(nmx[i][:, :], mx[i][:, :], -SCALE, None, ALU.mult).then_inc(a_masked, 1)

            for j in W_DVE[2:7]:
                sum_wte(j)
            later = iter(W_DVE[7:])
            masked_max0(0)
            for g in range(NT):
                i = g % 2
                sum_wte(next(later))
                dve.wait_ge(a_exp, g + 1)
                link(V.reciprocal(rinv[:, :], rsum[i][:, :]))
                link(V.tensor_scalar(rinv[:, :], rinv[:, :], nreg_sb[:, 0:1], None, ALU.mult))
                V.tensor_tensor(prob[i][:, :, :].rearrange("p (c h) t -> p c h t", c=2),
                                prob[i][:, :, :].rearrange("p (c h) t -> p c h t", c=2),
                                rinv[:, :].rearrange("p (h c) -> p c h", c=2).unsqueeze(3).to_broadcast([TT, 2, 6, TT]),
                                ALU.mult).then_inc(a_norm, 1)
                sum_wte(next(later))
                if g + 1 < NT:
                    masked_max0(g + 1)
                    sum_wte(next(later))
                    sum_wte(next(later))
                if g == NT - 1:
                    dve.wait_ge(wte_used, EARLY)
                    link(V.tensor_reduce(psum_all[:, :], part[:, 0:EARLY, :].rearrange("p j d -> p d j"), AX.X, ALU.add))
                dve.wait_ge(a_y, g + 1)
                V.tensor_tensor(res[:, g, :], res[:, g, :], ps[0:TT, 5, 0:D], ALU.add).then_inc(a_yout, 1)
            assert next(later, None) is None
            dve.wait_ge(wte_used, len(W_DVE))
            dve.wait_ge(s_wtail, 16)
            link(V.tensor_reduce(part[:, 0, :], part[:, EARLY:, :].rearrange("p j d -> p d j"), AX.X, ALU.add))
            link(V.tensor_tensor(psum_all[:, :], psum_all[:, :], part[:, 0, :], ALU.add))
            dve.wait_ge(pe_sum_out, 1)
            link(V.tensor_tensor(psum_all[0:1, :], psum_all[0:1, :], pe_sum[:, 0:D], ALU.add))
            V.tensor_tensor(psum_all[0:1, :], psum_all[0:1, :], pe_sum[:, D:2 * D], ALU.add).then_inc(avg_sum, 1)
            dve.wait_ge(rbc_ready, 1)
            dve.wait_ge(a_yout, NT)
            for g in range(NT):
                last = V.scalar_tensor_tensor(out=res[:, g, :], in0=ps[0:TT, 5, 0:D], scalar=nreg_sb[:, 1:2],
                                              in1=res[:, g, :], op0=ALU.mult, op1=ALU.add)
            link(last)
            layer_norm(2, res, hid, 1e-5, False)
            dve.wait_ge(biasm_ready, H)
            dve.wait_ge(zero_kv, 5)

            def gate_weights(v, width):
                both = (place[:, :, 0:width], cw[:, :, 0:width])
                for k in range(2):
                    last = V.tensor_tensor(both[k], iota_sb[:, 0:width].unsqueeze(1).to_broadcast([TT, NT, width]),
                                           idf[:, :, k].unsqueeze(2).to_broadcast([TT, NT, width]), ALU.is_equal)
                link(last)
                for k in range(2):
                    last = V.tensor_tensor(both[k], both[k], gsm[:, 2 + k, :].unsqueeze(2).to_broadcast([TT, NT, width]),
                                           ALU.mult)
                link(last)
                V.tensor_tensor(both[1], both[1], both[0], ALU.add).then_inc(cw_ready, 1)
                dve.wait_ge(cw_ready, v + 1)

            def top2(src, width):
                V.memset(idle[:, :], 0.0)
                for g in range(NT):
                    last = V.max(top[:, g, :], src[:, g, 0:width])
                link(last)
                V.memset(idle[:, :], 0.0)
                for g in range(NT):
                    last = V.max_index(idx[:, g, :], top[:, g, :], src[:, g, 0:width])
                link(last)
                link(V.tensor_copy(idf[:, :, :], idx[:, :, 0:2]))

            def places(v, n_experts, bank):
                dve.wait_ge(route_in, 16 * 3)
                V.scalar_tensor_tensor(out=asg[:, :, 0:n_experts], in0=cw[:, :, 0:n_experts], scalar=0.0,
                                       in1=valid_sb[:, :].unsqueeze(2).to_broadcast([TT, NT, n_experts]),
                                       op0=ALU.is_gt, op1=ALU.mult).then_inc(asg_ready, 1)
                dve.wait_ge(pos_ready, v + 1)
                V.tensor_copy(cnt[:, 0:n_experts], ps[0:TT, bank, NT * n_experts:(NT + 1) * n_experts])
                V.scalar_tensor_tensor(
                    out=place[:, :, 0:n_experts],
                    in0=ps[0:TT, bank, 0:NT * n_experts].rearrange("p (g e) -> p g e", g=NT),
                    scalar=1.0, in1=asg[:, :, 0:n_experts], op0=ALU.add, op1=ALU.mult).then_inc(pos_out, 1)
                dve.wait_ge(pos_out, v + 1)
                V.memset(idle[:, :], 0.0)

            def schedule(v, n_experts, cap):
                n = n_experts
                x = more[0][:, 8:8 + n]
                link(V.memset(x, 0.0))
                for m in range(1, -(-TOK // cap)):
                    link(V.scalar_tensor_tensor(out=x, in0=cnt[:, 0:n], scalar=float(m * cap), in1=x,
                                                op0=ALU.is_gt, op1=ALU.add))
                src, dst, step = more[0], more[1], 1
                while step < n:
                    link(V.tensor_tensor(dst[:, 8:8 + n], src[:, 8:8 + n], src[:, 8 - step:8 - step + n], ALU.add))
                    src, dst, step = dst, more[2] if dst is more[1] else more[1], 2 * step
                total = src[:, 8 + n - 1:8 + n]
                both = [few[:, 0:XMAX], offs[:, 2:2 + XMAX]]
                u_e = upto[:, 0:XMAX * n].rearrange("p (j e) -> p j e", e=n)
                link(V.tensor_tensor(u_e, iota_sb[:, 0:XMAX].unsqueeze(2).to_broadcast([TT, XMAX, n]),
                                     src[:, 8:8 + n].unsqueeze(1).to_broadcast([TT, XMAX, n]), ALU.is_ge))
                link(V.tensor_reduce(both[0], u_e, AX.X, ALU.add))
                link(V.tensor_tensor(u_e, u_e, x.unsqueeze(1).to_broadcast([TT, XMAX, n]), ALU.mult))
                link(V.tensor_reduce(both[1], u_e, AX.X, ALU.add))
                link(V.scalar_tensor_tensor(out=both[1], in0=both[1], scalar=-1.0, in1=iota_sb[:, 0:XMAX],
                                            op0=ALU.mult, op1=ALU.add))
                link(V.tensor_scalar(both[1], both[1], float(cap), float(cap), ALU.mult, ALU.add))
                V.tensor_scalar(ids_sb[0:1, 2:2 + XMAX], both[0][0:1, :], float(n - 1), None, ALU.min)
                link(V.tensor_copy(ids_sb[0:1, 0:2], iota_sb[0:1, n - 2:n]))
                link(V.tensor_scalar(both[0], both[0], float(n), BEYOND, ALU.is_ge, ALU.mult))
                V.tensor_tensor(both[1], both[1], both[0], ALU.add)
                link(V.tensor_scalar(upto[:, 0:XMAX // 2], iota_sb[:, 0:XMAX // 2], 2.0, total, ALU.mult, ALU.is_lt))
                link(V.tensor_reduce(few[:, XMAX:XMAX + 1], upto[:, 0:XMAX // 2], AX.X, ALU.add))
                link(V.scalar_tensor_tensor(out=pairs_f[:, :], in0=few[:, XMAX:XMAX + 1], scalar=float(n // 2),
                                            in1=pairs_f[:, :], op0=ALU.add, op1=ALU.add))
                V.tensor_scalar(dyn_sb[:, :], few[0:1, XMAX:XMAX + 1], 1.0, None, ALU.add).then_inc(sched_ready, 1)
                dve.wait_ge(sched_ready, v + 1)

            def schedule_links(n_experts, cap):
                return 1 + (-(-TOK // cap) - 1) + (n_experts - 1).bit_length() + 11

            def one_hots(cap, i, experts, off):
                pick, put, _ = unit_views(cap)
                for u in range(2):
                    e = experts(u)
                    V.tensor_scalar(shift[:, u, :], place[:, :, e].rearrange("p g e -> p (g e)"), off(u), None,
                                    ALU.subtract).then_inc(x_shift, 1)
                    dve.wait_ge(x_shift, 2 * i + u + 1)
                    for g in range(NT):
                        V.tensor_scalar(pick[:, g, u * cap:(u + 1) * cap], slots_sb[:, 0:cap], shift[:, u, g:g + 1],
                                        None, ALU.is_equal)
                        last = V.tensor_scalar(put[:, g, u * cap:(u + 1) * cap], slots_sb[:, 0:cap],
                                               shift[:, u, g:g + 1], cw[:, g, e], ALU.is_equal, ALU.mult)
                last.then_inc(x_pick, 1)

            def put_out(cap, i, first=False):
                dve.wait_ge(x_T, i + 1)
                if not first:
                    dve.wait_ge(x_back, NT * i)
                for u in range(2):
                    last = V.tensor_copy(putT[u][0:cap, 0:4 * TT], ps[0:cap, 2 + u, 0:4 * TT])
                last.then_inc(x_Td, 1)

            def add_back(i, dst):
                dve.wait_ge(x_yout, NT * (i + 1))
                for g in range(NT):
                    dve.wait_ge(x_back, NT * i + g + 1)
                    r = rows(g)
                    V.tensor_tensor(dst[0:r, g, :], dst[0:r, g, :], ps[0:r, BACK[g], 0:D], ALU.add).then_inc(x_yout, 1)

            def mixture(v, n_experts, cap, dst, before):
                static = n_experts // 2 - 2
                put_out(cap, before, first=True)
                with dve.Fori(0, static) as p:
                    i = before + p
                    one_hots(cap, i + 1, lambda u: bass.ds(2 * p + 2 + u, 1), lambda u: 0.0)
                    add_back(i, dst)
                    put_out(cap, i + 1)
                dyn = dve.value_load(dyn_sb[0:1, 0:1], min_val=1, max_val=XMAX // 2 + 1)
                with dve.Fori(0, dyn) as p:
                    i = before + static + p

                    def listed(u):
                        return bass.ds(dve.value_load(ids_sb[0:1, bass.ds(2 * p + u, 1)], min_val=0,
                                                      max_val=n_experts - 1), 1)

                    one_hots(cap, i + 1, listed, lambda u: offs[:, bass.ds(2 * p + u, 1)])
                    add_back(i, dst)
                    put_out(cap, i + 1)
                last = before + static + dyn
                add_back(last, dst)
                V.memset(idle[:, :], 0.0)
                dve.wait_ge(x_yout, NT * (last + 2))
                V.tensor_copy(pairs_sb[:, :], pairs_f[0:1, :]).then_inc(pairs_ready, 1)
                dve.wait_ge(pairs_ready, v + 2)
                V.memset(idle[:, :], 0.0)

            def first_pair(cap):
                before = dve.value_load(pairs_sb[0:1, 0:1], min_val=0, max_val=2 * E0)
                one_hots(cap, before, lambda u: slice(u, u + 1), lambda u: 0.0)
                return before

            def layer(lp, odd, base, per):
                L = 2 * lp + odd
                chain.base, chain.n = base, 0
                if not odd:
                    for w, src in enumerate((ln1_sb, ln2_sb)):
                        for o in range(2):
                            last = V.tensor_copy(lnc[2 * o + w][:, :, :], src[:, :, bass.ds(L + o, 1)])
                    link(last)
                if not odd:
                    t5_norm(NORM_L + lp, hid, xs)
                norm_out(1 + 2 * L, lnc[2 * odd])
                for m in range(6):
                    dve.wait_ge(qk_ready, 12 * L + 2 * m + 2)
                    V.tensor_copy(kT[0][0:64, m, 0:TOK].rearrange("p (c n) -> p c n", c=2), ps[0:64, 2:4, 0:CH])
                    V.tensor_copy(kT[1][64:128, m, 0:TOK].rearrange("p (c n) -> p c n", c=2),
                                  ps[64:128, 2:4, 0:CH]).then_inc(k_out, 1)

                def values_out(g):
                    dve.wait_ge(v_ready, NT * L + g + 1)
                    V.tensor_copy(v_sb[:, g, :].rearrange("p (c n) -> p c n", c=2),
                                  ps[0:TT, 6:8, 0:HD // 2]).then_inc(v_outD, 1)

                def masked_max(g, between=None):
                    i = g % 3
                    dve.wait_ge(s_ready, NT * L + g + 1)
                    ins = V.tensor_tensor(
                        prob[i][:, :, :].rearrange("p (c h) t -> p c (h t)", c=4), ps[0:TT, 0:4, 0:3 * TT],
                        biasM[:, :, :].rearrange("p (c h) t -> p c (h t)", c=4), ALU.add)
                    ins.then_inc(s_masked, 1)
                    if between is not None:
                        between()
                    dve.wait_ge(s_masked, NT * L + g + 1)
                    link(V.tensor_reduce(mx[i][:, :].rearrange("p (h c) -> p c h", c=2),
                                         prob[i][:, :, :].rearrange("p (c h) t -> p c h t", c=2), AX.X, ALU.max))
                    V.tensor_scalar(nmx[i][:, :], mx[i][:, :], -1.0, None, ALU.mult).then_inc(s_max, 1)

                def add_o(g):
                    dve.wait_ge(o_ready, NT * L + g + 1)
                    V.tensor_tensor(hid[:, g, :], hid[:, g, :], ps[0:TT, 7, 0:D], ALU.add).then_inc(o_out, 1)
                    dve.wait_ge(o_out, NT * L + g + 1)

                def normalise(g):
                    i = g % 3
                    dve.wait_ge(e_ready, NT * L + g + 1)
                    link(V.reciprocal(rinv[:, :], rsum[i][:, :]))
                    V.tensor_tensor(prob[i][:, :, :].rearrange("p (c h) t -> p c h t", c=2),
                                    prob[i][:, :, :].rearrange("p (c h) t -> p c h t", c=2),
                                    rinv[:, :].rearrange("p (h c) -> p c h", c=2).unsqueeze(3).to_broadcast([TT, 2, 6, TT]),
                                    ALU.mult).then_inc(p_ready, 1)

                masked_max(0)
                masked_max(1)
                values_out(1)
                normalise(0)
                values_out(3)
                masked_max(2)
                for g in range(NT):
                    for r in range(3):
                        dve.wait_ge(at_ready, 3 * (NT * L + g) + r + 1)
                        V.tensor_copy(probT[:, 4 * r:4 * r + 4, :].rearrange("p h t -> p (h t)"),
                                      ps[0:TT, 4 + (15 * odd + 3 * g + r) % 2, 0:4 * TT]).then_inc(at_out, 1)
                    def add_before():
                        if g >= 1:
                            add_o(g - 1)
                            tile_stats(g - 1)

                    if 0 < g < NT - 2:
                        masked_max(g + 2, add_before)
                    if g + 1 < NT:
                        normalise(g + 1)
                    if g + 2 >= NT:
                        add_before()
                    if g >= 2:
                        tile_scale(3 * lp + 2 * odd, g - 2)
                norm_out(2 + 2 * L, lnc[2 * odd + 1], range(1))
                tile_scale(3 * lp + 2 * odd, NT - 2)
                norm_out(2 + 2 * L, lnc[2 * odd + 1], range(1, 2))
                add_o(NT - 1)
                tile_stats(NT - 1)
                norm_out(2 + 2 * L, lnc[2 * odd + 1], range(2, 3))
                tile_scale(3 * lp + 2 * odd, NT - 1)
                norm_out(2 + 2 * L, lnc[2 * odd + 1], range(3, NT))
                if odd:
                    dve.wait_ge(lg_ready, lp + 1)
                    V.tensor_copy(logit[:, :, 0:E0], ps[0:TT, 7, 0:NT * E0].rearrange(
                        "p (g e) -> p g e", g=NT)).then_inc(lg_out, 1)
                    dve.wait_ge(lg_out, lp + 1)
                    top2(logit, E0)
                    V.tensor_tensor(gsm[:, 0, :], top[:, :, 1], top[:, :, 0], ALU.subtract).then_inc(g_mx, 1)
                    dve.wait_ge(g_exp, lp + 1)
                    link(V.tensor_scalar(gsm[:, 4, :], gsm[:, 1, :], 1.0, None, ALU.add))
                    link(V.reciprocal(gsm[:, 2, :], gsm[:, 4, :]))
                    link(V.tensor_tensor(gsm[:, 3, :], gsm[:, 1, :], gsm[:, 2, :], ALU.mult))
                    gate_weights(lp, E0)
                    places(lp, E0, 7)
                    before = first_pair(CAP0)
                add_ffn(L, lp, odd, 3 * lp + 1)
                if odd:
                    schedule(lp, E0, CAP0)
                    dve.wait_ge(y_out, NT * (L + 1))
                    mixture(lp, E0, CAP0, hid, before)
                assert chain.n == per, (odd, chain.n)

            def add_ffn(t, j, u, q):
                for g in range(NT):
                    dve.wait_ge(down_ready[u], NT * j + g + 1)
                    r = rows(g)
                    V.tensor_tensor(hid[0:r, g, :], hid[0:r, g, :], ps[0:r, 4 + g % 4, 0:D], ALU.add).then_inc(y_out, 1)
                    if u == 0:
                        dve.wait_ge(y_out, NT * t + g + 1)
                        tile_stats(g)
                        if g >= 1:
                            tile_scale(q, g - 1)
                if u == 0:
                    tile_scale(q, NT - 1)
                V.memset(idle[:, :], 0.0)

            base = chain.n
            PER = [1 + NT + NT, NT + NT + 3 + 3 + 2 + schedule_links(E0, CAP0)]
            with dve.Fori(0, LAYERS // 2) as lp:
                for odd in range(2):
                    layer(lp, odd, base + (PER[0] + PER[1]) * lp + PER[0] * odd, PER[odd])
            chain.base, chain.n = 0, base + (PER[0] + PER[1]) * (LAYERS // 2)
            dve.wait_ge(s_cn2, 16 * 5)
            for g in range(NT):
                last = mean_square(hid, xs, g)
            last.then_inc(n_stats, 1)
            dve.wait_ge(n_rstd, NORM_F + 1)
            for g in range(NT):
                last = V.scalar_tensor_tensor(out=xs[:, g, :], in0=hid[:, g, :], scalar=rstd[:, g:g + 1],
                                              in1=lnf_sb[:, :], op0=ALU.mult, op1=ALU.mult)
            link(last)
            for g in range(NT):
                last = V.tensor_tensor(res[:, g, :], res[:, g, :], xs[:, g, :], ALU.add)
            link(last)
            layer_norm(NORM_F + 1, res, xs, 1e-5, True)
            norm_out(1 + 2 * LAYERS)
            dve.wait_ge(ss_bu, 1)
            for k in range(2):
                last = V.tensor_scalar(hst[:, k, :].rearrange("p (c n) -> p c n", c=2), ps[0:NSTATE, 0:2, 0:CH],
                                       c(12 + k), None, ALU.mult)
            link(last)
            hv = hst.rearrange("p c (b s) -> p c b s", s=SEQ)
            for t in range(1, SEQ):
                link(V.scalar_tensor_tensor(out=hv[:, :, :, t], in0=hv[:, :, :, t - 1], scalar=c(9),
                                            in1=hv[:, :, :, t], op0=ALU.mult, op1=ALU.add))
                V.scalar_tensor_tensor(out=hv[:, 0, :, t], in0=hv[:, 1, :, t - 1], scalar=c(11),
                                       in1=hv[:, 0, :, t], op0=ALU.mult, op1=ALU.add)
                link(V.scalar_tensor_tensor(out=hv[:, 1, :, t], in0=hv[:, 0, :, t - 1], scalar=c(10),
                                            in1=hv[:, 1, :, t], op0=ALU.mult, op1=ALU.add))
            V.tensor_copy(lam[:, 14:15], lam[:, 13:14]).then_inc(ss_h, 1)
            for g in range(NT):
                dve.wait_ge(ss_y, g + 1)
                r = rows(g)
                V.tensor_tensor(res[0:r, g, :], res[0:r, g, :],
                                ps[0:r, 4 + g % 4, 0:D], ALU.add).then_inc(ss_yout, 1)
            dve.wait_ge(ss_yout, NT)
            layer_norm(NORM_F + 2, res, xs, 1e-5, True)
            norm_out(2 + 2 * LAYERS)
            dve.wait_ge(n_scaled, NT * (3 + 2 * LAYERS))
            for g in range(NT):
                last = V.tensor_tensor(res[:, g, :], res[:, g, :], xs[:, g, :], ALU.add)
            link(last)
            dve.wait_ge(lg_ready, LAYERS // 2 + 1)
            link(V.tensor_copy(logit[:, :, :], ps[0:TT, 0, 0:NT * E1].rearrange("p (g e) -> p g e", g=NT)))
            link(V.tensor_reduce(gsm[:, 5, :], logit[:, :, :], AX.X, ALU.max))
            V.tensor_scalar(gsm[:, 0, :], gsm[:, 5, :], -1.0, None, ALU.mult).then_inc(g_mx, 1)
            dve.wait_ge(g_exp, LAYERS // 2 + NT)
            link(V.reciprocal(gsm[:, 4, :], gsm[:, 1, :]))
            link(V.tensor_tensor(logit[:, :, :], cw[:, :, :],
                                 gsm[:, 4, :].unsqueeze(2).to_broadcast([TT, NT, E1]), ALU.mult))
            top2(logit, E1)
            for k in range(2):
                last = V.tensor_copy(gsm[:, 2 + k, :], top[:, :, k])
            link(last)
            gate_weights(LAYERS // 2, E1)
            places(LAYERS // 2, E1, 1)
            before = first_pair(CAP1)
            for g in range(NT):
                dve.wait_ge(b2_ready, g + 1)
                r = rows(g)
                V.tensor_tensor(res[0:r, g, :], res[0:r, g, :], ps[0:r, 4 + g % 4, 0:D], ALU.add).then_inc(b2_added, 1)
            dve.wait_ge(b2_added, NT)
            schedule(LAYERS // 2, E1, CAP1)
            mixture(LAYERS // 2, E1, CAP1, res, before)
            V.tensor_copy(lam[:, 14:15], lam[:, 13:14]).then_inc(fin, 1)

        @block.tensor
        def _(pe):
            T = nc.tensor

            def slot(g, n=TT):
                return ps[0:n, 4 + g % 4, 0:D]

            def tile(g, r=TT):
                return slice(g * TT, g * TT + r)

            def norm_transposes(v, tiles=range(NT)):
                for g in tiles:
                    pe.wait_ge(n_scaled, NT * v + g + 1)
                    if 2 <= g < NT - 1:
                        pe.wait_ge(n_outA, NT * v + g - 1)
                        pe.wait_ge(n_outD, NT * v + g - 1)
                    for k in range(2):
                        last = T.transpose(ps[0:KD, norm_bank(g, k), 0:TT],
                                           xs[:, g, k * KD:(k + 1) * KD], idn[0:TT, 0:TT])
                    last.then_inc(n_T, 1)

            def normed(v, tiles=NT):
                pe.wait_ge(n_outA, NT * v + tiles)
                pe.wait_ge(n_outD, NT * v + tiles)

            pe.wait_ge(s_in, 48)
            for f in range(6):
                if f >= 4:
                    pe.wait_ge(fold_out, f - 3)
                for i in range(2):
                    last = T.matmul(ps[:, f % 4, 0:D],
                                    k2_sb[:, i, (f % 2) * 128:(f % 2) * 128 + 128], wtok_sb[:, 2 * (f // 2) + i, :],
                                    start=(i == 0), stop=(i == 1))
                last.then_inc(fold_ready, 1)
            pe.wait_ge(fold_out, 6)
            pe.wait_ge(xp_ready, 6)
            pe.wait_ge(zeroed, 5)
            for g in range(NT):
                if g == NT - 1:
                    pe.wait_ge(tok_out, 1)
                for k in range(6):
                    last = T.matmul(slot(g), xp[:, k, tile(g)], wfold[:, k, :], start=(k == 0), stop=(k == 5))
                last.then_inc(tok_ready, 1)
            for j in W_PE:
                pe.wait_ge(s_wte[j % WBUF], 16 * (j // WBUF + 1))
                for row in range(0, WROWS, 2):
                    last = T.matmul(ps[:, 0, 0:2 * D], ones[:, :],
                                    wte_sb[:, j % WBUF, row:row + 2, :].rearrange("p r d -> p (r d)"),
                                    start=(j == W_PE[0] and row == 0), stop=(j == W_PE[-1] and row == WROWS - 2))
                last.then_inc(wte_used_pe, 1)
            pe.wait_ge(s_const, 16 * N_CONST)
            pe.wait_ge(pe_sum_out, 1)
            norm_transposes(0)
            normed(0)
            for t in range(SEQ):
                last = T.matmul(ps[0:TT, 7, t * H:(t + 1) * H], oh_sb[:, t, :], rel_sb[:, :], start=True, stop=True)
            last.then_inc(r_ready, 1)
            def scores(g):
                pe.wait_ge(qs_ready, 2 * (g + 1))
                if g >= 1:
                    pe.wait_ge(a_masked, g)
                for h in range(H):
                    p = pos(h)
                    for k in range(2):
                        last = T.matmul(ps[0:TT, p // 3, (p % 3) * TT:(p % 3 + 1) * TT], qs[g % 2][:, k, h, :],
                                        qs[g % 2][:, k, h, :], start=(k == 0), stop=(k == 1))
                last.then_inc(a_s, 1)

            def project0(g):
                for b in range(6):
                    n = 6 * g + b
                    if n >= 2:
                        pe.wait_ge(a_pout, n - 1)
                    for k in range(2):
                        last = T.matmul(ps[0:TT, 6 + b % 2, 0:2 * D], xT[:, k, tile(g)],
                                        wot_sb[:, k, 2 * b:2 * b + 2, :].rearrange("p h d -> p (h d)"),
                                        start=(k == 0), stop=(k == 1))
                    last.then_inc(a_p, 1)

            pe.wait_ge(s_wot, 16)
            pe.wait_ge(r_out, 1)
            project0(0)
            scores(0)
            for g in range(NT):
                if g + 1 < NT:
                    scores(g + 1)
                pe.wait_ge(a_norm, g + 1)
                for r in range(3):
                    if r == 1 and g >= 1:
                        pe.wait_ge(a_yout, g)
                    if r == 2:
                        pe.wait_ge(a_Tout, 3 * g + 1)
                    for q in range(4):
                        last = T.transpose(ps[0:TT, 4 + r % 2, q * TT:(q + 1) * TT], prob[g % 2][:, 4 * r + q, :],
                                           idn[0:TT, 0:TT])
                    last.then_inc(a_T, 1)
                pe.wait_ge(a_Tout, 3 * (g + 1))
                pe.wait_ge(a_pout, 6 * (g + 1))
                for h in range(H):
                    last = T.matmul(ps[0:TT, 5, 0:D], probT[:, pos(h), :], po_sb[:, h, :], start=(h == 0), stop=(h == H - 1))
                last.then_inc(a_y, 1)
                if g + 1 < NT:
                    project0(g + 1)
            pe.wait_ge(avg_sum, 1)
            for k in range(2):
                last = T.matmul(ps[0:KD, 4, k * TT:(k + 1) * TT], psum_all[:, k * KD:(k + 1) * KD], onesv[:, :],
                                start=True, stop=True)
            last.then_inc(avg_T, 1)
            pe.wait_ge(avg_out, 1)
            pe.wait_ge(wsum_ready, H - 1)
            for k in range(2):
                last = T.matmul(ps[0:TT, 5, 0:D], avgB[:, k, :], wsum[:, k, :], start=(k == 0), stop=(k == 1))
            last.then_inc(rbc_ready, 1)
            pe.wait_ge(zero_kv, 5)

            def columns(banks, w, m, c):
                for k in range(2):
                    last = T.matmul(ps[:, banks + c, 0:CH], w[:, k, m * 128:(m + 1) * 128],
                                    xT[:, k, c * CH:(c + 1) * CH], start=(k == 0), stop=(k == 1))
                return last

            def last_tile_between(v, pairs, signal, then=None):
                normed(v, 3)
                for banks, w, m in pairs:
                    columns(banks, w, m, 0)
                norm_transposes(v, [NT - 1])
                normed(v)
                if then is not None:
                    then()
                for banks, w, m in pairs:
                    columns(banks, w, m, 1).then_inc(signal, 1)

            def up(t, u, w1, v, then=None):
                last_tile_between(v, [(0, w1, 0), (2, w1, 1)], up_ready[u], then)
                for f in range(2, FT):
                    pe.wait_ge(hid_out, FT * t + f - 1)
                    columns(2 * (f % 2), w1, f, 0)
                    columns(2 * (f % 2), w1, f, 1).then_inc(up_ready[u], 1)

            def down(t, u, w2, read, count):
                for g in range(NT):
                    if g == 3 and read is not None:
                        pe.wait_ge(read, count)
                    if g == NT - 1:
                        pe.wait_ge(y_out, NT * t + 1)
                    for f in range(FT):
                        if g == 0:
                            pe.wait_ge(hid_out, FT * t + f + 1)
                        last = T.matmul(slot(g, rows(g)), hidden[u][:, f, tile(g, rows(g))], w2[:, f, :],
                                        start=(f == 0), stop=(f == FT - 1))
                    last.then_inc(down_ready[u], 1)

            def place_sums(n_experts, bank):
                def tiles(lo, n):
                    return asg[:, lo:lo + n, 0:n_experts]

                T.matmul(ps[0:TT, bank, 0:NT * n_experts], tri_sb[:, :], tiles(0, NT), start=True, stop=False)
                for b in range(1, NT):
                    T.matmul(ps[0:TT, bank, b * n_experts:NT * n_experts], ones[0:TT, 0:TT], tiles(0, NT - b),
                             start=False, stop=(b == NT - 1))
                for b in range(NT):
                    last = T.matmul(ps[0:TT, bank, NT * n_experts:(NT + 1) * n_experts], ones[0:TT, 0:TT],
                                    asg[:, b, 0:n_experts], start=(b == 0), stop=(b == NT - 1))
                last.then_inc(pos_ready, 1)

            def mixture(v, n_experts, cap, banks_read):
                static = n_experts // 2 - 2
                pick, put, xg = unit_views(cap)

                def gather(i, first=False):
                    if not first:
                        pe.wait_ge(x_Ta, i)
                        pe.wait_ge(x_Td, i)
                    else:
                        pe.wait_ge(x_parts, 4 * (v + 1))
                    pe.wait_ge(x_pick, i + 1)
                    for k in range(2):
                        for g in range(NT):
                            for n, part in enumerate(parts):
                                T.matmul(ps[0:KD, k, 0:2 * cap], part[:, g, k * KD:(k + 1) * KD], pick[:, g, :],
                                         start=(g == 0 and n == 0), stop=(g == NT - 1 and n == 2))
                    for u in range(2):
                        last = T.transpose(ps[0:cap, u, 256:256 + TT], put[:, NT - 1, u * cap:(u + 1) * cap], idn[0:TT, 0:TT])
                    last.then_inc(x_gather, 1)
                    if first:
                        banks_read()
                    for u in range(2):
                        for g in range(4):
                            last = T.transpose(ps[0:cap, 2 + u, g * TT:(g + 1) * TT], put[:, g, u * cap:(u + 1) * cap],
                                               idn[0:TT, 0:TT])
                    last.then_inc(x_T, 1)

                def units(i):
                    for u in range(2):
                        pe.wait_ge(e1_in[u], 16 * (i + 1))
                        if u == 0:
                            pe.wait_ge(x_gout, i + 1)
                        for f in range(FT):
                            n = FT * u + f
                            if n < 2:
                                pe.wait_ge(x_yout, NT * i + n + 1)
                            else:
                                pe.wait_ge(x_hout, 2 * FT * i + n - 1)
                            for k in range(2):
                                last = T.matmul(ps[:, 4 + f % 2, 0:cap], ew1_sb[u][:, k, f * 128:(f + 1) * 128],
                                                xg[:, k, u * cap:(u + 1) * cap], start=(k == 0), stop=(k == 1))
                            last.then_inc(x_up, 1)
                    for u in range(2):
                        pe.wait_ge(e2_in[u], 16 * (i + 1))
                        if u == 0:
                            pe.wait_ge(x_yout, NT * (i + 1))
                        pe.wait_ge(x_hout, 2 * FT * i + FT * (u + 1))
                        for f in range(FT):
                            last = T.matmul(ps[0:cap, 6 + u, 0:D], hidden[u][:, f, 0:cap], ew2_sb[u][:, f, :],
                                            start=(f == 0), stop=(f == FT - 1))
                        last.then_inc(x_down, 1)

                def put_back(i):
                    pe.wait_ge(x_ygout, 2 * (i + 1))
                    pe.wait_ge(x_Ta, i + 1)
                    pe.wait_ge(x_Td, i + 1)
                    for g in range(NT):
                        if g == NT - 1:
                            pe.wait_ge(x_yout, NT * (i + 1) + 3)
                        for u in range(2):
                            last = T.matmul(ps[0:rows(g), BACK[g], 0:D], putT[u][0:cap, tile(g, rows(g))], yg[u][0:cap, :],
                                            start=(u == 0), stop=(u == 1))
                        last.then_inc(x_back, 1)

                before = pe.value_load(pairs_sb[0:1, 0:1], min_val=0, max_val=2 * E0)
                gather(before, first=True)
                with pe.Fori(0, static) as p:
                    units(before + p)
                    gather(before + p + 1)
                    pe.wait_ge(sched_ready, v + 1)
                    put_back(before + p)
                dyn = pe.value_load(dyn_sb[0:1, 0:1], min_val=1, max_val=XMAX // 2 + 1)
                with pe.Fori(0, dyn) as p:
                    units(before + static + p)
                    gather(before + static + p + 1)
                    put_back(before + static + p)
                units(before + static + dyn)
                put_back(before + static + dyn)

            with pe.Fori(0, LAYERS // 2) as lp:
                for odd in range(2):
                    L = 2 * lp + odd
                    norm_transposes(1 + 2 * L, range(NT - 1))
                    pe.wait_ge(w_in["wq"], 16 * (L + 1))
                    pe.wait_ge(w_in["wk"], 16 * (L + 1))
                    last_tile_between(1 + 2 * L, [(0, wq_sb, 0), (2, wk_sb, 0)], qk_ready)
                    for m in range(1, 6):
                        for b, w, read in ((0, wq_sb, q_out), (2, wk_sb, k_out)):
                            pe.wait_ge(read, 6 * L + m)
                            columns(b, w, m, 0)
                            columns(b, w, m, 1).then_inc(qk_ready, 1)

                    def values(g):
                        if g == 0:
                            pe.wait_ge(w_in["wv"], 16 * (L + 1))
                        if g >= 2:
                            if g % 2 == 0:
                                pe.wait_ge(v_outA, 3 * L + g // 2)
                            else:
                                pe.wait_ge(v_outD, 2 * L + g // 2)
                        for c in range(2):
                            for k in range(2):
                                last = T.matmul(ps[0:TT, 4 + 2 * (g % 2) + c, 0:HD // 2], xT[:, k, tile(g)],
                                                wv_sb[:, k, c * (HD // 2):(c + 1) * (HD // 2)],
                                                start=(k == 0), stop=(k == 1))
                        last.then_inc(v_ready, 1)

                    def scores2(g):
                        if g == 0:
                            pe.wait_ge(q_out, 6 * (L + 1))
                            pe.wait_ge(k_out, 6 * (L + 1))
                        else:
                            pe.wait_ge(s_masked, NT * L + g)
                        for h in range(H):
                            p = pos(h)
                            last = T.matmul(ps[0:TT, p // 3, (p % 3) * TT:(p % 3 + 1) * TT], qT[:, h // 2, tile(g)],
                                            kT[h % 2][:, h // 2, tile(g)], start=True, stop=True)
                        last.then_inc(s_ready, 1)

                    def project(g):
                        if g == 0:
                            pe.wait_ge(w_in["wo"], 16 * (L + 1))
                        pe.wait_ge(ctx_out, NT * L + g + 1)
                        if g >= 1:
                            pe.wait_ge(o_out, NT * L + g)
                        for m in range(6):
                            last = T.matmul(ps[0:TT, 7, 0:D], ctxT[:, m, :], wo_sb[:, m, :],
                                            start=(m == 0), stop=(m == 5))
                        last.then_inc(o_ready, 1)

                    scores2(0)
                    values(0)
                    scores2(1)
                    for g in range(1, NT - 1):
                        values(g)
                    scores2(2)
                    values(NT - 1)
                    pe.wait_ge(v_outA, 3 * (L + 1))
                    pe.wait_ge(v_outD, 2 * (L + 1))
                    for g in range(NT):
                        if 0 < g < NT - 2:
                            scores2(g + 2)
                        pe.wait_ge(p_ready, NT * L + g + 1)
                        for r in range(3):
                            use = 3 * g + r
                            if use >= 2:
                                pe.wait_ge(at_out, 3 * NT * L + use - 1)
                            for q in range(4):
                                last = T.transpose(ps[0:TT, 4 + (15 * odd + use) % 2, q * TT:(q + 1) * TT],
                                                   prob[g % 3][:, 4 * r + q, :], idn[0:TT, 0:TT])
                            last.then_inc(at_ready, 1)
                        if g >= 1:
                            project(g - 1)
                        pe.wait_ge(at_out, 3 * (NT * L + g + 1))
                        for h in range(H):
                            m = h // 2
                            if g >= 1 and h == 8:
                                pe.wait_ge(o_out, NT * L + g)
                            last = T.matmul(ps[DK * (h % 2):DK * (h % 2 + 1), 6 + m // 4, (m % 4) * TT:(m % 4 + 1) * TT],
                                            v_sb[:, g, h * DK:(h + 1) * DK], probT[:, pos(h), :], start=True, stop=True)
                        last.then_inc(ctx_ready, 1)
                    norm_transposes(2 + 2 * L, range(2))
                    project(NT - 1)
                    norm_transposes(2 + 2 * L, range(2, NT - 1))

                    def gate_logits():
                        pe.wait_ge(gw_in, 16 * (lp + 1))
                        for g in range(NT):
                            for k in range(2):
                                last = T.matmul(ps[0:TT, 7, g * E0:(g + 1) * E0], xT[:, k, tile(g)],
                                                gw_sb[:, k, :], start=(k == 0), stop=(k == 1))
                        last.then_inc(lg_ready, 1)

                    pe.wait_ge(w_in["f1"], 16 * (L + 1))
                    up(L, odd, fw1_sb, 2 + 2 * L, gate_logits if odd else None)
                    if odd:
                        pe.wait_ge(asg_ready, lp + 1)
                        pe.wait_ge(pairs_ready, lp + 1)
                        place_sums(E0, 7)
                    pe.wait_ge(w_in["f2"], 16 * (L + 1))
                    down(L, odd, fw2_sb, pos_out if odd else None, lp + 1)
                mixture(lp, E0, CAP0, lambda: pe.wait_ge(y_out, NT * (2 * lp + 2)))
            norm_transposes(1 + 2 * LAYERS)
            normed(1 + 2 * LAYERS)
            for c in range(2):
                for k in range(2):
                    last = T.matmul(ps[0:NSTATE, c, 0:CH], bt_sb[:, k, :], xT[:, k, c * CH:(c + 1) * CH],
                                    start=(k == 0), stop=(k == 1))
            last.then_inc(ss_bu, 1)
            pe.wait_ge(ss_h, 1)
            for g in range(NT):
                if g == NT - 1:
                    pe.wait_ge(ss_yout, 1)
                T.matmul(slot(g, rows(g)), hst[:, 0, tile(g, rows(g))], ct_sb[:, :], start=True, stop=True).then_inc(ss_y, 1)
            norm_transposes(2 + 2 * LAYERS)
            normed(2 + 2 * LAYERS)
            for g in range(NT):
                for k in range(2):
                    last = T.matmul(ps[0:TT, 0, g * E1:(g + 1) * E1], xT[:, k, tile(g)], wr_sb[:, k, :],
                                    start=(k == 0), stop=(k == 1))
            last.then_inc(lg_ready, 1)
            pe.wait_ge(cw_ready, LAYERS // 2 + 1)
            for g in range(NT):
                T.transpose(ps[0:E1, 2 + g // 4, (g % 4) * TT:(g % 4 + 1) * TT], cw[:, g, :],
                            idn[0:TT, 0:TT]).then_inc(cwT_ready, 1)
            pe.wait_ge(asg_ready, LAYERS // 2 + 1)
            pe.wait_ge(pairs_ready, LAYERS // 2 + 1)
            place_sums(E1, 1)
            pe.wait_ge(cwT_out, 2)
            for g in range(NT):
                if g == NT - 1:
                    pe.wait_ge(b2_added, 1)
                T.matmul(slot(g, rows(g)), cwT[:, tile(g, rows(g))], b2_sb[:, :], start=True, stop=True).then_inc(b2_ready, 1)
            mixture(LAYERS // 2, E1, CAP1, lambda: pe.wait_ge(b2_added, NT))


def tables():
    n = np.arange(16, dtype=np.float32)
    dct = (2.0 * np.cos(np.float32(np.pi) * (2.0 * n[None, :] + 1.0) * n[:, None] / np.float32(32.0))).astype(np.float32)
    k2 = np.kron(dct, dct).astype(np.float32)
    tok = np.arange(TT)
    img, s = tok // SEQ, tok % SEQ
    same = img[:, None] == img[None, :]
    causal = np.where(same & (s[None, :] <= s[:, None]), 0.0, NEG).astype(np.float32)
    block = np.where(same, 0.0, NEG).astype(np.float32)
    nreg = (1.0 / (s + 1).astype(np.float32)).astype(np.float32)
    nreg = np.stack([nreg, -nreg], 1)
    clsmask = (s == 0).astype(np.float32)[:, None]
    rel = np.arange(SEQ)[None, :] - s[:, None]
    dist = np.abs(rel)
    large = 8 + (np.log(np.maximum(dist, 1).astype(np.float32) / np.float32(8)) / np.float32(np.log(128 / 8))
                 * np.float32(8)).astype(np.int32)
    bucket = (rel > 0) * 16 + np.where(dist < 8, dist, np.minimum(large, 15))
    onehot = (bucket.T[None, :, :] == np.arange(32)[:, None, None]).astype(np.float32)
    tri = (tok[:, None] < tok[None, :]).astype(np.float32)
    slots = np.tile(np.arange(1, CMAX + 1, dtype=np.float32), (TT, 1))
    valid = np.stack([(tok < rows(g)) for g in range(NT)], 1).astype(np.float32)
    iota = np.tile(np.arange(E1, dtype=np.float32), (TT, 1))
    return dict(k2=k2.reshape(2, 128, 256).transpose(1, 0, 2), causal=causal, nreg=nreg, clsmask=clsmask,
                onehot=onehot, block_mask=block, ident=np.eye(128, dtype=np.float32), iota=iota,
                tri=tri, slots=slots, valid=valid)


def kernel(x, cls_tok, L0_tok_W, L0_attn_e, L0_attn_p, L0_attn_ln_w, L0_attn_W_qk, L0_attn_W_o, L0_attn_wte,
           L0_ffn_attn_q, L0_ffn_attn_k, L0_ffn_attn_v, L0_ffn_attn_o, L0_ffn_ffn_wi, L0_ffn_ffn_wo, L0_ffn_ln1,
           L0_ffn_ln2, L0_ffn_ln_f, L0_ffn_rel_emb, L0_ffn_gate_w, L0_ffn_moe_w1, L0_ffn_moe_w2, L1_attn_A_real,
           L1_attn_A_imag, L1_attn_B, L1_attn_C, L1_ffn_wr, L1_ffn_w1, L1_ffn_b1, L1_ffn_w2, L1_ffn_b2):
    import numpy as _np
    import concourse.bacc as _bacc
    from concourse import mybir as _mybir
    from concourse.bass_utils import run_bass_kernel_spmd as _run

    a = _np.asarray

    def halves(w):
        w = a(w)
        w = w.reshape(w.shape[:-2] + (2, KD, w.shape[-1]))
        return w.swapaxes(-3, -2)

    def sixths(w):
        w = a(w)
        w = w.reshape(w.shape[:-2] + (6, 128, w.shape[-1]))
        return w.swapaxes(-3, -2)

    ins = dict(tables())
    xb = a(x).reshape(BATCH, 3, 4, 16, 4, 16).transpose(1, 3, 5, 0, 2, 4).reshape(6, 128, BATCH * 16)
    ins["xst"] = xb.transpose(1, 0, 2).reshape(128, 6 * BATCH * 16)
    ins["w_tok"] = sixths(a(L0_tok_W).T)
    ins["cls"] = a(cls_tok).reshape(1, D)
    wte = a(L0_attn_wte)
    ins["wte_main"] = wte[:WCH * WROWS * 128].reshape(WCH, 128, WROWS, D)
    ins["wte_tail"] = wte[WCH * WROWS * 128:]
    ins["ln_w"] = halves(a(L0_attn_ln_w)[:, None])
    ins["wqk"] = halves(a(L0_attn_W_qk).T)
    ins["wot"] = a(L0_attn_W_o).reshape(D, H, 2, KD).transpose(3, 2, 1, 0)
    ins["wq"], ins["wk"], ins["wv"] = halves(L0_ffn_attn_q), halves(L0_ffn_attn_k), halves(L0_ffn_attn_v)
    ins["wo"] = sixths(L0_ffn_attn_o)
    ins["fw1"], ins["fw2"] = halves(L0_ffn_ffn_wi), sixths(L0_ffn_ffn_wo)
    ins["ln1"], ins["ln2"] = halves(a(L0_ffn_ln1).T), halves(a(L0_ffn_ln2).T)
    ins["ln_f"] = a(L0_ffn_ln_f).reshape(1, D)
    ins["rel_emb"] = a(L0_ffn_rel_emb)
    ins["gate_w"] = halves(L0_ffn_gate_w)
    m1 = halves(L0_ffn_moe_w1).reshape(2 * E0, KD, 2, FF)
    m2 = sixths(L0_ffn_moe_w2).reshape(2 * E0, 128, FT, D)
    ins["ew1"] = _np.concatenate([m1, halves(a(L1_ffn_w1).transpose(0, 2, 1))])
    ins["ew2"] = _np.concatenate([m2, sixths(a(L1_ffn_w2).transpose(0, 2, 1))])
    ins["eb1"] = _np.concatenate([_np.zeros((2 * E0, 128, FT), _np.float32),
                                  a(L1_ffn_b1).reshape(E1, FT, 128).transpose(0, 2, 1)])
    ins["a_real"], ins["a_imag"] = a(L1_attn_A_real)[:, None], a(L1_attn_A_imag)[:, None]
    ins["bt"] = halves(a(L1_attn_B).T)
    ins["ct"] = a(L1_attn_C).T
    ins["wr"] = halves(a(L1_ffn_wr).T)
    ins["b2"] = a(L1_ffn_b2)

    nc = _bacc.Bacc("TRN2", target_bir_lowering=False, num_devices=1)
    arrays, args = {}, {}
    for name, v in ins.items():
        v = _np.ascontiguousarray(v)
        arrays[f"in_{name}"] = v
        args[name] = nc.dram_tensor(f"in_{name}", v.shape, _mybir.dt.from_np(v.dtype), kind="ExternalInput").ap()
    out = nc.dram_tensor("out", [TOK, D], _mybir.dt.float32, kind="ExternalOutput").ap()
    build(nc, out=out, **args)
    r = _run(nc, [arrays], core_ids=[0])
    return r.results[0]["out"].reshape(BATCH, SEQ, D)
```
